# Optimizing a Trainium2 kernel written in Bass

```python
import numpy as np
import jax
import jax.numpy as jnp

def _softmax(x, axis=-1):
    return jax.nn.softmax(x, axis=axis)

def _gelu(x):
    return jax.nn.gelu(x, approximate=True)

def _silu(x):
    return jax.nn.silu(x)

def _sigmoid(x):
    return jax.nn.sigmoid(x)

def _layernorm(x, axis=-1, eps=1e-05):
    m = jnp.mean(x, axis=axis, keepdims=True)
    v = jnp.var(x, axis=axis, keepdims=True)
    return (x - m) / jnp.sqrt(v + eps)

def _scatter_add(tgt, idx, src, axis=0):
    return tgt.at[idx].add(src)

def _segment_sum(src, seg, n):
    return jax.ops.segment_sum(src, seg, n)
kernel_name = 'mk_recurrent_d2_jaxref_r8_e12e67'

def setup_inputs(seed: int=0):
    np.random.seed(seed)
    _w = jnp.asarray

    def _L0_attn_setup():
        import jax, jax.numpy as jnp
        import numpy as np
        WINDOW = 4
        TOPK = 8
        key = jax.random.key(seed)
        ks = jax.random.split(key, 14)
        B, N, D = (4, 256, 128)
        s = 0.02
        w = lambda k_, shp: jax.random.normal(k_, shp, jnp.float32) * s
        return {'mu': jax.random.normal(ks[0], (B, N, D), jnp.float32), 'Wq': w(ks[1], (D, D)), 'bq': jnp.zeros((D,), jnp.float32), 'Wk': w(ks[2], (D, D)), 'bk': jnp.zeros((D,), jnp.float32), 'Wv': w(ks[3], (D, D)), 'bv': jnp.zeros((D,), jnp.float32), 'Wm1': w(ks[4], (2 * D, D)), 'bm1': jnp.zeros((D,), jnp.float32), 'Wm2': w(ks[5], (D, D)), 'bm2': jnp.zeros((D,), jnp.float32), 'Wo': w(ks[6], (2 * D, D)), 'bo': jnp.zeros((D,), jnp.float32)}
    _L0_attn_in = _L0_attn_setup()

    def _L0_ffn_setup():
        import jax, jax.numpy as jnp
        import numpy as np
        D = 128
        H = 256
        E = 8
        TOP_K = 2
        N_SHARED = 1
        B, S = (2, 128)
        key = jax.random.key(seed)
        ks = jax.random.split(key, 12)
        sc = 0.02
        return {'hidden': jax.random.normal(ks[0], (B, S, D), jnp.float32), 'router_w': jax.random.normal(ks[1], (D, E), jnp.float32) * sc, 'router_b': jnp.zeros((E,), jnp.float32), 'sw1': jax.random.normal(ks[2], (D, H), jnp.float32) * sc, 'sb1': jnp.zeros((H,), jnp.float32), 'sw2': jax.random.normal(ks[3], (H, D), jnp.float32) * sc, 'sb2': jnp.zeros((D,), jnp.float32), 'rw1': jax.random.normal(ks[4], (E, D, H), jnp.float32) * sc, 'rb1': jnp.zeros((E, H), jnp.float32), 'rw2': jax.random.normal(ks[5], (E, H, D), jnp.float32) * sc, 'rb2': jnp.zeros((E, D), jnp.float32)}
    _L0_ffn_in = _L0_ffn_setup()

    def _L1_attn_setup():
        import jax, jax.numpy as jnp
        import numpy as np
        EMB = 128
        NQ = 16
        NKV = 4
        D = 64
        B, S = (1, 256)
        ROPE_BASE = 10000.0

        def _rotary(t):
            d = t.shape[-1]
            inv_freq = 1.0 / ROPE_BASE ** (jnp.arange(0, d, 2, dtype=jnp.float32) / d)
            pos = jnp.arange(t.shape[1], dtype=jnp.float32)
            ang = pos[:, None] * inv_freq[None, :]
            cos = jnp.concatenate([jnp.cos(ang), jnp.cos(ang)], axis=-1)[None, :, None, :]
            sin = jnp.concatenate([jnp.sin(ang), jnp.sin(ang)], axis=-1)[None, :, None, :]
            x1, x2 = (t[..., :d // 2], t[..., d // 2:])
            t_rot = jnp.concatenate([-x2, x1], axis=-1)
            return t * cos + t_rot * sin
        key = jax.random.key(seed)
        ks = jax.random.split(key, 5)
        std = 0.02
        return {'x': jax.random.normal(ks[0], (B, S, EMB), jnp.float32), 'Wq': jax.random.normal(ks[1], (EMB, NQ * D), jnp.float32) * std, 'bq': jnp.zeros((NQ * D,), jnp.float32), 'Wk': jax.random.normal(ks[2], (EMB, NKV * D), jnp.float32) * std, 'bk': jnp.zeros((NKV * D,), jnp.float32), 'Wv': jax.random.normal(ks[3], (EMB, NKV * D), jnp.float32) * std, 'bv': jnp.zeros((NKV * D,), jnp.float32), 'Wo': jax.random.normal(ks[4], (NQ * D, EMB), jnp.float32) * std, 'bo': jnp.zeros((EMB,), jnp.float32)}
    _L1_attn_in = _L1_attn_setup()

    def _L1_ffn_setup():
        import jax, jax.numpy as jnp
        import numpy as np
        HIDDEN = 128
        FF = 512
        N_EXPERTS = 8
        CAP_FACTOR = 1.0
        B, S = (4, 256)
        STD = 0.02

        def _gelu(x):
            return x * 0.5 * (1.0 + jax.lax.erf(x / 1.41421))
        key = jax.random.key(seed)
        ks = jax.random.split(key, 6)
        x = jax.random.normal(ks[0], (B, S, HIDDEN), dtype=jnp.float32)
        W_sw = jax.random.normal(ks[1], (HIDDEN, N_EXPERTS), dtype=jnp.float32) * STD
        b_sw = jnp.zeros((N_EXPERTS,), dtype=jnp.float32)
        W1 = jax.random.normal(ks[2], (N_EXPERTS, HIDDEN, FF), dtype=jnp.float32) * STD
        b1 = jnp.zeros((N_EXPERTS, FF), dtype=jnp.float32)
        W2 = jax.random.normal(ks[3], (N_EXPERTS, FF, HIDDEN), dtype=jnp.float32) * STD
        b2 = jnp.zeros((N_EXPERTS, HIDDEN), dtype=jnp.float32)
        return {'x': x, 'W_sw': W_sw, 'b_sw': b_sw, 'W1': W1, 'b1': b1, 'W2': W2, 'b2': b2}
    _L1_ffn_in = _L1_ffn_setup()
    _d = {'L0_attn_mu': _L0_attn_in['mu'], 'L0_attn_Wq': _L0_attn_in['Wq'], 'L0_attn_bq': _L0_attn_in['bq'], 'L0_attn_Wk': _L0_attn_in['Wk'], 'L0_attn_bk': _L0_attn_in['bk'], 'L0_attn_Wv': _L0_attn_in['Wv'], 'L0_attn_bv': _L0_attn_in['bv'], 'L0_attn_Wm1': _L0_attn_in['Wm1'], 'L0_attn_bm1': _L0_attn_in['bm1'], 'L0_attn_Wm2': _L0_attn_in['Wm2'], 'L0_attn_bm2': _L0_attn_in['bm2'], 'L0_attn_Wo': _L0_attn_in['Wo'], 'L0_attn_bo': _L0_attn_in['bo'], 'L0_ffn_router_w': _L0_ffn_in['router_w'], 'L0_ffn_router_b': _L0_ffn_in['router_b'], 'L0_ffn_sw1': _L0_ffn_in['sw1'], 'L0_ffn_sb1': _L0_ffn_in['sb1'], 'L0_ffn_sw2': _L0_ffn_in['sw2'], 'L0_ffn_sb2': _L0_ffn_in['sb2'], 'L0_ffn_rw1': _L0_ffn_in['rw1'], 'L0_ffn_rb1': _L0_ffn_in['rb1'], 'L0_ffn_rw2': _L0_ffn_in['rw2'], 'L0_ffn_rb2': _L0_ffn_in['rb2'], 'L1_attn_Wq': _L1_attn_in['Wq'], 'L1_attn_bq': _L1_attn_in['bq'], 'L1_attn_Wk': _L1_attn_in['Wk'], 'L1_attn_bk': _L1_attn_in['bk'], 'L1_attn_Wv': _L1_attn_in['Wv'], 'L1_attn_bv': _L1_attn_in['bv'], 'L1_attn_Wo': _L1_attn_in['Wo'], 'L1_attn_bo': _L1_attn_in['bo'], 'L1_ffn_W_sw': _L1_ffn_in['W_sw'], 'L1_ffn_b_sw': _L1_ffn_in['b_sw'], 'L1_ffn_W1': _L1_ffn_in['W1'], 'L1_ffn_b1': _L1_ffn_in['b1'], 'L1_ffn_W2': _L1_ffn_in['W2'], 'L1_ffn_b2': _L1_ffn_in['b2']}
    _x0 = _d['L0_attn_mu']
    _d['L0_attn_mu'] = jax.random.normal(jax.random.fold_in(jax.random.key(seed), 1), (32, 256, 128), dtype=_x0.dtype)
    del _x0
    return _d

def reference(L0_attn_mu, L0_attn_Wq, L0_attn_bq, L0_attn_Wk, L0_attn_bk, L0_attn_Wv, L0_attn_bv, L0_attn_Wm1, L0_attn_bm1, L0_attn_Wm2, L0_attn_bm2, L0_attn_Wo, L0_attn_bo, L0_ffn_router_w, L0_ffn_router_b, L0_ffn_sw1, L0_ffn_sb1, L0_ffn_sw2, L0_ffn_sb2, L0_ffn_rw1, L0_ffn_rb1, L0_ffn_rw2, L0_ffn_rb2, L1_attn_Wq, L1_attn_bq, L1_attn_Wk, L1_attn_bk, L1_attn_Wv, L1_attn_bv, L1_attn_Wo, L1_attn_bo, L1_ffn_W_sw, L1_ffn_b_sw, L1_ffn_W1, L1_ffn_b1, L1_ffn_W2, L1_ffn_b2):

    def _L0_attn_ref(mu, Wq, bq, Wk, bk, Wv, bv, Wm1, bm1, Wm2, bm2, Wo, bo):
        import jax, jax.numpy as jnp
        import numpy as np
        WINDOW = 4
        TOPK = 8
        B, N, D = mu.shape
        padded = jnp.pad(mu, ((0, 0), (WINDOW, 0), (0, 0)))
        neighbors = jnp.stack([padded[:, WINDOW - w:WINDOW - w + N, :] for w in range(1, WINDOW + 1)], axis=2)
        self_exp = jnp.broadcast_to(mu[:, :, None, :], neighbors.shape)
        h = jnp.concatenate([self_exp, neighbors], axis=-1)
        h = jax.nn.silu(h @ Wm1 + bm1) @ Wm2 + bm2
        local_msgs = h.mean(axis=2)
        q = mu @ Wq + bq
        k = mu @ Wk + bk
        v = mu @ Wv + bv
        scores = jnp.einsum('bnd,bmd->bnm', q, k) / np.sqrt(D).astype(np.float32)
        causal_mask = jnp.triu(jnp.ones((N, N), dtype=bool), k=1)
        scores = jnp.where(causal_mask[None], -jnp.inf, scores)
        if N > TOPK:
            topk_v, topk_i = jax.lax.top_k(scores, TOPK)
            bi = jnp.arange(B)[:, None, None]
            ni = jnp.arange(N)[None, :, None]
            sparse = jnp.full_like(scores, -jnp.inf).at[bi, ni, topk_i].set(topk_v)
            attn = jax.nn.softmax(sparse, axis=-1)
        else:
            attn = jax.nn.softmax(scores, axis=-1)
        glob = jnp.einsum('bnm,bmd->bnd', attn, v)
        return jnp.concatenate([local_msgs, glob], axis=-1) @ Wo + bo

    def _L0_ffn_ref(hidden, router_w, router_b, sw1, sb1, sw2, sb2, rw1, rb1, rw2, rb2):
        import jax, jax.numpy as jnp
        import numpy as np
        D = 128
        H = 256
        E = 8
        TOP_K = 2
        N_SHARED = 1
        B, S = (2, 128)
        b, s, d = hidden.shape
        T = b * s
        flat = hidden.reshape(T, d)
        router_logits = flat @ router_w + router_b
        router_probs = jax.nn.softmax(router_logits, axis=-1)
        topk_probs, topk_idx = jax.lax.top_k(router_probs, TOP_K)
        weights = jnp.zeros_like(router_probs).at[jnp.arange(T)[:, None], topk_idx].add(topk_probs)
        sh = jax.nn.gelu(flat @ sw1 + sb1, approximate=False)
        shared_out = (sh @ sw2 + sb2) / N_SHARED
        h1 = jax.nn.gelu(jnp.einsum('td,edh->teh', flat, rw1) + rb1[None], approximate=False)
        expert_out = jnp.einsum('teh,ehd->ted', h1, rw2) + rb2[None]
        mixed = jnp.einsum('ted,te->td', expert_out, weights)
        return (shared_out + mixed).reshape(b, s, d)

    def _L1_attn_ref(x, Wq, bq, Wk, bk, Wv, bv, Wo, bo):
        import jax, jax.numpy as jnp
        import numpy as np
        EMB = 128
        NQ = 16
        NKV = 4
        D = 64
        B, S = (1, 256)
        ROPE_BASE = 10000.0

        def _rotary(t):
            d = t.shape[-1]
            inv_freq = 1.0 / ROPE_BASE ** (jnp.arange(0, d, 2, dtype=jnp.float32) / d)
            pos = jnp.arange(t.shape[1], dtype=jnp.float32)
            ang = pos[:, None] * inv_freq[None, :]
            cos = jnp.concatenate([jnp.cos(ang), jnp.cos(ang)], axis=-1)[None, :, None, :]
            sin = jnp.concatenate([jnp.sin(ang), jnp.sin(ang)], axis=-1)[None, :, None, :]
            x1, x2 = (t[..., :d // 2], t[..., d // 2:])
            t_rot = jnp.concatenate([-x2, x1], axis=-1)
            return t * cos + t_rot * sin
        b, s, _ = x.shape
        g = NQ // NKV
        q = (x @ Wq + bq).reshape(b, s, NQ, D)
        k = (x @ Wk + bk).reshape(b, s, NKV, D)
        v = (x @ Wv + bv).reshape(b, s, NKV, D)
        q = _rotary(q)
        k = _rotary(k)
        qg = q.reshape(b, s, NKV, g, D)
        scale = 1.0 / jnp.sqrt(jnp.float32(D))
        logits = jnp.einsum('bqhgd,bkhd->bhgqk', qg, k) * scale
        causal = jnp.tril(jnp.ones((s, s), bool))
        logits = jnp.where(causal, logits, jnp.float32(-1e+30))
        w = jax.nn.softmax(logits, axis=-1)
        out = jnp.einsum('bhgqk,bkhd->bqhgd', w, v).reshape(b, s, NQ * D)
        return out @ Wo + bo

    def _L1_ffn_ref(x, W_sw, b_sw, W1, b1, W2, b2):
        import jax, jax.numpy as jnp
        import numpy as np
        HIDDEN = 128
        FF = 512
        N_EXPERTS = 8
        CAP_FACTOR = 1.0
        B, S = (4, 256)
        STD = 0.02

        def _gelu(x):
            return x * 0.5 * (1.0 + jax.lax.erf(x / 1.41421))
        Bb, Ss, D = x.shape
        T = Bb * Ss
        E = W1.shape[0]
        capacity = int(CAP_FACTOR * T / E)
        xf = x.reshape(T, D)
        logits = xf @ W_sw + b_sw
        probs = jax.nn.softmax(logits, axis=-1)
        pmax = jnp.max(probs, axis=-1)
        routes = jnp.argmax(probs, axis=-1)
        factor = pmax / jax.lax.stop_gradient(pmax)
        xs = xf * factor[:, None]
        onehot = jax.nn.one_hot(routes, E, dtype=jnp.int32)
        pos = jnp.cumsum(onehot, axis=0) - 1
        pos_tok = jnp.take_along_axis(pos, routes[:, None], axis=1)[:, 0]
        keep = pos_tok < capacity
        pos_safe = jnp.where(keep, pos_tok, capacity)
        buf = jnp.zeros((E, capacity + 1, D), dtype=xs.dtype)
        buf = buf.at[routes, pos_safe].set(xs)
        buf = buf[:, :capacity]
        h = _gelu(jnp.einsum('ecd,edf->ecf', buf, W1) + b1[:, None, :])
        expert_out = jnp.einsum('ecf,efd->ecd', h, W2) + b2[:, None, :]
        gathered = expert_out[routes, jnp.minimum(pos_tok, capacity - 1)]
        final = jnp.where(keep[:, None], gathered, xs)
        return final.reshape(Bb, Ss, D)
    x = L0_attn_mu
    xn = _layernorm(x, axis=-1)
    s = _L0_attn_ref(xn, L0_attn_Wq, L0_attn_bq, L0_attn_Wk, L0_attn_bk, L0_attn_Wv, L0_attn_bv, L0_attn_Wm1, L0_attn_bm1, L0_attn_Wm2, L0_attn_bm2, L0_attn_Wo, L0_attn_bo)
    g = _silu(_L0_ffn_ref(xn, L0_ffn_router_w, L0_ffn_router_b, L0_ffn_sw1, L0_ffn_sb1, L0_ffn_sw2, L0_ffn_sb2, L0_ffn_rw1, L0_ffn_rb1, L0_ffn_rw2, L0_ffn_rb2))
    x = x + s * g
    xn = _layernorm(x, axis=-1)
    s = _L1_attn_ref(xn, L1_attn_Wq, L1_attn_bq, L1_attn_Wk, L1_attn_bk, L1_attn_Wv, L1_attn_bv, L1_attn_Wo, L1_attn_bo)
    g = _silu(_L1_ffn_ref(xn, L1_ffn_W_sw, L1_ffn_b_sw, L1_ffn_W1, L1_ffn_b1, L1_ffn_W2, L1_ffn_b2))
    x = x + s * g
    return x

_drawn_inputs = setup_inputs


def setup_inputs(seed=0):
    import zlib

    import numpy as np

    out = dict(_drawn_inputs(seed))
    spreads = {'L0_attn_bq': (0.0, 0.8),
     'L0_attn_bk': (0.0, 0.8),
     'L0_attn_bv': (0.0, 0.8),
     'L0_attn_bm1': (0.0, 0.8),
     'L0_attn_bm2': (0.0, 0.8),
     'L0_attn_bo': (0.0, 0.8),
     'L0_ffn_router_b': (0.0, 0.8),
     'L0_ffn_sb1': (0.0, 0.8),
     'L0_ffn_sb2': (0.0, 0.8),
     'L0_ffn_rb1': (0.0, 0.8),
     'L0_ffn_rb2': (0.0, 0.8),
     'L1_attn_bq': (0.0, 0.8),
     'L1_attn_bk': (0.0, 0.8),
     'L1_attn_bv': (0.0, 0.399),
     'L1_attn_bo': (0.0, 0.286),
     'L1_ffn_b_sw': (0.0, 0.1),
     'L1_ffn_b1': (0.0, 0.8),
     'L1_ffn_b2': (0.0, 0.8)}
    factors = {'L0_attn_Wq': 8.0,
     'L0_attn_Wk': 8.0,
     'L0_attn_Wv': 8.0,
     'L0_attn_Wm1': 8.0,
     'L0_attn_Wm2': 8.0,
     'L0_attn_Wo': 8.0,
     'L0_ffn_router_w': 8.0,
     'L0_ffn_sw1': 8.0,
     'L0_ffn_sw2': 8.0,
     'L0_ffn_rw1': 8.0,
     'L0_ffn_rw2': 8.0,
     'L1_attn_Wq': 8.0,
     'L1_attn_Wk': 8.0,
     'L1_attn_Wv': 8.0,
     'L1_attn_Wo': 2.892,
     'L1_ffn_W1': 8.0,
     'L1_ffn_W2': 8.0}
    for name, (base, spread) in spreads.items():
        noise = np.random.default_rng([zlib.crc32(name.encode()), seed]).standard_normal(out[name].shape)
        drawn = base * np.exp(spread * noise) if base else spread * noise
        out[name] = jnp.asarray(drawn.astype(out[name].dtype))
    for name, factor in factors.items():
        out[name] = (out[name] * factor).astype(out[name].dtype)
    return out
```

```python
from contextlib import ExitStack

import concourse.bass as bass
from concourse import mybir

F32 = mybir.dt.float32
F32R = mybir.dt.float32r
BF16 = mybir.dt.bfloat16
U32 = mybir.dt.uint32
ALU = mybir.AluOpType
ACT = mybir.ActivationFunctionType
AX_X = mybir.AxisListType.X

P = 128
D = 128
SEQ = 256
NB = 32
NT = NB * SEQ // P
WIN = 4
TOPK = 8
E = 8
H0 = 256
NQ, NKV, HD = 16, 4, 64
FF = 512
CAP = NB * SEQ // E
EPS = 1e-5
MASKED = -1e30
TAKEN = -3e38
FAR = 1e6
GS = 2.0 ** 0.5 / 1.41421

W0 = {n: slice(P * k, P * k + P) for k, n in enumerate(["q", "k", "m1a", "m1b", "v", "m2", "oa", "ob"])}
W0_ROUTER = slice(8 * P, 8 * P + E)
W0_BIAS = {n: slice(8 * P + E + k, 8 * P + E + k + 1) for k, n in enumerate(["q", "k", "m1", "v", "m2"])}
W0_COLS = 8 * P + E + 5
R_BO0, R_RB0, R_RB1, R_BO1, R_BV1 = 0, 128, 136, 144, 272
R_PREF, R_SLOT = 528, 536
R_COLS = 544


def wait(eng, sem, value):
    if not (isinstance(value, int) and value <= 0):
        eng.wait_ge(sem, value)


def steps(eng, rounds, depth, lead, step):
    for s in range(lead):
        step(s, s % 2, s // 2, lambda k: 0 <= s - k)
    with eng.Fori(0, (rounds - lead) // 2) as i:
        for u in range(2):
            step(2 * i + (lead + u), u, i + lead // 2, lambda k: True)
    for s in range(rounds, rounds + depth):
        step(s, s % 2, s // 2, lambda k: s - k < rounds)


def window(ap, pattern, offset=0):
    return bass.AP(ap.tensor, ap.offset + offset, [list(ap.ap[0])] + [list(x) for x in pattern])


def product_of_parts(pe, out, lhs, rhs, start=True, stop=True):
    pe.matmul(out, lhs[0], rhs[0], start=start, stop=False)
    pe.matmul(out, lhs[1], rhs[0], start=False, stop=False)
    return pe.matmul(out, lhs[0], rhs[1], start=False, stop=stop)


def norm_statistics(dve, stats, mean, var, tmp, chain, done):
    even, odd = stats[:, :, 1], stats[:, :, 4]
    dve.tensor_tensor(mean, even, odd, ALU.add)
    dve.tensor_tensor(tmp, even, odd, ALU.subtract)
    dve.tensor_tensor(var, stats[:, :, 2], stats[:, :, 5], ALU.add).then_inc(chain, 1)
    dve.wait_ge(chain, done + 1)
    dve.tensor_scalar(mean, mean, 0.5, None, ALU.mult)
    dve.tensor_tensor(tmp, tmp, tmp, ALU.mult)
    dve.tensor_scalar(var, var, 1.0 / D, None, ALU.mult).then_inc(chain, 1)
    dve.wait_ge(chain, done + 2)
    dve.tensor_scalar(tmp, tmp, 0.25, None, ALU.mult).then_inc(chain, 1)
    dve.wait_ge(chain, done + 3)
    dve.tensor_tensor(var, var, tmp, ALU.add).then_inc(chain, 1)
    dve.wait_ge(chain, done + 4)


def local_and_topk_attention(nc, outer, io):
    with ExitStack() as ctx:
        sb = lambda n, s, d=F32: ctx.enter_context(nc.sbuf_tensor("a_" + n, s, d))
        ps = lambda n, s, d=F32: ctx.enter_context(nc.psum_tensor("a_" + n, s, d))
        sem = lambda n: ctx.enter_context(nc.semaphore("a_" + n))
        x_all, s_all, xnt_all, logits0 = outer["x"], outer["s"], outer["xnt"], outer["logits0"]
        ident, identb, maskb, rows = outer["ident"], outer["identb"], outer["maskb"], outer["rows"]

        w = sb("w", [P, W0_COLS])
        wt = sb("wt", [P, 2, P])
        wvo = sb("wvo", [P, P + E])
        wm2o = sb("wm2o", [P, P])
        bcols = sb("bcols", [P, 2, P])
        vbias = sb("vbias", [P, P])
        stats = sb("stats", [P, NT, 6])
        mean, var, std, rstd = (sb(n, [P, NT]) for n in ("mean", "var", "std", "rstd"))
        xn = sb("xn", [P, 2, SEQ])
        xnt = sb("xnt", [P, 2, SEQ])
        qk = sb("qk", [P, 2, 2, SEQ])
        amsg = sb("amsg", [P, 2, SEQ])
        bmsg = sb("bmsg", [P, 2, WIN + SEQ])
        pre = sb("pre", [P, 2, WIN * SEQ])
        th = sb("th", [P, 2, WIN * SEQ])
        act4 = sb("act4", [P, WIN * SEQ])
        msum = sb("msum", [P, 2, SEQ])
        top = sb("top", [P, 2, 2, 8])
        nmax = sb("nmax", [P, 2, 2])
        rest = sb("rest", [P, 2, 384])
        ex = sb("ex", [P, 2, 384])
        ex8 = sb("ex8", [P, 2, 8])
        den = sb("den", [P, 2, 2])
        rden = sb("rden", [P, 2, 2])
        prob = sb("prob", [P, 2, 384])
        probt = sb("probt", [P, 2, 384])
        gn = sb("gn", [P, 2, SEQ])
        w1, w1_parts = sb("w1", [P, E + 1, H0]), outer["ffn0_w1"]

        ps_t = ps("ps_t", [P, 512])
        ps_qk = ps("ps_qk", [P, 512])
        ps_ab = ps("ps_ab", [P, 512])
        ps_v = ps("ps_v", [P, 512])
        ps_s = [ps(f"ps_s{k}", [P, 512]) for k in range(2)]
        ps_pt = ps("ps_pt", [P, 512])
        ps_gl = ps("ps_gl", [P, 512])

        names = """w1_in w1_high w1_low w_in wt_ps wt_sb bc fold_ps fold_sb vb_ps ready zero
            st var_done std_done rs_done chain xn_done t_done xnt_done copied qk_ps qk_done ab_ps ab_done v_ps v_done
            s_done max_done rest_done nm_done ex_done den_done rden_done prob_done pt_ps pt_done pre_done th_done
            act4_done sum_done l_done g_done gn_done s0_done""".split()
        S = {n: sem(n) for n in names}
        XC = 16
        x_in = [sem(f"x_in{c}") for c in range(NT // XC)]
        LEAD, DEPTH = 6, 5
        SC = float(D) ** -0.5
        vw = ps_v[:, 0:2 * (P + E)].rearrange("p (t n) -> p t n", t=2)
        block = ctx.enter_context(nc.Block())

        @block.sync
        def _(sp):
            sp.dma_start(w[:, :], io["w0"]).then_inc(S["w_in"], 16)
            xv = io["x"].rearrange("(n p) d -> p n d", p=P)
            for c, sem_x in enumerate(x_in):
                n = slice(c * XC, c * XC + XC)
                sp.dma_start(x_all[:, n, :], xv[:, n, :]).then_inc(sem_x, 16)
            sp.dma_start(w1[:, :, :], io["ffn0_w1"]).then_inc(S["w1_in"], 16)
            for sem_x in x_in:
                sp.wait_ge(sem_x, 16)

        @block.gpsimd
        def _(pool):
            pool.memset(bmsg[:, :, 0:WIN], 0.0).then_inc(S["zero"], 1)
            pool.wait_ge(S["w1_high"], 1)
            pool.tensor_tensor(w1_parts[1][:, :, :], w1[:, :, :], w1_parts[0][:, :, :], ALU.subtract).then_inc(S["w1_low"], 1)
            pool.wait_ge(S["zero"], 1)

            def step(s, u, turn, on):
                if on(2):
                    b, r = s - 2, u
                    pool.wait_ge(S["ab_done"], b + 1)
                    wait(pool, S["act4_done"], b - 1)
                    pool.tensor_tensor(
                        pre[:, r, :].rearrange("p (w n) -> p w n", w=WIN),
                        window(amsg[:, r, :], [(0, WIN), (1, SEQ)]),
                        window(bmsg[:, r, :], [(1, WIN), (1, SEQ)]), ALU.add).then_inc(S["pre_done"], 1)
                if on(1):
                    b, r = s - 1, 1 - u
                    pool.wait_ge(S["xnt_done"], b + 1)
                    pool.tensor_copy(xnt_all[:, bass.ds(b * SEQ, SEQ)], xnt[:, r, :]).then_inc(S["copied"], 1)

            steps(pool, NB, DEPTH, LEAD, step)

        @block.tensor
        def _(pe):
            pe.wait_ge(S["w_in"], 16)
            pe.transpose(ps_t[:, 0:P], w[:, W0["v"]], ident[:, :])
            pe.transpose(ps_t[:, P:2 * P], w[:, W0["m2"]], ident[:, :]).then_inc(S["wt_ps"], 1)
            pe.wait_ge(S["wt_sb"], 1)
            pe.matmul(ps_qk[:, 0:P], wt[:, 0, :], w[:, W0["ob"]], start=True, stop=True)
            pe.matmul(ps_qk[:, P:2 * P], wt[:, 1, :], w[:, W0["oa"]], start=True, stop=True).then_inc(S["fold_ps"], 1)
            pe.wait_ge(S["bc"], 2)
            pe.matmul(ps_ab[:, 0:P], bcols[:, 0, :], w[:, W0["ob"]], start=True, stop=False)
            pe.matmul(ps_ab[:, 0:P], bcols[:, 1, :], w[:, W0["oa"]], start=False, stop=True).then_inc(S["vb_ps"], 1)
            pe.wait_ge(S["ready"], 4)

            def step(s, u, turn, on):
                if on(2):
                    b, r = s - 2, u
                    pe.wait_ge(S["qk_done"], b + 1)
                    wait(pe, S["ex_done"], b - 1)
                    sc = ps_s[r]
                    pe.matmul(sc[:, 0:P], identb[:, :], maskb[:, :], start=True, stop=False, skip_group_check=True)
                    pe.matmul(sc[:, 2 * P:3 * P], identb[:, :], maskb[:, :], start=False, stop=False, skip_group_check=True)
                    pe.matmul(sc[:, 0:P], qk[:, r, 0, 0:P], qk[:, r, 1, 0:P], start=False, stop=False, skip_group_check=True)
                    pe.matmul(sc[:, P:3 * P], qk[:, r, 0, P:SEQ], qk[:, r, 1, :], start=False, stop=True,
                              skip_group_check=True).then_inc(S["s_done"], 1)
                if on(1):
                    b, r = s - 1, 1 - u
                    pe.wait_ge(S["xnt_done"], b + 1)
                    wait(pe, S["qk_done"], b)
                    for j, n in enumerate(("q", "k")):
                        last = pe.matmul(ps_qk[:, SEQ * j:SEQ * j + SEQ], w[:, W0[n]], xnt[:, r, :], start=True, stop=True)
                    last.then_inc(S["qk_ps"], 1)
                    wait(pe, S["ab_done"], b)
                    for j, n in enumerate(("m1a", "m1b")):
                        last = pe.matmul(ps_ab[:, SEQ * j:SEQ * j + SEQ], w[:, W0[n]], xnt[:, r, :], start=True, stop=True)
                    last.then_inc(S["ab_ps"], 1)
                    wait(pe, S["v_done"], b)
                    for t in range(2):
                        last = pe.matmul(vw[:, t, :], xnt[:, r, P * t:P * t + P], wvo[:, :], start=True, stop=True)
                    last.then_inc(S["v_ps"], 1)
                if on(3):
                    b, r = s - 3, 1 - u
                    pe.wait_ge(S["prob_done"], b + 1)
                    wait(pe, S["pt_done"], b)
                    for k in range(3):
                        last = pe.transpose(ps_pt[:, P * k:P * k + P], prob[:, r, P * k:P * k + P], ident[:, :])
                    last.then_inc(S["pt_ps"], 1)
                if on(4):
                    b, r = s - 4, u
                    pe.wait_ge(S["sum_done"], b + 1)
                    wait(pe, S["s0_done"], b)
                    for t in range(2):
                        last = pe.matmul(ps_gl[:, SEQ + P * t:SEQ + P * t + P], msum[:, r, P * t:P * t + P], wm2o[:, :],
                                         start=True, stop=True)
                    last.then_inc(S["l_done"], 1)
                    pe.wait_ge(S["pt_done"], b + 1)
                    pe.wait_ge(S["v_done"], b + 1)
                    v = [s_all[:, bass.ds(2 * b + t, 1), :] for t in range(2)]
                    pe.matmul(ps_gl[:, 0:P], probt[:, r, 0:P], v[0], start=True, stop=True)
                    pe.matmul(ps_gl[:, P:SEQ], probt[:, r, P:2 * P], v[0], start=True, stop=False)
                    pe.matmul(ps_gl[:, P:SEQ], probt[:, r, 2 * P:3 * P], v[1], start=False,
                              stop=True).then_inc(S["g_done"], 1)
                if on(0):
                    b, r = s, u
                    pe.wait_ge(S["xn_done"], b + 1)
                    wait(pe, S["xnt_done"], b)
                    for t in range(2):
                        last = pe.transpose(ps_t[:, P * t:P * t + P], xn[:, r, P * t:P * t + P], ident[:, :])
                    last.then_inc(S["t_done"], 1)

            steps(pe, NB, DEPTH, LEAD, step)

        @block.scalar
        def _(act):
            act.wait_ge(S["w1_in"], 16)
            act.activation(w1_parts[0][:, :, :], w1[:, :, :], ACT.Copy).then_inc(S["w1_high"], 1)
            act.wait_ge(S["var_done"], 1)
            act.activation(std[:, :], var[:, :], ACT.Sqrt).then_inc(S["std_done"], 1)
            act.wait_ge(S["wt_ps"], 1)
            act.activation(wt[:, :, :], ps_t[:, 0:2 * P].rearrange("p (a n) -> p a n", a=2), ACT.Copy).then_inc(S["wt_sb"], 1)
            act.wait_ge(S["w_in"], 16)
            act.activation(wvo[:, P:P + E], w[:, W0_ROUTER], ACT.Copy).then_inc(S["ready"], 1)
            act.wait_ge(S["fold_ps"], 1)
            act.activation(wvo[:, 0:P], ps_qk[:, 0:P], ACT.Copy).then_inc(S["ready"], 1)
            act.activation(wm2o[:, :], ps_qk[:, P:2 * P], ACT.Copy, scale=0.5 / WIN).then_inc(S["ready"], 1)

            def step(s, u, turn, on):
                if on(1):
                    b, r = s - 1, 1 - u
                    act.wait_ge(S["qk_ps"], b + 1)
                    wait(act, S["s_done"], b - 1)
                    for j, n in enumerate(("q", "k")):
                        last = act.activation(qk[:, r, j, :], ps_qk[:, SEQ * j:SEQ * j + SEQ], ACT.Identity,
                                              bias=w[:, W0_BIAS[n]])
                    last.then_inc(S["qk_done"], 1)
                    act.wait_ge(S["ab_ps"], b + 1)
                    wait(act, S["pre_done"], b - 1)
                    act.activation(amsg[:, r, :], ps_ab[:, 0:SEQ], ACT.Identity, bias=w[:, W0_BIAS["m1"]])
                    act.activation(bmsg[:, r, WIN:WIN + SEQ], ps_ab[:, SEQ:2 * SEQ], ACT.Copy).then_inc(S["ab_done"], 1)
                if on(2):
                    b, r = s - 2, u
                    act.wait_ge(S["nm_done"], b + 1)
                    wait(act, S["prob_done"], b - 1)
                    wait(act, S["rden_done"], b - 1)
                    for t, c in enumerate((slice(0, P), slice(P, 3 * P))):
                        act.activation(ex8[:, t, :], top[:, r, t, :], ACT.Exp, bias=nmax[:, r, t:t + 1], scale=SC,
                                       accum_out=den[:, r, t:t + 1])
                        last = act.activation(ex[:, r, c], ps_s[r][:, c], ACT.Exp, bias=nmax[:, r, t:t + 1], scale=SC)
                    last.then_inc(S["ex_done"], 1)
                if on(3):
                    b, r = s - 3, 1 - u
                    act.wait_ge(S["pt_ps"], b + 1)
                    wait(act, S["g_done"], b - 1)
                    act.activation(probt[:, r, :], ps_pt[:, 0:384], ACT.Copy).then_inc(S["pt_done"], 1)
                if on(0):
                    b, r = s, u
                    act.wait_ge(S["t_done"], b + 1)
                    wait(act, S["v_ps"], b - 1)
                    wait(act, S["copied"], b - 1)
                    act.activation(xnt[:, r, :], ps_t[:, 0:SEQ], ACT.Copy).then_inc(S["xnt_done"], 1)
                if on(4):
                    b, r = s - 4, u
                    act.wait_ge(S["g_done"], b + 1)
                    act.wait_ge(S["rden_done"], b + 1)
                    wait(act, S["s0_done"], b - 1)
                    for t in range(2):
                        last = act.activation(gn[:, r, P * t:P * t + P], ps_gl[:, P * t:P * t + P], ACT.Copy,
                                              scale=rden[:, r, t:t + 1])
                    last.then_inc(S["gn_done"], 1)
                if on(2):
                    b, r = s - 2, u
                    act.wait_ge(S["pre_done"], b + 1)
                    wait(act, S["act4_done"], b - 1)
                    act.activation(th[:, r, :], pre[:, r, :], ACT.Tanh, scale=0.5).then_inc(S["th_done"], 1)

            steps(act, NB, DEPTH, LEAD, step)

        @block.vector
        def _(dve):
            for c, sem_x in enumerate(x_in):
                dve.wait_ge(sem_x, 16)
                with dve.Fori(0, XC // 8) as i:
                    for u in range(8):
                        n = c * XC + 8 * i + u
                        last = dve.bn_stats(stats[:, bass.ds(n, 1), :], x_all[:, bass.ds(n, 1), :])
                    last.then_inc(S["st"], 1)
            dve.wait_ge(S["st"], NT // 8)
            norm_statistics(dve, stats[:, :, :], mean[:, :], var[:, :], rstd[:, :], S["chain"], 0)
            dve.tensor_scalar(var[:, :], var[:, :], EPS, None, ALU.add).then_inc(S["var_done"], 1)
            dve.wait_ge(S["std_done"], 1)
            dve.reciprocal(rstd[:, :], std[:, :]).then_inc(S["rs_done"], 1)
            dve.wait_ge(S["rs_done"], 1)
            dve.wait_ge(S["w_in"], 16)
            for j, n in enumerate(("v", "m2")):
                dve.tensor_scalar(bcols[:, j, :], outer["ones"][:, 0:P], w[:, W0_BIAS[n]], None, ALU.mult).then_inc(S["bc"], 1)
            dve.wait_ge(S["vb_ps"], 1)
            dve.tensor_tensor(vbias[:, :], ps_ab[:, 0:P], rows[:, R_BO0:R_BO0 + P], ALU.add).then_inc(S["ready"], 1)
            dve.wait_ge(S["ready"], 4)

            def step(s, u, turn, on):
                if on(4):
                    b, r = s - 4, u
                    wait(dve, S["gn_done"], b - 1)
                    dve.reciprocal(rden[:, r, :], den[:, r, :]).then_inc(S["rden_done"], 1)
                if on(3):
                    b, r = s - 3, 1 - u
                    dve.wait_ge(S["ex_done"], b + 1)
                    wait(dve, S["pt_ps"], b - 1)
                    dve.scalar_tensor_tensor(out=prob[:, r, :], in0=rest[:, r, :], scalar=TAKEN, in1=ex[:, r, :],
                                             op0=ALU.is_equal, op1=ALU.mult).then_inc(S["prob_done"], 1)
                if on(5):
                    b, r = s - 5, 1 - u
                    if on(2):
                        wait(dve, S["ex_done"], s - 3)
                        dve.wait_ge(S["s_done"], s - 1)
                    dve.wait_ge(S["gn_done"], b + 1)
                    dve.tensor_tensor(s_all[:, bass.ds(b * 2, 2), :], ps_gl[:, SEQ:2 * SEQ].rearrange("p (t n) -> p t n", t=2),
                                      gn[:, r, :].rearrange("p (t n) -> p t n", t=2), ALU.add).then_inc(S["s0_done"], 1)
                if on(2):
                    b, r = s - 2, u
                    if not on(5):
                        wait(dve, S["ex_done"], s - 3)
                        dve.wait_ge(S["s_done"], s - 1)
                    for t, c in enumerate((slice(0, P), slice(P, 3 * P))):
                        last = dve.max(top[:, r, t, :], ps_s[r][:, c])
                    last.then_inc(S["max_done"], 1)
                    dve.wait_ge(S["max_done"], b + 1)
                    dve.tensor_scalar(nmax[:, r, :], top[:, r, :, 0], -SC, None, ALU.mult)
                    for t, c in enumerate((slice(0, P), slice(P, 3 * P))):
                        last = dve.match_replace(rest[:, r, c], top[:, r, t, :], ps_s[r][:, c], TAKEN)
                    last.then_inc(S["nm_done"], 1)
                if on(0):
                    b, r = s, u
                    wait(dve, S["t_done"], b - 1)
                    for t in range(2):
                        last = dve.tensor_scalar(xn[:, r, P * t:P * t + P], x_all[:, 2 * b + t, :],
                                                 mean[:, bass.ds(2 * b + t, 1)], rstd[:, bass.ds(2 * b + t, 1)],
                                                 ALU.subtract, ALU.mult)
                    last.then_inc(S["xn_done"], 1)
                if on(3):
                    b, r = s - 3, 1 - u
                    dve.wait_ge(S["th_done"], b + 1)
                    wait(dve, S["sum_done"], b)
                    dve.scalar_tensor_tensor(out=act4[:, :], in0=th[:, r, :], scalar=1.0, in1=pre[:, r, :],
                                             op0=ALU.add, op1=ALU.mult).then_inc(S["act4_done"], 1)
                if on(3):
                    b, r = s - 3, 1 - u
                    dve.wait_ge(S["act4_done"], b + 1)
                    wait(dve, S["l_done"], b - 1)
                    dve.tensor_reduce(msum[:, r, :], act4[:, :].rearrange("p (w n) -> p n w", w=WIN), AX_X,
                                      ALU.add).then_inc(S["sum_done"], 1)
                if on(1):
                    b = s - 1
                    dve.wait_ge(S["v_ps"], b + 1)
                    dve.tensor_tensor(s_all[:, bass.ds(b * 2, 2), :], vw[:, :, 0:P], window(vbias[:, :], [(0, 2), (1, P)]), ALU.add)
                    dve.tensor_tensor(logits0[:, bass.ds(b * 2, 2), :], vw[:, :, P:P + E],
                                      window(rows[:, R_RB0:R_RB0 + E], [(0, 2), (1, E)]), ALU.add).then_inc(S["v_done"], 1)

            steps(dve, NB, DEPTH, LEAD, step)
            dve.wait_ge(S["s0_done"], NB)


def softmax_of_experts(dve, link, logits, ex_wait, work, row):
    dve_max = row
    link(dve.tensor_reduce(dve_max, logits, AX_X, ALU.max))
    link(dve.tensor_tensor(work, logits, over_experts(dve_max), ALU.subtract))
    ex_wait()
    link(dve.tensor_reduce(row, work, AX_X, ALU.add))
    link(dve.reciprocal(row, row))
    link(dve.tensor_tensor(work, work, over_experts(row), ALU.mult))


def over_experts(ap):
    return bass.AP(ap.tensor, ap.offset, [list(x) for x in ap.ap] + [[0, E]])


def over_tiles(ap):
    return bass.AP(ap.tensor, ap.offset, [list(ap.ap[0]), [0, NT], [1, E]])


def first_of_the_largest(dve, link, probs, out, pref, row, top=None):
    link(dve.tensor_reduce(row, probs, AX_X, ALU.max))
    if top is not None:
        link(dve.tensor_copy(top, row))
    link(dve.tensor_tensor(out, probs, over_experts(row), ALU.is_equal))
    link(dve.tensor_tensor(out, out, pref, ALU.mult))
    link(dve.tensor_reduce(row, out, AX_X, ALU.max))
    link(dve.tensor_tensor(out, out, over_experts(row), ALU.is_equal))


def mixture_of_all_experts(nc, outer, io):
    with ExitStack() as ctx:
        sb = lambda n, s, d=F32: ctx.enter_context(nc.sbuf_tensor("b_" + n, s, d))
        ps = lambda n, s, d=F32: ctx.enter_context(nc.psum_tensor("b_" + n, s, d))
        x_all, s_all, xnt_all, logits0, logits1 = (outer[k] for k in ("x", "s", "xnt", "logits0", "logits1"))
        ident, rows = outer["ident"], outer["rows"]
        NX = E + 1
        HC = H0 // P
        TC = 4
        CT = TC * P
        NC = NT // TC
        w1_parts = outer["ffn0_w1"]
        xnt_parts = [sb(f"xnt_{n}", [P, 2, CT], F32R) for n in ("high", "low")]
        w2 = sb("w2", [P, NX, HC, P])
        b1 = sb("b1", [P, NX * HC])
        b2 = sb("b2", [NX, P])
        wsw = sb("wsw", [P, E])
        probs = sb("probs", [P, NT, E])
        one1 = sb("one1", [P, NT, E])
        one2 = sb("one2", [P, NT, E])
        row = sb("row", [P, NT])
        wx = sb("wx", [P, NT, NX])
        wxs = sb("wxs", [P, 2, TC * NX])
        wt = sb("wt", [NX, 2, CT])
        h = sb("h", [P, 2, HC, CT])
        acc = sb("acc", [P, 2, TC, P])
        th = sb("th", [P, CT])
        z = sb("z", [P, CT])
        x1 = sb("x1", [P, TC, P])
        stats = sb("stats", [P, TC, 6])
        mean, var, std, rstd = (sb(n, [P, TC]) for n in ("mean", "var", "std", "rstd"))
        xs = sb("xs", [P, TC, P])
        xst = sb("xst", [P, CT])
        ps_h = [ps(f"ps_h{k}", [P, HC, CT]) for k in range(2)]
        ps_o = [ps(f"ps_o{k}", [P, TC, P]) for k in range(2)]
        ps_m = ps("ps_m", [P, 512])
        ps_t = ps("ps_t", [P, CT])
        zeros = sb("zeros", [P, 1024])
        names = """xnt_high xnt_low zeros_set slots_cleared w2_in b_in shifted exped chain ready one wxs_done wt_ps wt_done up_done gelu_done down_done acc_done
            th_done x1_done var_done std_done xs_done kept t_done xst_done r_done logits_done xs_out xst_out round""".split()
        S = {n: ctx.enter_context(nc.semaphore("b_" + n)) for n in names}
        LINKS = 8
        block = ctx.enter_context(nc.Block())

        @block.sync
        def _(sp):
            sp.dma_start(b1[:, :], io["ffn0_b1"]).then_inc(S["b_in"], 16)
            sp.dma_start(b2[:, :], io["ffn0_b2"]).then_inc(S["b_in"], 16)
            sp.dma_start(wsw[:, :], io["wsw"]).then_inc(S["b_in"], 16)
            sp.dma_start(w2[:, :, :, :], io["ffn0_w2"]).then_inc(S["w2_in"], 16)
            sp.wait_ge(S["zeros_set"], 1)
            clears = E * CAP * D // (P * 1024)
            for c in range(clears):
                sp.dma_start(io["slots_in"].rearrange("(c p r) d -> c p (r d)", c=clears, p=P)[c], zeros[:, :]
                             ).then_inc(S["slots_cleared"], 16)

            def step(s, u, turn, on):
                if on(1):
                    c = s - 1
                    sp.wait_ge(S["xs_done"], c + 1)
                    sp.dma_start(io["xn1"].rearrange("(n p) d -> p n d", p=P)[:, bass.ds(c * TC, TC), :],
                                 xs[:, :, :]).then_inc(S["xs_out"], 16)
                    sp.wait_ge(S["xst_done"], c + 1)
                    sp.dma_start(io["xnt1"][:, bass.ds(c * CT, CT)], xst[:, :]).then_inc(S["xst_out"], 16)

            steps(sp, NC, 1, 2, step)
            sp.wait_ge(S["slots_cleared"], 16 * clears)
            sp.wait_ge(S["xs_out"], 16 * NC)
            sp.wait_ge(S["xst_out"], 16 * NC)

        @block.gpsimd
        def _(pool):
            pool.memset(zeros[:, :], 0.0).then_inc(S["zeros_set"], 1)
            pool.memset(wx[:, :, E:NX], 1.0).then_inc(S["one"], 1)
            pool.wait_ge(S["zeros_set"], 1)
            FIRST = 0

            def split_low(s, u, cols):
                pool.tensor_tensor(xnt_parts[1][:, u, :], xnt_all[:, cols], xnt_parts[0][:, u, :],
                                   ALU.subtract).then_inc(S["xnt_low"], 1)

            def step(s, u, turn, on):
                if on(0):
                    wait(pool, S["up_done"], (s - 1) * NX)
                    cols = bass.ds(s * CT, CT)
                    pool.tensor_copy(xnt_parts[0][:, u, :], xnt_all[:, cols]).then_inc(S["xnt_high"], 1)
                    pool.wait_ge(S["xnt_high"], s + 1)
                    if s is FIRST:
                        split_low(s, u, cols)
                        pool.wait_ge(S["ready"], 1)
                        pool.wait_ge(S["one"], 1)
                    wait(pool, S["wt_ps"], s - 1)
                    pool.tensor_copy(wxs[:, u, :].rearrange("p (t e) -> p t e", t=TC),
                                     wx[:, bass.ds(s * TC, TC), :]).then_inc(S["wxs_done"], 1)
                    if s is not FIRST:
                        split_low(s, u, cols)
                if on(1):
                    pool.wait_ge(S["x1_done"], s)
                    pool.tensor_copy(x_all[:, bass.ds((s - 1) * TC, TC), :], x1[:, :, :]).then_inc(S["kept"], 1)

            steps(pool, NC, 1, 2, step)
            pool.wait_ge(S["kept"], NC)

        @block.tensor
        def _(pe):
            pe.wait_ge(S["b_in"], 48)
            pe.wait_ge(S["w2_in"], 16)

            def up(s, u, e):
                g = s * NX + e
                if e == 0:
                    pe.wait_ge(S["xnt_low"], s + 1)
                wait(pe, S["gelu_done"], g if e == 0 else g - 1)
                for j in range(HC):
                    last = product_of_parts(pe, ps_h[e % 2][:, j, :], [w[:, e, P * j:P * j + P] for w in w1_parts],
                                            [x[:, u, :] for x in xnt_parts])
                last.then_inc(S["up_done"], 1)

            def down(s, u, e):
                g = s * NX + e
                pe.wait_ge(S["gelu_done"], g + 1)
                wait(pe, S["acc_done"], g if e == 0 else g - 1)
                if e == 0:
                    pe.wait_ge(S["wt_done"], s + 1)
                for t in range(TC):
                    for j in range(HC):
                        last = pe.matmul(ps_o[e % 2][:, t, :], h[:, e % 2, j, P * t:P * t + P], w2[:, e, j, :],
                                         start=(j == 0), stop=(j == HC - 1 and e > 0))
                    if e == 0:
                        last = pe.matmul(ps_o[0][:, t, :], wt[:, u, P * t:P * t + P], b2[:, :], start=False, stop=True)
                last.then_inc(S["down_done"], 1)

            def step(s, u, turn, on):
                for e in range(NX):
                    if on(0):
                        up(s, u, e)
                    if e == 0 and on(0):
                        pe.wait_ge(S["wxs_done"], s + 1)
                        wait(pe, S["logits_done"], s - 1)
                        wait(pe, S["wt_done"], s)
                        for t in range(TC):
                            last = pe.transpose(ps_m[0:NX, P * t:P * t + P], wxs[:, u, NX * t:NX * t + NX], ident[:, :])
                        last.then_inc(S["wt_ps"], 1)
                    if e == 0 and on(1):
                        down(s - 1, 1 - u, NX - 1)
                    if e > 0 and on(0):
                        down(s, u, e - 1)
                    if e == 6 and on(1):
                        pe.wait_ge(S["xs_done"], s)
                        wait(pe, S["xst_done"], s - 1)
                        for t in range(TC):
                            last = pe.transpose(ps_t[:, P * t:P * t + P], xs[:, t, :], ident[:, :])
                        last.then_inc(S["t_done"], 1)
                    if e == 8 and on(1):
                        pe.wait_ge(S["xst_done"], s)
                        pe.wait_ge(S["wt_done"], s + 1 if on(0) else NC)
                        for t in range(TC):
                            last = pe.matmul(ps_m[:, E * t:E * t + E], xst[:, P * t:P * t + P], wsw[:, :], start=True, stop=True)
                        last.then_inc(S["r_done"], 1)

            steps(pe, NC, 1, 2, step)

        @block.scalar
        def _(act):
            act.wait_ge(S["shifted"], 1)
            act.activation(probs[:, :, :], probs[:, :, :], ACT.Exp).then_inc(S["exped"], 1)

            def step(s, u, turn, on):
                for e in range(NX):
                    if on(0):
                        g = s * NX + e
                        act.wait_ge(S["up_done"], g + 1)
                        wait(act, S["down_done"], g if e == 0 else g - 1)
                        for j in range(HC):
                            last = act.activation(h[:, e % 2, j, :], ps_h[e % 2][:, j, :], ACT.Gelu,
                                                  bias=b1[:, HC * e + j:HC * e + j + 1])
                        last.then_inc(S["gelu_done"], 1)
                    if e == 0 and on(0):
                        act.wait_ge(S["wt_ps"], s + 1)
                        act.activation(wt[:, u, :], ps_m[0:NX, :], ACT.Copy).then_inc(S["wt_done"], 1)
                    if e == 1 and on(1):
                        act.wait_ge(S["acc_done"], s * NX)
                        act.activation(th[:, :], acc[:, 1 - u, :, :].rearrange("p t n -> p (t n)"), ACT.Tanh,
                                       scale=0.5).then_inc(S["th_done"], 1)
                    if e == 4 and on(1):
                        act.wait_ge(S["var_done"], s)
                        act.activation(std[:, :], var[:, :], ACT.Sqrt).then_inc(S["std_done"], 1)
                    if e == 7 and on(1):
                        act.wait_ge(S["t_done"], s)
                        wait(act, S["xst_out"], (s - 1) * 16)
                        act.activation(xst[:, :], ps_t[:, :], ACT.Copy).then_inc(S["xst_done"], 1)

            steps(act, NC, 1, 2, step)

        @block.vector
        def _(dve):
            count = [0]

            def link(ins):
                count[0] += 1
                ins.then_inc(S["chain"], 1)
                dve.wait_ge(S["chain"], count[0])

            def take_exp():
                dve.sem_inc(S["shifted"], 1)
                dve.wait_ge(S["exped"], 1)

            softmax_of_experts(dve, link, logits0[:, :, :], take_exp, probs[:, :, :], row[:, :])
            pref = over_tiles(rows[:, R_PREF:R_PREF + E])
            first_of_the_largest(dve, link, probs[:, :, :], one1[:, :, :], pref, row[:, :])
            flat = lambda t: t[:, :, :].rearrange("p n e -> p (n e)")
            link(dve.scalar_tensor_tensor(out=flat(one2), in0=flat(one1), scalar=-2.0, in1=flat(probs),
                                          op0=ALU.mult, op1=ALU.add))
            link(dve.tensor_copy(wx[:, :, 0:E], one2[:, :, :]))
            first_of_the_largest(dve, link, wx[:, :, 0:E], one2[:, :, :], pref, row[:, :])
            link(dve.tensor_tensor(one1[:, :, :], one1[:, :, :], one2[:, :, :], ALU.add))
            dve.tensor_tensor(wx[:, :, 0:E], one1[:, :, :], probs[:, :, :], ALU.mult).then_inc(S["ready"], 1)
            dve.wait_ge(S["ready"], 1)
            base = count[0]

            def step(s, u, turn, on):
                def linked(j, ins):
                    ins.then_inc(S["chain"], 1)
                    dve.wait_ge(S["chain"], (s - 1) * LINKS + (base + j + 1))

                for e in range(NX):
                    c, v = (s - 1, 1 - u) if e == 0 else (s, u)
                    done = e - 1 if e else NX - 1
                    if on(1) if e == 0 else on(0):
                        g = c * NX + done
                        dve.wait_ge(S["down_done"], g + 1)
                        if done == 0:
                            dve.tensor_copy(acc[:, v, :, :], ps_o[0][:, :, :]).then_inc(S["acc_done"], 1)
                        else:
                            dve.wait_ge(S["acc_done"], g)
                            for t in range(TC):
                                last = dve.scalar_tensor_tensor(
                                    out=acc[:, v, t, :], in0=ps_o[done % 2][:, t, :],
                                    scalar=wx[:, bass.ds(c * TC + t, 1), done - 1:done],
                                    in1=acc[:, v, t, :], op0=ALU.mult, op1=ALU.add)
                            last.then_inc(S["acc_done"], 1)
                    if e == 2 and on(1):
                        b, r = s - 1, 1 - u
                        dve.wait_ge(S["th_done"], b + 1)
                        linked(0, dve.scalar_tensor_tensor(out=z[:, :], in0=th[:, :], scalar=1.0,
                                                           in1=acc[:, r, :, :].rearrange("p t n -> p (t n)"),
                                                           op0=ALU.add, op1=ALU.mult))
                        linked(1, dve.scalar_tensor_tensor(
                            out=z[:, :], in0=z[:, :], scalar=0.5, op0=ALU.mult, op1=ALU.mult,
                            in1=s_all[:, :, :].rearrange("p n d -> p (n d)")[:, bass.ds(b * CT, CT)]))
                        wait(dve, S["kept"], b)
                        dve.tensor_tensor(x1[:, :, :], z[:, :].rearrange("p (t n) -> p t n", t=TC),
                                          x_all[:, bass.ds(b * TC, TC), :], ALU.add).then_inc(S["x1_done"], 1)
                        dve.wait_ge(S["x1_done"], b + 1)
                    if e == 3 and on(1):
                        for t in range(TC):
                            last = dve.bn_stats(stats[:, t, :], x1[:, t, :])
                        linked(2, last)
                        norm_statistics(dve, stats[:, :, :], mean[:, :], var[:, :], rstd[:, :], S["chain"],
                                        (s - 1) * LINKS + (base + 3))
                        dve.tensor_scalar(var[:, :], var[:, :], EPS, None, ALU.add).then_inc(S["var_done"], 1)
                    if e == 5 and on(1):
                        b = s - 1
                        dve.wait_ge(S["std_done"], b + 1)
                        linked(7, dve.reciprocal(rstd[:, :], std[:, :]))
                        wait(dve, S["xs_out"], b * 16)
                        for t in range(TC):
                            last = dve.tensor_scalar(xs[:, t, :], x1[:, t, :], mean[:, t:t + 1], rstd[:, t:t + 1],
                                                     ALU.subtract, ALU.mult)
                        last.then_inc(S["xs_done"], 1)
                    if e == 8 and on(1):
                        b = s - 1
                        dve.wait_ge(S["r_done"], b + 1)
                        dve.tensor_tensor(logits1[:, bass.ds(b * TC, TC), :],
                                          ps_m[:, 0:TC * E].rearrange("p (t e) -> p t e", t=TC),
                                          window(rows[:, R_RB1:R_RB1 + E], [(0, TC), (1, E)]), ALU.add).then_inc(S["logits_done"], 1)

            steps(dve, NC, 1, 2, step)
            dve.wait_ge(S["logits_done"], NC)


def route_to_slots(nc, outer, io):
    with ExitStack() as ctx:
        sb = lambda n, s, d=F32: ctx.enter_context(nc.sbuf_tensor("r_" + n, s, d))
        probs = sb("probs", [P, NT, E])
        one = sb("one", [P, NT, E])
        row = sb("row", [P, NT])
        over = sb("over", [P, NT])
        total = sb("total", [P, NT, E])
        sums = [sb(f"sums{k}", [P, NT, E]) for k in range(2)]
        place = sb("place", [P, NT, E])
        work = sb("work", [P, NT, E])
        ps_in = ctx.enter_context(nc.psum_tensor("r_ps_in", [P, NT * E], F32))
        ps_all = ctx.enter_context(nc.psum_tensor("r_ps_all", [P, NT * E], F32))
        s_shift, s_exp, s_chain, s_one, s_count = (ctx.enter_context(nc.semaphore("r_" + n)) for n in
                                                   ("shifted", "exped", "chain", "one", "count"))
        rows = outer["rows"]
        flat = lambda t: t[:, :, :].rearrange("p n e -> p (n e)")
        block = ctx.enter_context(nc.Block())

        @block.scalar
        def _(act):
            act.wait_ge(s_shift, 1)
            act.activation(probs[:, :, :], probs[:, :, :], ACT.Exp).then_inc(s_exp, 1)

        @block.tensor
        def _(pe):
            pe.wait_ge(s_one, 1)
            pe.matmul(ps_in[:, :], outer["upto"][:, :], flat(one), start=True, stop=True).then_inc(s_count, 1)
            pe.matmul(ps_all[:, :], outer["ones"][:, :], flat(one), start=True, stop=True).then_inc(s_count, 1)

        @block.vector
        def _(dve):
            count = [0]

            def link(ins):
                count[0] += 1
                ins.then_inc(s_chain, 1)
                dve.wait_ge(s_chain, count[0])

            def take_exp():
                dve.sem_inc(s_shift, 1)
                dve.wait_ge(s_exp, 1)

            softmax_of_experts(dve, link, outer["logits1"][:, :, :], take_exp, probs[:, :, :], row[:, :])
            first_of_the_largest(dve, link, probs[:, :, :], one[:, :, :], over_tiles(rows[:, R_PREF:R_PREF + E]), row[:, :])
            dve.sem_inc(s_one, 1)
            dve.wait_ge(s_count, 2)
            link(dve.tensor_copy(flat(total), ps_all[:, :]))
            src, d, k = total, 1, 0
            while d < NT:
                dst = sums[k % 2]
                link(dve.tensor_copy(dst[:, 0:d, :], src[:, 0:d, :]))
                link(dve.tensor_tensor(dst[:, d:NT, :], src[:, d:NT, :], src[:, 0:NT - d, :], ALU.add))
                src, d, k = dst, 2 * d, k + 1
            link(dve.tensor_tensor(flat(place), flat(src), flat(total), ALU.subtract))
            link(dve.tensor_tensor(flat(place), flat(place), ps_in[:, :], ALU.add))
            link(dve.tensor_tensor(flat(work), flat(place), flat(one), ALU.mult))
            link(dve.tensor_reduce(row[:, :], work[:, :, :], AX_X, ALU.add))
            link(dve.tensor_scalar(over[:, :], row[:, :], float(CAP), FAR, ALU.is_gt, ALU.mult))
            link(dve.tensor_tensor(work[:, :, :], place[:, :, :], over_tiles(rows[:, R_SLOT:R_SLOT + E]), ALU.add))
            link(dve.tensor_tensor(flat(work), flat(work), flat(one), ALU.mult))
            link(dve.tensor_reduce(row[:, :], work[:, :, :], AX_X, ALU.add))
            link(dve.scalar_tensor_tensor(out=outer["slot"][:, :], in0=over[:, :], scalar=-1.0, in1=row[:, :],
                                          op0=ALU.add, op1=ALU.add))


def rotary_attention(nc, outer, io):
    with ExitStack() as ctx:
        sb = lambda n, s, d=F32: ctx.enter_context(nc.sbuf_tensor("c_" + n, s, d))
        ps = lambda n, s, d=F32: ctx.enter_context(nc.psum_tensor("c_" + n, s, d))
        s_all, ident, identb, maskb, rows, slot = (outer[k] for k in ("s", "ident", "identb", "maskb", "rows", "slot"))
        G = NQ // NKV
        NH2 = NQ // 2
        wq = sb("wq", [P, G + 1, 2, P])
        bq = sb("bq", [P, G + 1, 2])
        wv = sb("wv", [P, NKV * HD])
        wo = sb("wo", [P, NH2, P])
        rope = sb("rope", [P, 2, 2, SEQ])
        xnt = sb("xnt", [P, 2, SEQ])
        prod = sb("prod", [P, 2, 4, SEQ])
        rot = sb("rot", [P, G + 1, 2, SEQ])
        qt = sb("qt", [P, 2, NH2, SEQ])
        kt = sb("kt", [P, 2, NKV, SEQ])
        v = sb("v", [P, 2, 2, NKV, HD + 1])
        nmax = sb("nmax", [P, 2, 4])
        ex = [sb(f"ex{k}", [P, 2, 2, SEQ]) for k in range(2)]
        pt = sb("pt", [P, 2, 2, 2, SEQ])
        rden = sb("rden", [P, 2, G])
        o = sb("o", [P, 2, NQ, HD])
        ot = sb("ot", [P, 2, NH2, P])
        xr = sb("xr", [P, 2, 2, P])
        idx = sb("idx", [P, 2, 2], U32)
        ps_s = [ps(f"ps_s{k}", [P, 2, 512]) for k in range(2)]
        ps_t = ps("ps_t", [P, 2, 512])
        ps_o = ps("ps_o", [P, 512])
        ps_p = ps("ps_p", [P, 512])
        names = """w_in one x_in xr_in rel p_done rope_done rot_done v_done s_done max_done exp_done t_done ta_done td_done
            pv_done rd_done o_done ot_ps ota_done otd_done wo_ps wo_done idx_done""".split()
        S = {n: ctx.enter_context(nc.semaphore("c_" + n)) for n in names}
        scattered = [ctx.enter_context(nc.semaphore(f"c_scattered{u}")) for u in range(2)]
        U = 2 * NKV
        RELS = 24
        LEAD, DEPTH = 4, 2
        block = ctx.enter_context(nc.Block())

        @block.sync
        def _(sp):
            for dst, src in ((wq[:, :, :, :], "wq1"), (bq[:, :, :], "bq1"), (wv[:, :], "wv1"), (wo[:, :, :], "wo1"),
                             (rope[:, :, :, :], "rope")):
                sp.dma_start(dst, io[src]).then_inc(S["w_in"], 16)

            def step(s, u, turn, on):
                if on(0):
                    wait(sp, S["p_done"], 6 * (s - 1))
                    sp.dma_start(xnt[:, u, :], io["xnt1"][:, bass.ds(s * SEQ, SEQ)]).then_inc(S["x_in"], 16)
                    wait(sp, scattered[u], 32 * turn)
                    sp.dma_start(xr[:, u, :, :], io["xn1"].rearrange("(n p) d -> p n d", p=P)[:, bass.ds(2 * s, 2), :]
                                 ).then_inc(S["xr_in"], 16)
                    sp.wait_ge(S["rot_done"], (G + 1) * s + G)
                    for i in range(4):
                        for x in range(2):
                            sp.dma_start(qt[64 * (i % 2) + 32 * x:64 * (i % 2) + 32 * x + 32, u, i // 2:NH2:2, :],
                                         rot[32 * i:32 * i + 32, 0:G, x, :]).then_inc(S["rel"], 16)
                    sp.wait_ge(S["rot_done"], (G + 1) * (s + 1))
                    for i in range(4):
                        for x in range(2):
                            for half in range(2):
                                sp.dma_start(kt[64 * half + 32 * x:64 * half + 32 * x + 32, u, i, :],
                                             rot[32 * i:32 * i + 32, G, x, :]).then_inc(S["rel"], 16)

            steps(sp, NB, DEPTH, LEAD, step)

        @block.gpsimd
        def _(pool):
            pool.memset(v[:, :, :, :, HD:HD + 1], 1.0).then_inc(S["one"], 1)

            def step(s, u, turn, on):
                if on(0):
                    wait(pool, scattered[u], 32 * turn)
                    pool.tensor_copy(idx[:, u, :], slot[:, bass.ds(2 * s, 2)]).then_inc(S["idx_done"], 1)
                    for k in range(G + 1):
                        if k == G:
                            pool.wait_ge(S["idx_done"], s + 1)
                            pool.wait_ge(S["xr_in"], 16 * (s + 1))
                        pool.wait_ge(S["rope_done"], (G + 1) * s + (k + 1))
                        if k == 0:
                            wait(pool, S["rel"], 16 * RELS * s)
                        r = k % 2
                        pool.tensor_tensor(rot[:, k, 0, :], prod[:, r, 0, :], prod[:, r, 1, :], ALU.subtract)
                        pool.tensor_tensor(rot[:, k, 1, :], prod[:, r, 2, :], prod[:, r, 3, :], ALU.add).then_inc(S["rot_done"], 1)
                    for t in range(2):
                        pool.indirect_dma_start(
                            out=io["slots_in"], out_offset=bass.IndirectOffsetOnAxis(ap=idx[:, u, t:t + 1], axis=0),
                            in_=xr[:, u, t, :], in_offset=None, bounds_check=E * CAP - 1,
                            oob_is_err=False).then_inc(scattered[u], 16)

            steps(pool, NB, DEPTH, LEAD, step)
            for u in range(2):
                pool.wait_ge(scattered[u], 32 * NB // 2)

        @block.tensor
        def _(pe):
            pe.wait_ge(S["w_in"], 80)

            def mask_scores(b, k):
                n, t = b * U + k, k // NKV
                if k == 0:
                    pe.wait_ge(S["rel"], 16 * RELS * (b + 1))
                wait(pe, S["exp_done"], n - 1)
                sc = ps_s[k % 2]
                for half in range(2):
                    pe.matmul(window(sc[:, half, :], [(2 * P, 2), (1, P)], t * P), identb[:, :],
                              window(maskb[:, :], [(0, 2), (1, P)]), start=True, stop=False, skip_group_check=True)

            def scores(u, k, w):
                t, g = k // NKV, k % NKV
                cols = P * (t + 1)
                for half in range(2):
                    last = pe.matmul(ps_s[k % 2][:, half, 2 * P * w:2 * P * w + cols],
                                     qt[64 * half:64 * half + 64, u, 2 * g + w, P * t:P * t + P],
                                     kt[64 * half:64 * half + 64, u, g, 0:cols],
                                     start=False, stop=True, skip_group_check=True)
                if w == 1:
                    last.then_inc(S["s_done"], 1)

            def project(s, u, k):
                if k == 0:
                    pe.wait_ge(S["x_in"], 16 * (s + 1))
                    wait(pe, S["v_done"], s)
                    wait(pe, S["wo_done"], 2 * (s - 2))
                else:
                    pe.wait_ge(S["rope_done"], (G + 1) * s + k)
                if k <= G:
                    for x in range(2):
                        last = pe.matmul(ps_p[:, SEQ * x:SEQ * x + SEQ], wq[:, k, x, :], xnt[:, u, :], start=True, stop=True)
                else:
                    for t in range(2):
                        last = pe.matmul(ps_p[:, SEQ * t:SEQ * t + SEQ], xnt[:, u, P * t:P * t + P], wv[:, :], start=True, stop=True)
                last.then_inc(S["p_done"], 1)

            def turn_probs(b, k):
                n, t = b * U + k, k // NKV
                pe.wait_ge(S["exp_done"], n + 1)
                wait(pe, S["ta_done"], n)
                wait(pe, S["td_done"], n)
                outs = 2 * b - 1 if k <= 1 else 2 * b if k <= 5 else 2 * b + 1
                wait(pe, S["ota_done"], outs)
                wait(pe, S["otd_done"], outs)
                for w in range(2):
                    for half in range(2):
                        for blk in range(t + 1):
                            at = P * (half * (t + 1) + blk)
                            last = pe.transpose(ps_t[:, w, at:at + P], ex[k % 2][:, half, w, P * blk:P * blk + P], ident[:, :])
                last.then_inc(S["t_done"], 1)

            def weigh(b, r, k):
                n, t, g = b * U + k, k // NKV, k % NKV
                pe.wait_ge(S["ta_done"], n + 1)
                pe.wait_ge(S["td_done"], n + 1)
                pe.wait_ge(S["v_done"], b + 1)
                wait(pe, S["o_done"], n)
                for w in range(2):
                    for half in range(2):
                        h = 2 * w + half
                        for blk in range(t + 1):
                            at = P * (half * (t + 1) + blk)
                            last = pe.matmul(ps_o[:, (HD + 1) * h:(HD + 1) * (h + 1)], pt[:, k % 2, w, at // SEQ, at % SEQ:at % SEQ + P],
                                             v[:, r, blk, g, :], start=(blk == 0), stop=(blk == t))
                last.then_inc(S["pv_done"], 1)

            def step(s, u, turn, on):
                for k in range(U):
                    if on(1):
                        mask_scores(s - 1, k)
                        scores(1 - u, k, 0)
                    if on(2) and k in (0, 4):
                        b, t = s - 2, k // 4
                        pe.wait_ge(S["o_done"], b * U + (4 * t + 4))
                        n = (b + 1) * U + k - 2
                        last_unit = n if on(1) else min(n, NB * U)
                        pe.wait_ge(S["ta_done"], last_unit)
                        pe.wait_ge(S["td_done"], last_unit)
                        for j in range(NH2):
                            last = pe.transpose(ps_t[:, j // 4, P * (j % 4):P * (j % 4) + P], o[:, t, 2 * j:2 * j + 2, :]
                                                .rearrange("p a d -> p (a d)"), ident[:, :])
                        last.then_inc(S["ot_ps"], 1)
                    if on(1):
                        scores(1 - u, k, 1)
                    if on(0) and k < G + 2:
                        project(s, u, k)
                    if (on(1) if k >= 2 else on(2)):
                        turn_probs(s - 1 if k >= 2 else s - 2, (k - 2) % U)
                    if (on(1) if k >= 3 else on(2)):
                        weigh(s - 1 if k >= 3 else s - 2, (1 - u) if k >= 3 else u, (k - 3) % U)
                    if on(2) and k >= 6:
                        b, t = s - 2, k - 6
                        pe.wait_ge(S["ota_done"], 2 * b + (t + 1))
                        pe.wait_ge(S["otd_done"], 2 * b + (t + 1))
                        if k == 6:
                            pe.wait_ge(S["v_done"], s + 1 if on(0) else NB)
                            wait(pe, S["wo_done"], 2 * b)
                        else:
                            pe.wait_ge(S["wo_done"], 2 * b + 1)
                        for j in range(NH2):
                            last = pe.matmul(ps_p[:, 0:P], ot[:, t, j, :], wo[:, j, :], start=(j == 0), stop=(j == NH2 - 1))
                        last.then_inc(S["wo_ps"], 1)

            steps(pe, NB, DEPTH, LEAD, step)

        @block.scalar
        def _(act):
            def step(s, u, turn, on):
                for k in range(U):
                    if on(2) and k in (0, 4):
                        b, t = s - 2, k // 4
                        act.wait_ge(S["ot_ps"], 2 * b + (t + 1))
                        wait(act, S["wo_ps"], 2 * (b - 1) + (t + 1))
                        act.activation(ot[:, t, 0:4, :].rearrange("p j n -> p (j n)"), ps_t[:, 0, :], ACT.Copy).then_inc(S["ota_done"], 1)
                    if (on(1) if k >= 2 else on(2)):
                        b, kk = (s - 1 if k >= 2 else s - 2), (k - 2) % U
                        n, t = b * U + kk, kk // NKV
                        act.wait_ge(S["t_done"], n + 1)
                        wait(act, S["pv_done"], n - 1)
                        act.activation(pt[:, kk % 2, 0, 0:t + 1, :], ps_t[:, 0, 0:SEQ * (t + 1)].rearrange("p (a n) -> p a n", n=SEQ),
                                       ACT.Copy).then_inc(S["ta_done"], 1)
                    if on(1):
                        b = s - 1
                        n, t = b * U + k, k // NKV
                        cols = P * (t + 1)
                        act.wait_ge(S["max_done"], n + 1)
                        wait(act, S["t_done"], n - 1)
                        for half in range(2):
                            for w in range(2):
                                last = act.activation(ex[k % 2][:, half, w, 0:cols], ps_s[k % 2][:, half, 2 * P * w:2 * P * w + cols],
                                                      ACT.Exp, bias=nmax[:, k % 2, 2 * half + w:2 * half + w + 1])
                        last.then_inc(S["exp_done"], 1)

            steps(act, NB, DEPTH, LEAD, step)

        @block.vector
        def _(dve):
            dve.wait_ge(S["w_in"], 80)
            dve.wait_ge(S["one"], 1)

            def step(s, u, turn, on):
                for k in range(U):
                    if on(2) and k in (0, 4):
                        b, t = s - 2, k // 4
                        dve.wait_ge(S["ot_ps"], 2 * b + (t + 1))
                        wait(dve, S["wo_ps"], 2 * (b - 1) + (t + 1))
                        dve.tensor_copy(ot[:, t, 4:8, :].rearrange("p j n -> p (j n)"), ps_t[:, 1, :]).then_inc(S["otd_done"], 1)
                    if on(1):
                        b = s - 1
                        n, t = b * U + k, k // NKV
                        dve.wait_ge(S["s_done"], n + 1)
                        wait(dve, S["exp_done"], n - 1)
                        dve.tensor_reduce(nmax[:, k % 2, :].rearrange("p (h w) -> p h w", h=2),
                                          ps_s[k % 2][:, :, :].rearrange("p h (w n) -> p h w n", w=2)[:, :, :, 0:P * (t + 1)],
                                          AX_X, ALU.max, negate=True).then_inc(S["max_done"], 1)
                    if on(0) and k <= G:
                        dve.wait_ge(S["p_done"], 6 * s + (k + 1))
                        wait(dve, S["rot_done"], (G + 1) * s + max(k - 1, 0))
                        tab, r = int(k == G), k % 2
                        for j, (x, f) in enumerate(((0, 0), (1, 1), (1, 0), (0, 1))):
                            last = dve.scalar_tensor_tensor(out=prod[:, r, j, :], in0=ps_p[:, SEQ * x:SEQ * x + SEQ],
                                                            scalar=bq[:, k, x:x + 1], in1=rope[:, tab, f, :],
                                                            op0=ALU.add, op1=ALU.mult)
                        last.then_inc(S["rope_done"], 1)
                    if on(0) and k == G + 1:
                        dve.wait_ge(S["p_done"], 6 * (s + 1))
                        wait(dve, S["pv_done"], U * (s - 1))
                        for t in range(2):
                            last = dve.tensor_tensor(v[:, u, t, :, 0:HD],
                                                     ps_p[:, SEQ * t:SEQ * t + SEQ].rearrange("p (g d) -> p g d", g=NKV),
                                                     rows[:, R_BV1:R_BV1 + SEQ].rearrange("p (g d) -> p g d", g=NKV), ALU.add)
                        last.then_inc(S["v_done"], 1)
                    if (on(1) if k >= 2 else on(2)):
                        b, kk = (s - 1 if k >= 2 else s - 2), (k - 2) % U
                        n, t = b * U + kk, kk // NKV
                        dve.wait_ge(S["t_done"], n + 1)
                        wait(dve, S["pv_done"], n - 1)
                        dve.tensor_copy(pt[:, kk % 2, 1, 0:t + 1, :], ps_t[:, 1, 0:SEQ * (t + 1)].rearrange("p (a n) -> p a n", n=SEQ)
                                        ).then_inc(S["td_done"], 1)
                    if (on(1) if k >= 3 else on(2)):
                        b, kk = (s - 1 if k >= 3 else s - 2), (k - 3) % U
                        n, t, g = b * U + kk, kk // NKV, kk % NKV
                        heads = ps_o[:, 0:G * (HD + 1)].rearrange("p (h d) -> p h d", h=G)
                        dve.wait_ge(S["pv_done"], n + 1)
                        dve.reciprocal(rden[:, kk % 2, :], heads[:, :, HD]).then_inc(S["rd_done"], 1)
                        dve.wait_ge(S["rd_done"], n + 1)
                        if g == 0:
                            wait(dve, S["ot_ps"], 2 * (b - 1) + (t + 1))
                        dve.tensor_tensor(o[:, t, G * g:G * g + G, :], heads[:, :, 0:HD],
                                          window(rden[:, kk % 2, :], [(1, G), (0, HD)]), ALU.mult).then_inc(S["o_done"], 1)
                    if on(2) and k >= 6:
                        b, t = s - 2, k - 6
                        dve.wait_ge(S["wo_ps"], 2 * b + (t + 1))
                        dve.tensor_tensor(s_all[:, bass.ds(2 * b + t, 1), :].rearrange("p a d -> p (a d)"), ps_p[:, 0:P],
                                          rows[:, R_BO1:R_BO1 + P], ALU.add).then_inc(S["wo_done"], 1)

            steps(dve, NB, DEPTH, LEAD, step)
            dve.wait_ge(S["wo_done"], 2 * NB)


def mixture_by_slots(nc, outer, io):
    with ExitStack() as ctx:
        sb = lambda n, s, d=F32: ctx.enter_context(nc.sbuf_tensor("d_" + n, s, d))
        ps = lambda n, s, d=F32: ctx.enter_context(nc.psum_tensor("d_" + n, s, d))
        ident = outer["ident"]
        FC = FF // P
        TC = 4
        CT = TC * P
        w1 = sb("w1", [P, 2, FF])
        w2 = sb("w2", [P, 2, FC, P])
        b1 = sb("b1", [P, 2, FC])
        b1s = sb("b1s", [P, 2, FC])
        b2 = sb("b2", [P, 2, P])
        xin = sb("xin", [P, 2, 2, TC, P])
        xt = sb("xt", [P, 2, CT])
        h = sb("h", [P, 2, FC, CT])
        y = sb("y", [P, 2, TC, P])
        ps_t = ps("ps_t", [P, CT])
        ps_h = [ps(f"ps_h{k}", [P, 2, CT]) for k in range(2)]
        ps_o = [ps(f"ps_o{k}", [P, TC, P]) for k in range(2)]
        names = "b1_done t_done xt_done up_done gelu_done down_done y_done".split()
        S = {n: ctx.enter_context(nc.semaphore("d_" + n)) for n in names}
        loaded = [ctx.enter_context(nc.semaphore(f"d_loaded{u}")) for u in range(2)]
        stored = [ctx.enter_context(nc.semaphore(f"d_stored{u}")) for u in range(2)]
        LOADS = 5
        block = ctx.enter_context(nc.Block())

        @block.sync
        def _(sp):
            def step(s, u, turn, on):
                if on(0):
                    wait(sp, S["y_done"], 2 * (s - 1))
                    sp.dma_start(xin[:, u, :, :, :], io["slots_in"].rearrange("(n p) d -> p n d", p=P)
                                 [:, bass.ds(s * 2 * TC, 2 * TC), :].rearrange("p (c t) d -> p c t d", c=2)).then_inc(loaded[u], 16)
                    sp.dma_start(w1[:, u, :], io["ffn1_w1"][bass.ds(s * P, P), :]).then_inc(loaded[u], 16)
                    sp.dma_start(w2[:, u, :, :].rearrange("p j d -> p (j d)"), io["ffn1_w2"][bass.ds(s * P, P), :]).then_inc(loaded[u], 16)
                    sp.dma_start(b1[:, u, :], io["ffn1_b1"][bass.ds(s * P, P), :]).then_inc(loaded[u], 16)
                    sp.dma_start(b2[:, u, :], io["ffn1_b2"][bass.ds(s, 1), :].rearrange("a d -> (a d)").partition_broadcast(P)
                                 ).then_inc(loaded[u], 16)

            steps(sp, E, 1, 2, step)

        @block.gpsimd
        def _(pool):
            slots = io["slots_out"].rearrange("(n p) d -> p n d", p=P)

            def step(s, u, turn, on):
                for c in range(2):
                    if on(1):
                        pool.wait_ge(S["y_done"], 2 * s - 1 + c)
                        pool.dma_start(slots[:, bass.ds((s - 1) * 2 * TC + c * TC, TC), :], y[:, c, :, :]).then_inc(stored[c], 16)

            steps(pool, E, 1, 2, step)
            for c in range(2):
                pool.wait_ge(stored[c], 16 * E)

        @block.tensor
        def _(pe):
            def turn_x(s, u, turn, c):
                m = 2 * s + c
                if c == 0:
                    pe.wait_ge(loaded[u], 16 * LOADS * (turn + 1))
                wait(pe, S["xt_done"], m)
                for t in range(TC):
                    last = pe.transpose(ps_t[:, P * t:P * t + P], xin[:, u, c, t, :], ident[:, :])
                last.then_inc(S["t_done"], 1)

            def up(s, u, c):
                m = 2 * s + c
                pe.wait_ge(S["xt_done"], m + 1)
                for q in range(2):
                    wait(pe, S["gelu_done"], 2 * m - 1 + q)
                    for j in range(2):
                        last = pe.matmul(ps_h[q][:, j, :], w1[:, u, P * (2 * q + j):P * (2 * q + j) + P], xt[:, c, :],
                                         start=True, stop=True)
                    last.then_inc(S["up_done"], 1)

            def down(s, u, c):
                m = 2 * s + c
                pe.wait_ge(S["gelu_done"], 2 * m + 2)
                wait(pe, S["y_done"], m - 1)
                for t in range(TC):
                    for j in range(FC):
                        last = pe.matmul(ps_o[c][:, t, :], h[:, c, j, P * t:P * t + P], w2[:, u, j, :],
                                         start=(j == 0), stop=(j == FC - 1))
                last.then_inc(S["down_done"], 1)

            def step(s, u, turn, on):
                if on(0):
                    turn_x(s, u, turn, 0)
                if on(1):
                    down(s - 1, 1 - u, 1)
                if on(0):
                    up(s, u, 0)
                    turn_x(s, u, turn, 1)
                    up(s, u, 1)
                    down(s, u, 0)

            steps(pe, E, 1, 2, step)

        @block.scalar
        def _(act):
            def step(s, u, turn, on):
                for c in range(2):
                    if on(0):
                        m = 2 * s + c
                        act.wait_ge(S["t_done"], m + 1)
                        act.activation(xt[:, c, :], ps_t[:, :], ACT.Copy).then_inc(S["xt_done"], 1)
                        if c == 0:
                            act.wait_ge(S["b1_done"], s + 1)
                        wait(act, S["down_done"], m - 1)
                        for q in range(2):
                            act.wait_ge(S["up_done"], 2 * m + q + 1)
                            for j in range(2):
                                last = act.activation(h[:, c, 2 * q + j, :], ps_h[q][:, j, :], ACT.Gelu,
                                                      bias=b1s[:, u, 2 * q + j:2 * q + j + 1], scale=GS)
                            last.then_inc(S["gelu_done"], 1)

            steps(act, E, 1, 2, step)

        @block.vector
        def _(dve):
            def step(s, u, turn, on):
                for c in range(2):
                    if c == 0 and on(0):
                        dve.wait_ge(loaded[u], 16 * LOADS * (turn + 1))
                        wait(dve, S["gelu_done"], 4 * (s - 1))
                        dve.tensor_scalar(b1s[:, u, :], b1[:, u, :], GS, None, ALU.mult).then_inc(S["b1_done"], 1)
                    if on(1):
                        m = 2 * (s - 1) + c
                        dve.wait_ge(S["down_done"], m + 1)
                        wait(dve, stored[c], 16 * (s - 1))
                        dve.scalar_tensor_tensor(out=y[:, c, :, :], in0=ps_o[c][:, :, :], scalar=1.0 / GS,
                                                 in1=window(b2[:, 1 - u, :], [(0, TC), (1, P)]),
                                                 op0=ALU.mult, op1=ALU.add).then_inc(S["y_done"], 1)

            steps(dve, E, 1, 2, step)


def gather_and_gate(nc, outer, io):
    with ExitStack() as ctx:
        sb = lambda n, s, d=F32: ctx.enter_context(nc.sbuf_tensor("e_" + n, s, d))
        x_all, s_all, slot = outer["x"], outer["s"], outer["slot"]
        TC = 4
        NC = NT // TC
        CT = TC * P
        y = sb("y", [P, 2, TC, P])
        idx = sb("idx", [P, 2, TC], U32)
        th = sb("th", [P, 2, CT])
        z = sb("z", [P, 2, CT])
        x2 = sb("x2", [P, 2, CT])
        S = {n: ctx.enter_context(nc.semaphore("e_" + n)) for n in "idx_done th_done z1_done z_done x2_done".split()}
        loaded, gathered, stored = ([ctx.enter_context(nc.semaphore(f"e_{n}{u}")) for u in range(2)]
                                    for n in ("loaded", "gathered", "stored"))
        LEAD, DEPTH = 4, 2
        flat = lambda t: t[:, :, :].rearrange("p n d -> p (n d)")
        block = ctx.enter_context(nc.Block())

        @block.sync
        def _(sp):
            def step(s, u, turn, on):
                if on(0):
                    wait(sp, S["z1_done"], s - 1)
                    sp.dma_start(y[:, u, :, :], io["xn1"].rearrange("(n p) d -> p n d", p=P)[:, bass.ds(s * TC, TC), :]
                                 ).then_inc(loaded[u], 16)
                if on(2):
                    sp.wait_ge(S["x2_done"], s - 1)
                    sp.dma_start(io["out"].rearrange("(n p) d -> p n d", p=P)[:, bass.ds((s - 2) * TC, TC), :],
                                 x2[:, u, :].rearrange("p (t d) -> p t d", t=TC)).then_inc(stored[u], 16)

            steps(sp, NC, DEPTH, LEAD, step)
            for u in range(2):
                sp.wait_ge(stored[u], 16 * NC // 2)

        @block.gpsimd
        def _(pool):
            def step(s, u, turn, on):
                if on(0):
                    pool.wait_ge(S["idx_done"], s + 1)
                    pool.wait_ge(loaded[u], 16 * (turn + 1))
                if on(2):
                    wait(pool, stored[u], 16 * (turn - 1))
                    pool.wait_ge(S["z_done"], s - 1)
                    pool.tensor_tensor(x2[:, u, :], z[:, u, :], flat(x_all)[:, bass.ds((s - 2) * CT, CT)], ALU.add
                                       ).then_inc(S["x2_done"], 1)
                if on(0):
                    for t in range(TC):
                        pool.indirect_dma_start(
                            out=y[:, u, t, :], out_offset=None, in_=io["slots_out"],
                            in_offset=bass.IndirectOffsetOnAxis(ap=idx[:, u, t:t + 1], axis=0),
                            bounds_check=E * CAP - 1, oob_is_err=False).then_inc(gathered[u], 16)

            steps(pool, NC, DEPTH, LEAD, step)

        @block.scalar
        def _(act):
            def step(s, u, turn, on):
                if on(1):
                    b, r = s - 1, 1 - u
                    act.wait_ge(gathered[r], 16 * TC * (turn + u))
                    act.activation(th[:, r, :], y[:, r, :, :].rearrange("p t n -> p (t n)"), ACT.Tanh, scale=0.5).then_inc(S["th_done"], 1)

            steps(act, NC, DEPTH, LEAD, step)

        @block.vector
        def _(dve):
            def step(s, u, turn, on):
                if on(0):
                    wait(dve, gathered[u], 16 * TC * turn)
                    dve.tensor_copy(idx[:, u, :], slot[:, bass.ds(s * TC, TC)]).then_inc(S["idx_done"], 1)
                if on(1):
                    b, r = s - 1, 1 - u
                    dve.wait_ge(S["th_done"], b + 1)
                    wait(dve, S["x2_done"], b - 1)
                    dve.scalar_tensor_tensor(out=z[:, r, :], in0=th[:, r, :], scalar=1.0,
                                             in1=y[:, r, :, :].rearrange("p t n -> p (t n)"), op0=ALU.add, op1=ALU.mult
                                             ).then_inc(S["z1_done"], 1)
                    dve.wait_ge(S["z1_done"], b + 1)
                    dve.scalar_tensor_tensor(out=z[:, r, :], in0=z[:, r, :], scalar=0.5, in1=flat(s_all)[:, bass.ds(b * CT, CT)],
                                             op0=ALU.mult, op1=ALU.mult).then_inc(S["z_done"], 1)

            steps(dve, NC, DEPTH, LEAD, step)


def program(nc, io):
    with ExitStack() as ctx:
        sb = lambda n, s, d=F32: ctx.enter_context(nc.sbuf_tensor(n, s, d))
        outer = {
            "x": sb("x_all", [P, NT, D]), "s": sb("s_all", [P, NT, D]),
            "logits1": sb("logits1", [P, NT, E]), "ident": sb("ident", [P, P]), "identb": sb("identb", [P, P], BF16),
            "mask": sb("mask", [P, P]), "maskb": sb("maskb", [P, P], BF16), "rows": sb("rows", [P, R_COLS]),
            "ones": sb("ones", [P, P]), "upto": sb("upto", [P, P]), "slot": sb("slot", [P, NT], U32),
        }
        with ExitStack() as c2:
            s_id = c2.enter_context(nc.semaphore("s_id"))
            s_z = c2.enter_context(nc.semaphore("s_z"))
            s_rows = c2.enter_context(nc.semaphore("s_rows"))
            block = c2.enter_context(nc.Block())

            @block.sync
            def _(sp):
                sp.dma_start(outer["rows"][:, :], io["rows"].partition_broadcast(P)).then_inc(s_rows, 16)
                sp.wait_ge(s_rows, 16)

            @block.gpsimd
            def _(pool):
                pool.memset(outer["ident"][:, :], 0.0).then_inc(s_z, 1)
                pool.memset(outer["mask"][:, :], 0.0).then_inc(s_z, 1)
                pool.memset(outer["upto"][:, :], 1.0).then_inc(s_z, 1)
                pool.wait_ge(s_z, 3)
                pool.affine_select(out=outer["ident"][:, :], in_=outer["ident"][:, :], compare_op=ALU.not_equal, fill=1.0,
                                   base=0, pattern=[[-1, P]], channel_multiplier=1).then_inc(s_id, 1)
                pool.affine_select(out=outer["mask"][:, :], in_=outer["mask"][:, :], compare_op=ALU.is_ge, fill=MASKED,
                                   base=0, pattern=[[-1, P]], channel_multiplier=1).then_inc(s_id, 1)

                pool.affine_select(out=outer["upto"][:, :], in_=outer["upto"][:, :], compare_op=ALU.is_ge, fill=0.0,
                                   base=0, pattern=[[1, P]], channel_multiplier=-1).then_inc(s_id, 1)
                pool.wait_ge(s_id, 3)

            @block.vector
            def _(dve):
                dve.memset(outer["ones"][:, :], 1.0)
                dve.wait_ge(s_id, 3)
                dve.tensor_copy(outer["identb"][:, :], outer["ident"][:, :])
                dve.tensor_copy(outer["maskb"][:, :], outer["mask"][:, :]).then_inc(s_z, 1)
                dve.wait_ge(s_z, 4)
        with ExitStack() as first:
            sb1 = lambda n, s, d=F32: first.enter_context(nc.sbuf_tensor(n, s, d))
            layer = dict(outer, xnt=sb1("xnt_all", [P, NT * P]), logits0=sb1("logits0", [P, NT, E]),
                         ffn0_w1=[sb1(f"ffn0_w1_{n}", [P, E + 1, H0], F32R) for n in ("high", "low")])
            local_and_topk_attention(nc, layer, io)
            mixture_of_all_experts(nc, layer, io)
        route_to_slots(nc, outer, io)
        rotary_attention(nc, outer, io)
        mixture_by_slots(nc, outer, io)
        gather_and_gate(nc, outer, io)




def rope_tables():
    import numpy as np

    inv = (1.0 / np.float32(10000.0) ** (np.arange(0, HD, 2, dtype=np.float32) / np.float32(HD))).astype(np.float32)
    ang = (np.arange(SEQ, dtype=np.float32)[None, :] * inv[:, None]).astype(np.float32).astype(np.float64)
    one = np.stack([np.cos(ang), np.sin(ang)], axis=1)
    return np.tile(np.stack([one / HD ** 0.5, one], axis=1), (4, 1, 1, 1)).astype(np.float32)


def kernel(**inputs):
    import numpy as _np
    import concourse.bacc as _bacc
    from concourse import mybir as _mybir
    from concourse.bass_utils import run_bass_kernel_spmd as _run

    x = {k: _np.asarray(v) for k, v in inputs.items()}
    col = lambda v: v.reshape(-1, 1)
    halves = lambda w: w.reshape(len(w), -1, 4, 2, HD // 2).transpose(0, 1, 3, 2, 4).reshape(len(w), -1, 2, P)
    arrays = {
        "x": x["L0_attn_mu"].reshape(NB * SEQ, D),
        "w0": _np.concatenate([x["L0_attn_Wq"], x["L0_attn_Wk"], x["L0_attn_Wm1"][:D], x["L0_attn_Wm1"][D:],
                               x["L0_attn_Wv"], x["L0_attn_Wm2"], x["L0_attn_Wo"][:D], x["L0_attn_Wo"][D:],
                               x["L0_ffn_router_w"], col(x["L0_attn_bq"]), col(x["L0_attn_bk"]), col(x["L0_attn_bm1"]),
                               col(x["L0_attn_bv"]), col(x["L0_attn_bm2"])], axis=1),
        "rows": _np.concatenate([x["L0_attn_bo"], x["L0_ffn_router_b"], x["L1_ffn_b_sw"], x["L1_attn_bo"],
                                 x["L1_attn_bv"], _np.arange(E, 0, -1, dtype=_np.float32),
                                 CAP * _np.arange(E, dtype=_np.float32)]),
        "ffn0_w1": _np.concatenate([x["L0_ffn_sw1"][None], x["L0_ffn_rw1"]]).transpose(1, 0, 2),
        "ffn0_b1": _np.concatenate([x["L0_ffn_sb1"][None], x["L0_ffn_rb1"]]).reshape(-1, P).T,
        "ffn0_w2": _np.concatenate([x["L0_ffn_sw2"][None], x["L0_ffn_rw2"]]).reshape(E + 1, H0 // P, P, D).transpose(2, 0, 1, 3),
        "ffn0_b2": _np.concatenate([x["L0_ffn_rb2"], x["L0_ffn_sb2"][None]]),
        "wsw": x["L1_ffn_W_sw"],
        "wq1": _np.concatenate([halves(x["L1_attn_Wq"]), halves(x["L1_attn_Wk"])], axis=1),
        "bq1": _np.concatenate([halves(x["L1_attn_bq"][None])[0], halves(x["L1_attn_bk"][None])[0]]).transpose(2, 0, 1),
        "wv1": x["L1_attn_Wv"],
        "wo1": x["L1_attn_Wo"].reshape(NQ // 2, P, D).transpose(1, 0, 2),
        "rope": rope_tables(),
        "ffn1_w1": x["L1_ffn_W1"].reshape(E * P, FF),
        "ffn1_w2": x["L1_ffn_W2"].reshape(E, FF // P, P, D).transpose(0, 2, 1, 3).reshape(E * P, FF // P * D),
        "ffn1_b1": x["L1_ffn_b1"].reshape(E, FF // P, P).transpose(0, 2, 1).reshape(E * P, FF // P),
        "ffn1_b2": x["L1_ffn_b2"],
    }
    arrays = {f"{k}_dram": _np.ascontiguousarray(v) for k, v in arrays.items()}
    nc = _bacc.Bacc("TRN2", target_bir_lowering=False, num_devices=1)
    io = {k[:-5]: nc.dram_tensor(k, a.shape, _mybir.dt.from_np(a.dtype), kind="ExternalInput").ap()
          for k, a in arrays.items()}
    io["out"] = nc.dram_tensor("out_dram", (NB * SEQ, D), F32, kind="ExternalOutput").ap()
    io["xn1"] = nc.dram_tensor("xn1_scratch", (NB * SEQ, D), F32, kind="Internal").ap()
    io["xnt1"] = nc.dram_tensor("xnt1_scratch", (P, NB * SEQ), F32, kind="Internal").ap()
    io["slots_in"] = nc.dram_tensor("slots_in_scratch", (E * CAP, D), F32, kind="Internal").ap()
    io["slots_out"] = nc.dram_tensor("slots_out_scratch", (E * CAP, D), F32, kind="Internal").ap()
    program(nc, io)
    r = _run(nc, [arrays], core_ids=[0])
    return r.results[0]["out_dram"].reshape(NB, SEQ, D)
```

```python
from contextlib import ExitStack

import concourse.bass as bass
from concourse import mybir

F32 = mybir.dt.float32
F32R = mybir.dt.float32r
BF16 = mybir.dt.bfloat16
U32 = mybir.dt.uint32
ALU = mybir.AluOpType
ACT = mybir.ActivationFunctionType
AX_X = mybir.AxisListType.X

P = 128
D = 128
SEQ = 256
NB = 32
NT = NB * SEQ // P
WIN = 4
TOPK = 8
E = 8
H0 = 256
NQ, NKV, HD = 16, 4, 64
FF = 512
CAP = NB * SEQ // E
EPS = 1e-5
MASKED = -1e30
TAKEN = -3e38
FAR = 1e6
GS = 2.0 ** 0.5 / 1.41421

W0 = {n: slice(P * k, P * k + P) for k, n in enumerate(["q", "k", "m1a", "m1b", "v", "m2", "oa", "ob"])}
W0_ROUTER = slice(8 * P, 8 * P + E)
W0_BIAS = {n: slice(8 * P + E + k, 8 * P + E + k + 1) for k, n in enumerate(["q", "k", "m1", "v", "m2"])}
W0_COLS = 8 * P + E + 5
R_BO0, R_RB0, R_RB1, R_BO1, R_BV1 = 0, 128, 136, 144, 272
R_PREF, R_SLOT, R_LAST = 528, 536, 544
R_COLS = 552


def wait(eng, sem, value):
    if not (isinstance(value, int) and value <= 0):
        eng.wait_ge(sem, value)


def steps(eng, rounds, depth, lead, step, tail=0):
    for s in range(lead):
        step(s, s % 2, s // 2, lambda k: 0 <= s - k)
    with eng.Fori(0, (rounds - lead - tail) // 2) as i:
        for u in range(2):
            step(2 * i + (lead + u), u, i + lead // 2, lambda k: True)
    for s in range(rounds - tail, rounds + depth):
        step(s, s % 2, s // 2, lambda k: s - k < rounds)


def window(ap, pattern, offset=0):
    return bass.AP(ap.tensor, ap.offset + offset, [list(ap.ap[0])] + [list(x) for x in pattern])


def product_of_parts(pe, out, lhs, rhs, start=True, stop=True):
    pe.matmul(out, lhs[0], rhs[0], start=start, stop=False)
    pe.matmul(out, lhs[1], rhs[0], start=False, stop=False)
    return pe.matmul(out, lhs[0], rhs[1], start=False, stop=stop)


def norm_statistics(dve, stats, mean, var, tmp, chain, done):
    even, odd = stats[:, :, 1], stats[:, :, 4]
    dve.tensor_tensor(mean, even, odd, ALU.add)
    dve.tensor_tensor(tmp, even, odd, ALU.subtract)
    dve.tensor_tensor(var, stats[:, :, 2], stats[:, :, 5], ALU.add).then_inc(chain, 1)
    dve.wait_ge(chain, done + 1)
    dve.tensor_scalar(mean, mean, 0.5, None, ALU.mult)
    dve.tensor_tensor(tmp, tmp, tmp, ALU.mult)
    dve.tensor_scalar(var, var, 1.0 / D, None, ALU.mult).then_inc(chain, 1)
    dve.wait_ge(chain, done + 2)
    dve.tensor_scalar(tmp, tmp, 0.25, None, ALU.mult).then_inc(chain, 1)
    dve.wait_ge(chain, done + 3)
    dve.tensor_tensor(var, var, tmp, ALU.add).then_inc(chain, 1)
    dve.wait_ge(chain, done + 4)


def local_and_topk_attention(nc, outer, io):
    with ExitStack() as ctx:
        sb = lambda n, s, d=F32: ctx.enter_context(nc.sbuf_tensor("a_" + n, s, d))
        ps = lambda n, s, d=F32: ctx.enter_context(nc.psum_tensor("a_" + n, s, d))
        sem = lambda n: ctx.enter_context(nc.semaphore("a_" + n))
        x_all, s_all, xnt_all, logits0 = outer["x"], outer["s"], outer["xnt"], outer["logits0"]
        ident, identb, maskb, rows = outer["ident"], outer["identb"], outer["maskb"], outer["rows"]

        w = sb("w", [P, W0_COLS])
        wt = sb("wt", [P, 2, P])
        wvo = sb("wvo", [P, P + E])
        wm2o = sb("wm2o", [P, P])
        bcols = sb("bcols", [P, 2, P])
        vbias = sb("vbias", [P, P])
        stats = sb("stats", [P, NT, 6])
        mean, var, std, rstd = (sb(n, [P, NT]) for n in ("mean", "var", "std", "rstd"))
        xn = sb("xn", [P, 2, SEQ])
        xnt = sb("xnt", [P, 2, SEQ])
        qk = sb("qk", [P, 2, 2, SEQ])
        amsg = sb("amsg", [P, 2, SEQ])
        bmsg = sb("bmsg", [P, 2, WIN + SEQ])
        pre = sb("pre", [P, 2, WIN * SEQ])
        th = sb("th", [P, 2, WIN * SEQ])
        act4 = sb("act4", [P, WIN * SEQ])
        msum = sb("msum", [P, 2, SEQ])
        top = sb("top", [P, 2, 2, 8])
        nmax = sb("nmax", [P, 2, 2])
        rest = sb("rest", [P, 2, 384])
        ex = sb("ex", [P, 2, 384])
        ex8 = sb("ex8", [P, 2, 8])
        den = sb("den", [P, 2, 2])
        rden = sb("rden", [P, 2, 2])
        prob = sb("prob", [P, 2, 384])
        probt = sb("probt", [P, 2, 384])
        gn = sb("gn", [P, 2, SEQ])
        w1, w1_parts = sb("w1", [P, E + 1, H0]), outer["ffn0_w1"]

        ps_t = ps("ps_t", [P, 512])
        ps_qk = ps("ps_qk", [P, 512])
        ps_ab = ps("ps_ab", [P, 512])
        ps_v = ps("ps_v", [P, 512])
        ps_s = [ps(f"ps_s{k}", [P, 512]) for k in range(2)]
        ps_pt = ps("ps_pt", [P, 512])
        ps_gl = ps("ps_gl", [P, 512])

        names = """w1_in w1_high w1_low w_in wt_ps wt_sb bc fold_ps fold_sb vb_ps ready zero
            st var_done std_done rs_done chain xn_done t_done xnt_done copied qk_ps qk_done ab_ps ab_done v_ps v_done
            s_done max_done rest_done nm_done ex_done den_done rden_done prob_done pt_ps pt_done pre_done th_done
            act4_done sum_done l_done g_done gn_done s0_done""".split()
        S = {n: sem(n) for n in names}
        XC = 16
        x_in = [sem(f"x_in{c}") for c in range(NT // XC)]
        LEAD, DEPTH = 6, 5
        SC = float(D) ** -0.5
        vw = ps_v[:, 0:2 * (P + E)].rearrange("p (t n) -> p t n", t=2)
        block = ctx.enter_context(nc.Block())

        @block.sync
        def _(sp):
            sp.dma_start(w[:, :], io["w0"]).then_inc(S["w_in"], 16)
            xv = io["x"].rearrange("(n p) d -> p n d", p=P)
            for c, sem_x in enumerate(x_in):
                n = slice(c * XC, c * XC + XC)
                sp.dma_start(x_all[:, n, :], xv[:, n, :]).then_inc(sem_x, 16)
            sp.dma_start(w1[:, :, :], io["ffn0_w1"]).then_inc(S["w1_in"], 16)
            for sem_x in x_in:
                sp.wait_ge(sem_x, 16)

        @block.gpsimd
        def _(pool):
            pool.memset(bmsg[:, :, 0:WIN], 0.0).then_inc(S["zero"], 1)
            pool.wait_ge(S["w1_high"], 1)
            pool.tensor_tensor(w1_parts[1][:, :, :], w1[:, :, :], w1_parts[0][:, :, :], ALU.subtract).then_inc(S["w1_low"], 1)
            pool.wait_ge(S["zero"], 1)

            def step(s, u, turn, on):
                if on(2):
                    b, r = s - 2, u
                    pool.wait_ge(S["ab_done"], b + 1)
                    wait(pool, S["act4_done"], b - 1)
                    pool.tensor_tensor(
                        pre[:, r, :].rearrange("p (w n) -> p w n", w=WIN),
                        window(amsg[:, r, :], [(0, WIN), (1, SEQ)]),
                        window(bmsg[:, r, :], [(1, WIN), (1, SEQ)]), ALU.add).then_inc(S["pre_done"], 1)
                if on(1):
                    b, r = s - 1, 1 - u
                    pool.wait_ge(S["xnt_done"], b + 1)
                    pool.tensor_copy(xnt_all[:, bass.ds(b * SEQ, SEQ)], xnt[:, r, :]).then_inc(S["copied"], 1)

            steps(pool, NB, DEPTH, LEAD, step)

        @block.tensor
        def _(pe):
            pe.wait_ge(S["w_in"], 16)
            pe.transpose(ps_t[:, 0:P], w[:, W0["v"]], ident[:, :])
            pe.transpose(ps_t[:, P:2 * P], w[:, W0["m2"]], ident[:, :]).then_inc(S["wt_ps"], 1)
            pe.wait_ge(S["wt_sb"], 1)
            pe.matmul(ps_qk[:, 0:P], wt[:, 0, :], w[:, W0["ob"]], start=True, stop=True)
            pe.matmul(ps_qk[:, P:2 * P], wt[:, 1, :], w[:, W0["oa"]], start=True, stop=True).then_inc(S["fold_ps"], 1)
            pe.wait_ge(S["bc"], 2)
            pe.matmul(ps_ab[:, 0:P], bcols[:, 0, :], w[:, W0["ob"]], start=True, stop=False)
            pe.matmul(ps_ab[:, 0:P], bcols[:, 1, :], w[:, W0["oa"]], start=False, stop=True).then_inc(S["vb_ps"], 1)
            pe.wait_ge(S["ready"], 4)

            def step(s, u, turn, on):
                if on(2):
                    b, r = s - 2, u
                    pe.wait_ge(S["qk_done"], b + 1)
                    wait(pe, S["ex_done"], b - 1)
                    sc = ps_s[r]
                    pe.matmul(sc[:, 0:P], identb[:, :], maskb[:, :], start=True, stop=False, skip_group_check=True)
                    pe.matmul(sc[:, 2 * P:3 * P], identb[:, :], maskb[:, :], start=False, stop=False, skip_group_check=True)
                    pe.matmul(sc[:, 0:P], qk[:, r, 0, 0:P], qk[:, r, 1, 0:P], start=False, stop=False, skip_group_check=True)
                    pe.matmul(sc[:, P:3 * P], qk[:, r, 0, P:SEQ], qk[:, r, 1, :], start=False, stop=True,
                              skip_group_check=True).then_inc(S["s_done"], 1)
                if on(1):
                    b, r = s - 1, 1 - u
                    pe.wait_ge(S["xnt_done"], b + 1)
                    wait(pe, S["qk_done"], b)
                    for j, n in enumerate(("q", "k")):
                        last = pe.matmul(ps_qk[:, SEQ * j:SEQ * j + SEQ], w[:, W0[n]], xnt[:, r, :], start=True, stop=True)
                    last.then_inc(S["qk_ps"], 1)
                    wait(pe, S["ab_done"], b)
                    for j, n in enumerate(("m1a", "m1b")):
                        last = pe.matmul(ps_ab[:, SEQ * j:SEQ * j + SEQ], w[:, W0[n]], xnt[:, r, :], start=True, stop=True)
                    last.then_inc(S["ab_ps"], 1)
                    wait(pe, S["v_done"], b)
                    for t in range(2):
                        last = pe.matmul(vw[:, t, :], xnt[:, r, P * t:P * t + P], wvo[:, :], start=True, stop=True)
                    last.then_inc(S["v_ps"], 1)
                if on(3):
                    b, r = s - 3, 1 - u
                    pe.wait_ge(S["prob_done"], b + 1)
                    wait(pe, S["pt_done"], b)
                    for k in range(3):
                        last = pe.transpose(ps_pt[:, P * k:P * k + P], prob[:, r, P * k:P * k + P], ident[:, :])
                    last.then_inc(S["pt_ps"], 1)
                if on(4):
                    b, r = s - 4, u
                    pe.wait_ge(S["sum_done"], b + 1)
                    wait(pe, S["s0_done"], b)
                    for t in range(2):
                        last = pe.matmul(ps_gl[:, SEQ + P * t:SEQ + P * t + P], msum[:, r, P * t:P * t + P], wm2o[:, :],
                                         start=True, stop=True)
                    last.then_inc(S["l_done"], 1)
                    pe.wait_ge(S["pt_done"], b + 1)
                    pe.wait_ge(S["v_done"], b + 1)
                    v = [s_all[:, bass.ds(2 * b + t, 1), :] for t in range(2)]
                    pe.matmul(ps_gl[:, 0:P], probt[:, r, 0:P], v[0], start=True, stop=True)
                    pe.matmul(ps_gl[:, P:SEQ], probt[:, r, P:2 * P], v[0], start=True, stop=False)
                    pe.matmul(ps_gl[:, P:SEQ], probt[:, r, 2 * P:3 * P], v[1], start=False,
                              stop=True).then_inc(S["g_done"], 1)
                if on(0):
                    b, r = s, u
                    pe.wait_ge(S["xn_done"], b + 1)
                    wait(pe, S["xnt_done"], b)
                    for t in range(2):
                        last = pe.transpose(ps_t[:, P * t:P * t + P], xn[:, r, P * t:P * t + P], ident[:, :])
                    last.then_inc(S["t_done"], 1)

            steps(pe, NB, DEPTH, LEAD, step)

        @block.scalar
        def _(act):
            act.wait_ge(S["w1_in"], 16)
            act.activation(w1_parts[0][:, :, :], w1[:, :, :], ACT.Copy).then_inc(S["w1_high"], 1)
            act.wait_ge(S["var_done"], 1)
            act.activation(std[:, :], var[:, :], ACT.Sqrt).then_inc(S["std_done"], 1)
            act.wait_ge(S["wt_ps"], 1)
            act.activation(wt[:, :, :], ps_t[:, 0:2 * P].rearrange("p (a n) -> p a n", a=2), ACT.Copy).then_inc(S["wt_sb"], 1)
            act.wait_ge(S["w_in"], 16)
            act.activation(wvo[:, P:P + E], w[:, W0_ROUTER], ACT.Copy).then_inc(S["ready"], 1)
            act.wait_ge(S["fold_ps"], 1)
            act.activation(wvo[:, 0:P], ps_qk[:, 0:P], ACT.Copy).then_inc(S["ready"], 1)
            act.activation(wm2o[:, :], ps_qk[:, P:2 * P], ACT.Copy, scale=0.5 / WIN).then_inc(S["ready"], 1)

            def step(s, u, turn, on):
                if on(1):
                    b, r = s - 1, 1 - u
                    act.wait_ge(S["qk_ps"], b + 1)
                    wait(act, S["s_done"], b - 1)
                    for j, n in enumerate(("q", "k")):
                        last = act.activation(qk[:, r, j, :], ps_qk[:, SEQ * j:SEQ * j + SEQ], ACT.Identity,
                                              bias=w[:, W0_BIAS[n]])
                    last.then_inc(S["qk_done"], 1)
                    act.wait_ge(S["ab_ps"], b + 1)
                    wait(act, S["pre_done"], b - 1)
                    act.activation(amsg[:, r, :], ps_ab[:, 0:SEQ], ACT.Identity, bias=w[:, W0_BIAS["m1"]])
                    act.activation(bmsg[:, r, WIN:WIN + SEQ], ps_ab[:, SEQ:2 * SEQ], ACT.Copy).then_inc(S["ab_done"], 1)
                if on(2):
                    b, r = s - 2, u
                    act.wait_ge(S["nm_done"], b + 1)
                    wait(act, S["prob_done"], b - 1)
                    wait(act, S["rden_done"], b - 1)
                    for t, c in enumerate((slice(0, P), slice(P, 3 * P))):
                        act.activation(ex8[:, t, :], top[:, r, t, :], ACT.Exp, bias=nmax[:, r, t:t + 1], scale=SC,
                                       accum_out=den[:, r, t:t + 1])
                        last = act.activation(ex[:, r, c], ps_s[r][:, c], ACT.Exp, bias=nmax[:, r, t:t + 1], scale=SC)
                    last.then_inc(S["ex_done"], 1)
                if on(3):
                    b, r = s - 3, 1 - u
                    act.wait_ge(S["pt_ps"], b + 1)
                    wait(act, S["g_done"], b - 1)
                    act.activation(probt[:, r, :], ps_pt[:, 0:384], ACT.Copy).then_inc(S["pt_done"], 1)
                if on(0):
                    b, r = s, u
                    act.wait_ge(S["t_done"], b + 1)
                    wait(act, S["v_ps"], b - 1)
                    wait(act, S["copied"], b - 1)
                    act.activation(xnt[:, r, :], ps_t[:, 0:SEQ], ACT.Copy).then_inc(S["xnt_done"], 1)
                if on(4):
                    b, r = s - 4, u
                    act.wait_ge(S["g_done"], b + 1)
                    act.wait_ge(S["rden_done"], b + 1)
                    wait(act, S["s0_done"], b - 1)
                    for t in range(2):
                        last = act.activation(gn[:, r, P * t:P * t + P], ps_gl[:, P * t:P * t + P], ACT.Copy,
                                              scale=rden[:, r, t:t + 1])
                    last.then_inc(S["gn_done"], 1)
                if on(2):
                    b, r = s - 2, u
                    act.wait_ge(S["pre_done"], b + 1)
                    wait(act, S["act4_done"], b - 1)
                    act.activation(th[:, r, :], pre[:, r, :], ACT.Tanh, scale=0.5).then_inc(S["th_done"], 1)

            steps(act, NB, DEPTH, LEAD, step)

        @block.vector
        def _(dve):
            for c, sem_x in enumerate(x_in):
                dve.wait_ge(sem_x, 16)
                with dve.Fori(0, XC // 8) as i:
                    for u in range(8):
                        n = c * XC + 8 * i + u
                        last = dve.bn_stats(stats[:, bass.ds(n, 1), :], x_all[:, bass.ds(n, 1), :])
                    last.then_inc(S["st"], 1)
            dve.wait_ge(S["st"], NT // 8)
            norm_statistics(dve, stats[:, :, :], mean[:, :], var[:, :], rstd[:, :], S["chain"], 0)
            dve.tensor_scalar(var[:, :], var[:, :], EPS, None, ALU.add).then_inc(S["var_done"], 1)
            dve.wait_ge(S["std_done"], 1)
            dve.reciprocal(rstd[:, :], std[:, :]).then_inc(S["rs_done"], 1)
            dve.wait_ge(S["rs_done"], 1)
            dve.wait_ge(S["w_in"], 16)
            for j, n in enumerate(("v", "m2")):
                dve.tensor_scalar(bcols[:, j, :], outer["ones"][:, 0:P], w[:, W0_BIAS[n]], None, ALU.mult).then_inc(S["bc"], 1)
            dve.wait_ge(S["vb_ps"], 1)
            dve.tensor_tensor(vbias[:, :], ps_ab[:, 0:P], rows[:, R_BO0:R_BO0 + P], ALU.add).then_inc(S["ready"], 1)
            dve.wait_ge(S["ready"], 4)

            def step(s, u, turn, on):
                if on(4):
                    b, r = s - 4, u
                    wait(dve, S["gn_done"], b - 1)
                    dve.reciprocal(rden[:, r, :], den[:, r, :]).then_inc(S["rden_done"], 1)
                if on(3):
                    b, r = s - 3, 1 - u
                    dve.wait_ge(S["ex_done"], b + 1)
                    wait(dve, S["pt_ps"], b - 1)
                    dve.scalar_tensor_tensor(out=prob[:, r, :], in0=rest[:, r, :], scalar=TAKEN, in1=ex[:, r, :],
                                             op0=ALU.is_equal, op1=ALU.mult).then_inc(S["prob_done"], 1)
                if on(5):
                    b, r = s - 5, 1 - u
                    if on(2):
                        wait(dve, S["ex_done"], s - 3)
                        dve.wait_ge(S["s_done"], s - 1)
                    dve.wait_ge(S["gn_done"], b + 1)
                    dve.tensor_tensor(s_all[:, bass.ds(b * 2, 2), :], ps_gl[:, SEQ:2 * SEQ].rearrange("p (t n) -> p t n", t=2),
                                      gn[:, r, :].rearrange("p (t n) -> p t n", t=2), ALU.add).then_inc(S["s0_done"], 1)
                if on(2):
                    b, r = s - 2, u
                    if not on(5):
                        wait(dve, S["ex_done"], s - 3)
                        dve.wait_ge(S["s_done"], s - 1)
                    for t, c in enumerate((slice(0, P), slice(P, 3 * P))):
                        last = dve.max(top[:, r, t, :], ps_s[r][:, c])
                    last.then_inc(S["max_done"], 1)
                    dve.wait_ge(S["max_done"], b + 1)
                    dve.tensor_scalar(nmax[:, r, :], top[:, r, :, 0], -SC, None, ALU.mult)
                    for t, c in enumerate((slice(0, P), slice(P, 3 * P))):
                        last = dve.match_replace(rest[:, r, c], top[:, r, t, :], ps_s[r][:, c], TAKEN)
                    last.then_inc(S["nm_done"], 1)
                if on(0):
                    b, r = s, u
                    wait(dve, S["t_done"], b - 1)
                    for t in range(2):
                        last = dve.tensor_scalar(xn[:, r, P * t:P * t + P], x_all[:, 2 * b + t, :],
                                                 mean[:, bass.ds(2 * b + t, 1)], rstd[:, bass.ds(2 * b + t, 1)],
                                                 ALU.subtract, ALU.mult)
                    last.then_inc(S["xn_done"], 1)
                if on(3):
                    b, r = s - 3, 1 - u
                    dve.wait_ge(S["th_done"], b + 1)
                    wait(dve, S["sum_done"], b)
                    dve.scalar_tensor_tensor(out=act4[:, :], in0=th[:, r, :], scalar=1.0, in1=pre[:, r, :],
                                             op0=ALU.add, op1=ALU.mult).then_inc(S["act4_done"], 1)
                if on(3):
                    b, r = s - 3, 1 - u
                    dve.wait_ge(S["act4_done"], b + 1)
                    wait(dve, S["l_done"], b - 1)
                    dve.tensor_reduce(msum[:, r, :], act4[:, :].rearrange("p (w n) -> p n w", w=WIN), AX_X,
                                      ALU.add).then_inc(S["sum_done"], 1)
                if on(1):
                    b = s - 1
                    dve.wait_ge(S["v_ps"], b + 1)
                    dve.tensor_tensor(s_all[:, bass.ds(b * 2, 2), :], vw[:, :, 0:P], window(vbias[:, :], [(0, 2), (1, P)]), ALU.add)
                    dve.tensor_tensor(logits0[:, bass.ds(b * 2, 2), :], vw[:, :, P:P + E],
                                      window(rows[:, R_RB0:R_RB0 + E], [(0, 2), (1, E)]), ALU.add).then_inc(S["v_done"], 1)

            steps(dve, NB, DEPTH, LEAD, step)
            dve.wait_ge(S["s0_done"], NB)


def softmax_of_experts(dve, link, logits, ex_wait, work, row):
    dve_max = row
    link(dve.tensor_reduce(dve_max, logits, AX_X, ALU.max))
    link(dve.tensor_tensor(work, logits, over_experts(dve_max), ALU.subtract))
    ex_wait()
    link(dve.tensor_reduce(row, work, AX_X, ALU.add))
    link(dve.reciprocal(row, row))
    link(dve.tensor_tensor(work, work, over_experts(row), ALU.mult))


def over_experts(ap):
    return bass.AP(ap.tensor, ap.offset, [list(x) for x in ap.ap] + [[0, E]])


def over_tiles(ap):
    return bass.AP(ap.tensor, ap.offset, [list(ap.ap[0]), [0, NT], [1, E]])


def first_of_the_largest(link, dve, values, out, pref, row):
    link(dve.tensor_reduce(row, values, AX_X, ALU.max))
    link(dve.tensor_tensor(out, values, over_experts(row), ALU.is_equal))
    link(dve.tensor_tensor(out, out, pref, ALU.mult))
    link(dve.tensor_reduce(row, out, AX_X, ALU.max))
    return dve.tensor_tensor(out, out, over_experts(row), ALU.is_equal)


def mixture_of_all_experts(nc, outer, io):
    with ExitStack() as ctx:
        sb = lambda n, s, d=F32: ctx.enter_context(nc.sbuf_tensor("b_" + n, s, d))
        ps = lambda n, s, d=F32: ctx.enter_context(nc.psum_tensor("b_" + n, s, d))
        x_all, s_all, xnt_all, logits0, slot = (outer[k] for k in ("x", "s", "xnt", "logits0", "slot"))
        ident, rows = outer["ident"], outer["rows"]
        NX = E + 1
        HC = H0 // P
        TC = 4
        CT = TC * P
        NC = NT // TC
        w1_parts = outer["ffn0_w1"]
        xnt_parts = [sb(f"xnt_{n}", [P, 2, CT], F32R) for n in ("high", "low")]
        w2 = sb("w2", [P, NX, HC, P])
        b1 = sb("b1", [P, NX * HC])
        b2 = sb("b2", [NX, P])
        wsw = sb("wsw", [P, E])
        probs = sb("probs", [P, NT, E])
        one1 = sb("one1", [P, NT, E])
        one2 = sb("one2", [P, NT, E])
        row = sb("row", [P, NT])
        wx = sb("wx", [P, NT, NX])
        wxs = sb("wxs", [P, 2, TC * NX])
        wt = sb("wt", [NX, 2, CT])
        h = sb("h", [P, 2, HC, CT])
        acc = sb("acc", [P, 2, TC, P])
        th = sb("th", [P, CT])
        z = sb("z", [P, CT])
        x1 = sb("x1", [P, TC, P])
        stats = sb("stats", [P, TC, 6])
        mean, var, std, rstd = (sb(n, [P, TC]) for n in ("mean", "var", "std", "rstd"))
        xs = sb("xs", [P, 2, TC, P])
        logits1 = sb("logits1", [P, TC, E])
        best = sb("best", [P, TC])
        chosen = sb("chosen", [P, TC, E])
        taken = sb("taken", [P, E])
        place = sb("place", [P, TC, E])
        full = sb("full", [P, TC, E])
        idx = sb("idx", [P, 2, TC], U32)
        xst = sb("xst", [P, CT])
        ps_h = [ps(f"ps_h{k}", [P, HC, CT]) for k in range(2)]
        ps_o = [ps(f"ps_o{k}", [P, TC, P]) for k in range(2)]
        ps_m = ps("ps_m", [P, 512])
        ps_t = ps("ps_t", [P, CT])
        counts = ps_m[:, P:P + (TC + 1) * E]
        zeros = sb("zeros", [P, 1024])
        names = """xnt_high xnt_low zeros_set slots_cleared w2_in b_in shifted exped chain ready one wxs_done wt_ps wt_done up_done gelu_done down_done acc_done
            th_done x1_done var_done std_done xs_done kept t_done xst_done r_done logits_done chosen_done count_done place_chain idx_done xst_out""".split()
        S = {n: ctx.enter_context(nc.semaphore("b_" + n)) for n in names}
        xs_out, scattered = ([ctx.enter_context(nc.semaphore(f"b_{n}{u}")) for u in range(2)] for n in ("xs_out", "scattered"))
        LEAD, DEPTH = 4, 2
        CLEARS = E * CAP * D // (P * 1024)
        LINKS, PLACE_LINKS = 12, 6
        block = ctx.enter_context(nc.Block())

        @block.sync
        def _(sp):
            sp.dma_start(b1[:, :], io["ffn0_b1"]).then_inc(S["b_in"], 16)
            sp.dma_start(b2[:, :], io["ffn0_b2"]).then_inc(S["b_in"], 16)
            sp.dma_start(wsw[:, :], io["wsw"]).then_inc(S["b_in"], 16)
            sp.dma_start(w2[:, :, :, :], io["ffn0_w2"]).then_inc(S["w2_in"], 16)
            sp.wait_ge(S["zeros_set"], 1)
            for c in range(CLEARS):
                sp.dma_start(io["slots_in"].rearrange("(c p r) d -> c p (r d)", c=CLEARS, p=P)[c], zeros[:, :]
                             ).then_inc(S["slots_cleared"], 16)

            def step(s, u, turn, on):
                if on(1):
                    c = s - 1
                    sp.wait_ge(S["xs_done"], c + 1)
                    sp.dma_start(io["xn1"].rearrange("(n p) d -> p n d", p=P)[:, bass.ds(c * TC, TC), :],
                                 xs[:, 1 - u, :, :]).then_inc(xs_out[1 - u], 16)
                    sp.wait_ge(S["xst_done"], c + 1)
                    sp.dma_start(io["xnt1"][:, bass.ds(c * CT, CT)], xst[:, :]).then_inc(S["xst_out"], 16)

            steps(sp, NC, DEPTH, LEAD, step)
            sp.wait_ge(S["slots_cleared"], 16 * CLEARS)
            for u in range(2):
                sp.wait_ge(xs_out[u], 16 * NC // 2)
            sp.wait_ge(S["xst_out"], 16 * NC)

        @block.gpsimd
        def _(pool):
            pool.memset(zeros[:, :], 0.0).then_inc(S["zeros_set"], 1)
            pool.memset(wx[:, :, E:NX], 1.0).then_inc(S["one"], 1)
            pool.wait_ge(S["zeros_set"], 1)
            CLEARED = 2
            FIRST = 0

            def split_low(s, u, cols):
                pool.tensor_tensor(xnt_parts[1][:, u, :], xnt_all[:, cols], xnt_parts[0][:, u, :],
                                   ALU.subtract).then_inc(S["xnt_low"], 1)

            def step(s, u, turn, on):
                if on(0):
                    wait(pool, S["up_done"], (s - 1) * NX)
                    cols = bass.ds(s * CT, CT)
                    pool.tensor_copy(xnt_parts[0][:, u, :], xnt_all[:, cols]).then_inc(S["xnt_high"], 1)
                    pool.wait_ge(S["xnt_high"], s + 1)
                    if s is FIRST:
                        split_low(s, u, cols)
                        pool.wait_ge(S["ready"], 1)
                        pool.wait_ge(S["one"], 1)
                    wait(pool, S["wt_ps"], s - 1)
                    pool.tensor_copy(wxs[:, u, :].rearrange("p (t e) -> p t e", t=TC),
                                     wx[:, bass.ds(s * TC, TC), :]).then_inc(S["wxs_done"], 1)
                    if s is not FIRST:
                        split_low(s, u, cols)
                if on(2):
                    pool.wait_ge(S["idx_done"], s - 1)
                    if s is CLEARED:
                        pool.wait_ge(S["slots_cleared"], 16 * CLEARS)
                if on(1):
                    pool.wait_ge(S["x1_done"], s)
                    pool.tensor_copy(x_all[:, bass.ds((s - 1) * TC, TC), :], x1[:, :, :]).then_inc(S["kept"], 1)
                if on(2):
                    for t in range(TC):
                        pool.indirect_dma_start(
                            out=io["slots_in"], out_offset=bass.IndirectOffsetOnAxis(ap=idx[:, u, t:t + 1], axis=0),
                            in_=xs[:, u, t, :], in_offset=None, bounds_check=E * CAP - 1,
                            oob_is_err=False).then_inc(scattered[u], 16)

            steps(pool, NC, DEPTH, LEAD, step)
            pool.wait_ge(S["kept"], NC)
            for u in range(2):
                pool.wait_ge(scattered[u], 16 * TC * NC // 2)

        @block.tensor
        def _(pe):
            pe.wait_ge(S["b_in"], 48)
            pe.wait_ge(S["w2_in"], 16)

            def up(s, u, e):
                g = s * NX + e
                if e == 0:
                    pe.wait_ge(S["xnt_low"], s + 1)
                wait(pe, S["gelu_done"], g if e == 0 else g - 1)
                for j in range(HC):
                    last = product_of_parts(pe, ps_h[e % 2][:, j, :], [w[:, e, P * j:P * j + P] for w in w1_parts],
                                            [x[:, u, :] for x in xnt_parts])
                last.then_inc(S["up_done"], 1)

            def down(s, u, e):
                g = s * NX + e
                pe.wait_ge(S["gelu_done"], g + 1)
                wait(pe, S["acc_done"], g if e == 0 else g - 1)
                if e == 0:
                    pe.wait_ge(S["wt_done"], s + 1)
                for t in range(TC):
                    for j in range(HC):
                        last = pe.matmul(ps_o[e % 2][:, t, :], h[:, e % 2, j, P * t:P * t + P], w2[:, e, j, :],
                                         start=(j == 0), stop=(j == HC - 1 and e > 0))
                    if e == 0:
                        last = pe.matmul(ps_o[0][:, t, :], wt[:, u, P * t:P * t + P], b2[:, :], start=False, stop=True)
                last.then_inc(S["down_done"], 1)

            def step(s, u, turn, on):
                for e in range(NX):
                    if on(0):
                        up(s, u, e)
                    if e == 0 and on(0):
                        pe.wait_ge(S["wxs_done"], s + 1)
                        wait(pe, S["logits_done"], s - 1)
                        wait(pe, S["place_chain"], (s - 2) * PLACE_LINKS)
                        wait(pe, S["wt_done"], s)
                        for t in range(TC):
                            last = pe.transpose(ps_m[0:NX, P * t:P * t + P], wxs[:, u, NX * t:NX * t + NX], ident[:, :])
                        last.then_inc(S["wt_ps"], 1)
                    if e == 0 and on(1):
                        down(s - 1, 1 - u, NX - 1)
                    if e > 0 and on(0):
                        down(s, u, e - 1)
                    if e == 3 and on(2):
                        pe.wait_ge(S["chosen_done"], s - 1)
                        pe.wait_ge(S["wt_done"], s + 1 if on(0) else NC)
                        pe.matmul(counts[:, 0:TC * E], outer["upto"][:, :], chosen[:, :, :].rearrange("p t e -> p (t e)"),
                                  start=True, stop=False, skip_group_check=True)
                        for t in range(TC):
                            last = pe.matmul(counts[:, E * (t + 1):E * (TC + 1)], outer["ones"][:, :],
                                             window(chosen[:, t, :], [(0, TC - t), (1, E)]), start=False, stop=(t == TC - 1),
                                             skip_group_check=True)
                        last.then_inc(S["count_done"], 1)
                    if e == 6 and on(1):
                        pe.wait_ge(S["xs_done"], s)
                        wait(pe, S["xst_done"], s - 1)
                        for t in range(TC):
                            last = pe.transpose(ps_t[:, P * t:P * t + P], xs[:, 1 - u, t, :], ident[:, :])
                        last.then_inc(S["t_done"], 1)
                    if e == 8 and on(1):
                        pe.wait_ge(S["xst_done"], s)
                        pe.wait_ge(S["wt_done"], s + 1 if on(0) else NC)
                        for t in range(TC):
                            last = pe.matmul(ps_m[:, E * t:E * t + E], xst[:, P * t:P * t + P], wsw[:, :], start=True, stop=True)
                        last.then_inc(S["r_done"], 1)

            steps(pe, NC, DEPTH, LEAD, step)

        @block.scalar
        def _(act):
            act.wait_ge(S["shifted"], 1)
            act.activation(probs[:, :, :], probs[:, :, :], ACT.Exp).then_inc(S["exped"], 1)

            def step(s, u, turn, on):
                for e in range(NX):
                    if on(0):
                        g = s * NX + e
                        act.wait_ge(S["up_done"], g + 1)
                        wait(act, S["down_done"], g if e == 0 else g - 1)
                        for j in range(HC):
                            last = act.activation(h[:, e % 2, j, :], ps_h[e % 2][:, j, :], ACT.Gelu,
                                                  bias=b1[:, HC * e + j:HC * e + j + 1])
                        last.then_inc(S["gelu_done"], 1)
                    if e == 0 and on(0):
                        act.wait_ge(S["wt_ps"], s + 1)
                        act.activation(wt[:, u, :], ps_m[0:NX, :], ACT.Copy).then_inc(S["wt_done"], 1)
                    if e == 1 and on(1):
                        act.wait_ge(S["acc_done"], s * NX)
                        act.activation(th[:, :], acc[:, 1 - u, :, :].rearrange("p t n -> p (t n)"), ACT.Tanh,
                                       scale=0.5).then_inc(S["th_done"], 1)
                    if e == 4 and on(1):
                        act.wait_ge(S["var_done"], s)
                        act.activation(std[:, :], var[:, :], ACT.Sqrt).then_inc(S["std_done"], 1)
                    if e == 7 and on(1):
                        act.wait_ge(S["t_done"], s)
                        wait(act, S["xst_out"], (s - 1) * 16)
                        act.activation(xst[:, :], ps_t[:, :], ACT.Copy).then_inc(S["xst_done"], 1)

            steps(act, NC, DEPTH, LEAD, step)

        @block.vector
        def _(dve):
            count = [0]

            def link(ins):
                count[0] += 1
                ins.then_inc(S["chain"], 1)
                dve.wait_ge(S["chain"], count[0])

            def take_exp():
                dve.sem_inc(S["shifted"], 1)
                dve.wait_ge(S["exped"], 1)

            softmax_of_experts(dve, link, logits0[:, :, :], take_exp, probs[:, :, :], row[:, :])
            pref = over_tiles(rows[:, R_PREF:R_PREF + E])
            link(first_of_the_largest(link, dve, probs[:, :, :], one1[:, :, :], pref, row[:, :]))
            flat = lambda t: t[:, :, :].rearrange("p n e -> p (n e)")
            link(dve.scalar_tensor_tensor(out=flat(one2), in0=flat(one1), scalar=-2.0, in1=flat(probs),
                                          op0=ALU.mult, op1=ALU.add))
            link(dve.tensor_copy(wx[:, :, 0:E], one2[:, :, :]))
            link(first_of_the_largest(link, dve, wx[:, :, 0:E], one2[:, :, :], pref, row[:, :]))
            link(dve.tensor_tensor(one1[:, :, :], one1[:, :, :], one2[:, :, :], ALU.add))
            dve.tensor_tensor(wx[:, :, 0:E], one1[:, :, :], probs[:, :, :], ALU.mult).then_inc(S["ready"], 1)
            dve.wait_ge(S["ready"], 1)
            link(dve.tensor_copy(taken[:, :], rows[:, R_SLOT:R_SLOT + E]))
            base = count[0]

            def step(s, u, turn, on):
                def linked(j, ins):
                    ins.then_inc(S["chain"], 1)
                    dve.wait_ge(S["chain"], (s - 1) * LINKS + (base + j + 1))

                for e in range(NX):
                    c, v = (s - 1, 1 - u) if e == 0 else (s, u)
                    done = e - 1 if e else NX - 1
                    if on(1) if e == 0 else on(0):
                        g = c * NX + done
                        dve.wait_ge(S["down_done"], g + 1)
                        if done == 0:
                            dve.tensor_copy(acc[:, v, :, :], ps_o[0][:, :, :]).then_inc(S["acc_done"], 1)
                        else:
                            dve.wait_ge(S["acc_done"], g)
                            for t in range(TC):
                                last = dve.scalar_tensor_tensor(
                                    out=acc[:, v, t, :], in0=ps_o[done % 2][:, t, :],
                                    scalar=wx[:, bass.ds(c * TC + t, 1), done - 1:done],
                                    in1=acc[:, v, t, :], op0=ALU.mult, op1=ALU.add)
                            last.then_inc(S["acc_done"], 1)
                    if e == 2 and on(1):
                        b, r = s - 1, 1 - u
                        dve.wait_ge(S["th_done"], b + 1)
                        linked(0, dve.scalar_tensor_tensor(out=z[:, :], in0=th[:, :], scalar=1.0,
                                                           in1=acc[:, r, :, :].rearrange("p t n -> p (t n)"),
                                                           op0=ALU.add, op1=ALU.mult))
                        linked(1, dve.scalar_tensor_tensor(
                            out=z[:, :], in0=z[:, :], scalar=0.5, op0=ALU.mult, op1=ALU.mult,
                            in1=s_all[:, :, :].rearrange("p n d -> p (n d)")[:, bass.ds(b * CT, CT)]))
                        wait(dve, S["kept"], b)
                        dve.tensor_tensor(x1[:, :, :], z[:, :].rearrange("p (t n) -> p t n", t=TC),
                                          x_all[:, bass.ds(b * TC, TC), :], ALU.add).then_inc(S["x1_done"], 1)
                        dve.wait_ge(S["x1_done"], b + 1)
                    if e == 3 and on(1):
                        for t in range(TC):
                            last = dve.bn_stats(stats[:, t, :], x1[:, t, :])
                        linked(2, last)
                        norm_statistics(dve, stats[:, :, :], mean[:, :], var[:, :], rstd[:, :], S["chain"],
                                        (s - 1) * LINKS + (base + 3))
                        dve.tensor_scalar(var[:, :], var[:, :], EPS, None, ALU.add).then_inc(S["var_done"], 1)
                    if e == 5 and on(1):
                        b = s - 1
                        dve.wait_ge(S["std_done"], b + 1)
                        linked(7, dve.reciprocal(rstd[:, :], std[:, :]))
                        wait(dve, xs_out[1 - u], 16 * (turn + u - 1))
                        wait(dve, scattered[1 - u], 16 * TC * (turn + u - 1))
                        for t in range(TC):
                            last = dve.tensor_scalar(xs[:, 1 - u, t, :], x1[:, t, :], mean[:, t:t + 1], rstd[:, t:t + 1],
                                                     ALU.subtract, ALU.mult)
                        last.then_inc(S["xs_done"], 1)
                    if e == 8 and on(1):
                        b = s - 1
                        dve.wait_ge(S["r_done"], b + 1)
                        dve.tensor_tensor(logits1[:, :, :], ps_m[:, 0:TC * E].rearrange("p (t e) -> p t e", t=TC),
                                          window(rows[:, R_RB1:R_RB1 + E], [(0, TC), (1, E)]), ALU.add).then_inc(S["logits_done"], 1)
                        dve.wait_ge(S["logits_done"], b + 1)
                        links = iter(range(8, LINKS))
                        first_of_the_largest(lambda ins: linked(next(links), ins), dve, logits1[:, :, :], chosen[:, :, :],
                                             window(rows[:, R_PREF:R_PREF + E], [(0, TC), (1, E)]), best[:, :]
                                             ).then_inc(S["chosen_done"], 1)
                        dve.wait_ge(S["chosen_done"], b + 1)
                    if e == 4 and on(2):
                        b = s - 2

                        def placed(j, ins):
                            ins.then_inc(S["place_chain"], 1)
                            dve.wait_ge(S["place_chain"], (s - 2) * PLACE_LINKS + (j + 1))

                        dve.wait_ge(S["count_done"], b + 1)
                        placed(0, dve.tensor_tensor(place[:, :, :], counts[:, 0:TC * E].rearrange("p (t e) -> p t e", t=TC),
                                                    window(taken[:, :], [(0, TC), (1, E)]), ALU.add))
                        placed(1, dve.tensor_tensor(taken[:, :], taken[:, :], counts[:, TC * E:(TC + 1) * E], ALU.add))
                        placed(2, dve.tensor_tensor(full[:, :, :], place[:, :, :],
                                                    window(rows[:, R_LAST:R_LAST + E], [(0, TC), (1, E)]), ALU.is_gt))
                        placed(3, dve.scalar_tensor_tensor(out=place[:, :, :], in0=full[:, :, :], scalar=FAR, in1=place[:, :, :],
                                                           op0=ALU.mult, op1=ALU.add))
                        placed(4, dve.tensor_tensor(place[:, :, :], place[:, :, :], chosen[:, :, :], ALU.mult))
                        placed(5, dve.tensor_reduce(best[:, :], place[:, :, :], AX_X, ALU.add))
                        wait(dve, scattered[u], 16 * TC * (turn - 1))
                        dve.tensor_copy(idx[:, u, :], best[:, :])
                        dve.tensor_copy(slot[:, bass.ds(b * TC, TC)], best[:, :]).then_inc(S["idx_done"], 1)

            steps(dve, NC, DEPTH, LEAD, step)
            dve.wait_ge(S["idx_done"], NC)


def mixture_by_slots(nc, outer, io):
    with ExitStack() as ctx:
        sb = lambda n, s, d=F32: ctx.enter_context(nc.sbuf_tensor("d_" + n, s, d))
        ps = lambda n, s, d=F32: ctx.enter_context(nc.psum_tensor("d_" + n, s, d))
        ident = outer["ident"]
        wq1 = sb("wq1", [P, NQ // 4 + 1, 2, P])
        wv1 = sb("wv1", [P, NKV * HD])
        FC = FF // P
        TC = 4
        CT = TC * P
        w1 = sb("w1", [P, 2, FF])
        w2 = sb("w2", [P, 2, FC, P])
        b1 = sb("b1", [P, 2, FC])
        b1s = sb("b1s", [P, 2, FC])
        b2 = sb("b2", [P, 2, P])
        xin = sb("xin", [P, 2, 2, TC, P])
        xt = sb("xt", [P, 2, CT])
        h = sb("h", [P, 2, FC, CT])
        y = sb("y", [P, 2, TC, P])
        ps_t = ps("ps_t", [P, CT])
        ps_h = [ps(f"ps_h{k}", [P, 2, CT]) for k in range(2)]
        ps_o = [ps(f"ps_o{k}", [P, TC, P]) for k in range(2)]
        names = "next_in next_high next_done b1_done t_done xt_done up_done gelu_done down_done y_done".split()
        S = {n: ctx.enter_context(nc.semaphore("d_" + n)) for n in names}
        loaded = [ctx.enter_context(nc.semaphore(f"d_loaded{u}")) for u in range(2)]
        stored = [ctx.enter_context(nc.semaphore(f"d_stored{u}")) for u in range(2)]
        LOADS = 5
        block = ctx.enter_context(nc.Block())

        @block.sync
        def _(sp):
            def step(s, u, turn, on):
                if on(0):
                    wait(sp, S["y_done"], 2 * (s - 1))
                    sp.dma_start(xin[:, u, :, :, :], io["slots_in"].rearrange("(n p) d -> p n d", p=P)
                                 [:, bass.ds(s * 2 * TC, 2 * TC), :].rearrange("p (c t) d -> p c t d", c=2)).then_inc(loaded[u], 16)
                    sp.dma_start(w1[:, u, :], io["ffn1_w1"][bass.ds(s * P, P), :]).then_inc(loaded[u], 16)
                    sp.dma_start(w2[:, u, :, :].rearrange("p j d -> p (j d)"), io["ffn1_w2"][bass.ds(s * P, P), :]).then_inc(loaded[u], 16)
                    sp.dma_start(b1[:, u, :], io["ffn1_b1"][bass.ds(s * P, P), :]).then_inc(loaded[u], 16)
                    sp.dma_start(b2[:, u, :], io["ffn1_b2"][bass.ds(s, 1), :].rearrange("a d -> (a d)").partition_broadcast(P)
                                 ).then_inc(loaded[u], 16)

            steps(sp, E, 1, 2, step)
            for dst, src in ((wq1[:, :, :, :], "wq1"), (wv1[:, :], "wv1"), (outer["bq1"][:, :, :], "bq1"),
                             (outer["wo1"][:, :, :], "wo1"), (outer["rope"][:, :, :, :], "rope")):
                sp.dma_start(dst, io[src]).then_inc(S["next_in"], 16)
            sp.wait_ge(S["next_in"], 80)

        @block.gpsimd
        def _(pool):
            slots = io["slots_out"].rearrange("(n p) d -> p n d", p=P)

            def step(s, u, turn, on):
                for c in range(2):
                    if on(1):
                        pool.wait_ge(S["y_done"], 2 * s - 1 + c)
                        pool.dma_start(slots[:, bass.ds((s - 1) * 2 * TC + c * TC, TC), :], y[:, c, :, :]).then_inc(stored[c], 16)

            steps(pool, E, 1, 2, step)
            pool.wait_ge(S["next_high"], 1)
            pool.tensor_tensor(outer["wq1"][1][:, :, :, :], wq1[:, :, :, :], outer["wq1"][0][:, :, :, :], ALU.subtract)
            pool.tensor_tensor(outer["wv1"][1][:, :], wv1[:, :], outer["wv1"][0][:, :], ALU.subtract).then_inc(S["next_done"], 1)
            pool.wait_ge(S["next_done"], 1)
            for c in range(2):
                pool.wait_ge(stored[c], 16 * E)

        @block.tensor
        def _(pe):
            def turn_x(s, u, turn, c):
                m = 2 * s + c
                if c == 0:
                    pe.wait_ge(loaded[u], 16 * LOADS * (turn + 1))
                wait(pe, S["xt_done"], m)
                for t in range(TC):
                    last = pe.transpose(ps_t[:, P * t:P * t + P], xin[:, u, c, t, :], ident[:, :])
                last.then_inc(S["t_done"], 1)

            def up(s, u, c):
                m = 2 * s + c
                pe.wait_ge(S["xt_done"], m + 1)
                for q in range(2):
                    wait(pe, S["gelu_done"], 2 * m - 1 + q)
                    for j in range(2):
                        last = pe.matmul(ps_h[q][:, j, :], w1[:, u, P * (2 * q + j):P * (2 * q + j) + P], xt[:, c, :],
                                         start=True, stop=True)
                    last.then_inc(S["up_done"], 1)

            def down(s, u, c):
                m = 2 * s + c
                pe.wait_ge(S["gelu_done"], 2 * m + 2)
                wait(pe, S["y_done"], m - 1)
                for t in range(TC):
                    for j in range(FC):
                        last = pe.matmul(ps_o[c][:, t, :], h[:, c, j, P * t:P * t + P], w2[:, u, j, :],
                                         start=(j == 0), stop=(j == FC - 1))
                last.then_inc(S["down_done"], 1)

            def step(s, u, turn, on):
                if on(0):
                    turn_x(s, u, turn, 0)
                if on(1):
                    down(s - 1, 1 - u, 1)
                if on(0):
                    up(s, u, 0)
                    turn_x(s, u, turn, 1)
                    up(s, u, 1)
                    down(s, u, 0)

            steps(pe, E, 1, 2, step)

        @block.scalar
        def _(act):
            def step(s, u, turn, on):
                for c in range(2):
                    if on(0):
                        m = 2 * s + c
                        act.wait_ge(S["t_done"], m + 1)
                        act.activation(xt[:, c, :], ps_t[:, :], ACT.Copy).then_inc(S["xt_done"], 1)
                        if c == 0:
                            act.wait_ge(S["b1_done"], s + 1)
                        wait(act, S["down_done"], m - 1)
                        for q in range(2):
                            act.wait_ge(S["up_done"], 2 * m + q + 1)
                            for j in range(2):
                                last = act.activation(h[:, c, 2 * q + j, :], ps_h[q][:, j, :], ACT.Gelu,
                                                      bias=b1s[:, u, 2 * q + j:2 * q + j + 1], scale=GS)
                            last.then_inc(S["gelu_done"], 1)

            steps(act, E, 1, 2, step)
            act.wait_ge(S["next_in"], 80)
            act.activation(outer["wq1"][0][:, :, :, :], wq1[:, :, :, :], ACT.Copy)
            act.activation(outer["wv1"][0][:, :], wv1[:, :], ACT.Copy).then_inc(S["next_high"], 1)

        @block.vector
        def _(dve):
            def step(s, u, turn, on):
                for c in range(2):
                    if c == 0 and on(0):
                        dve.wait_ge(loaded[u], 16 * LOADS * (turn + 1))
                        wait(dve, S["gelu_done"], 4 * (s - 1))
                        dve.tensor_scalar(b1s[:, u, :], b1[:, u, :], GS, None, ALU.mult).then_inc(S["b1_done"], 1)
                    if on(1):
                        m = 2 * (s - 1) + c
                        dve.wait_ge(S["down_done"], m + 1)
                        wait(dve, stored[c], 16 * (s - 1))
                        dve.scalar_tensor_tensor(out=y[:, c, :, :], in0=ps_o[c][:, :, :], scalar=1.0 / GS,
                                                 in1=window(b2[:, 1 - u, :], [(0, TC), (1, P)]),
                                                 op0=ALU.mult, op1=ALU.add).then_inc(S["y_done"], 1)

            steps(dve, E, 1, 2, step)


def rotary_attention(nc, outer, io):
    with ExitStack() as ctx:
        sb = lambda n, s, d=F32: ctx.enter_context(nc.sbuf_tensor("c_" + n, s, d))
        ps = lambda n, s, d=F32: ctx.enter_context(nc.psum_tensor("c_" + n, s, d))
        x_all = outer["x"]
        s_all, ident, identb, maskb, rows, slot = (outer[k] for k in ("s", "ident", "identb", "maskb", "rows", "slot"))
        G = NQ // NKV
        NH2 = NQ // 2
        wq, bq, wv, wo, rope = (outer[k] for k in ("wq1", "bq1", "wv1", "wo1", "rope"))
        xnt = sb("xnt", [P, 2, SEQ])
        xnt_parts = [sb(f"xnt_{n}", [P, 2, SEQ], F32R) for n in ("high", "low")]
        prod = sb("prod", [P, 2, 4, SEQ])
        rot = sb("rot", [P, G + 1, 2, SEQ])
        qt = sb("qt", [P, NQ, SEQ])
        kt = sb("kt", [P, 2, NKV, SEQ])
        q_stack = sb("q_stack", [P, NQ, P], F32R)
        lower = sb("lower", [P, 1])
        k_parts = [sb(f"k_{n}", [P, NKV, SEQ], F32R) for n in ("high", "low")]
        v = sb("v", [P, 2, 2, NKV, HD + 1])
        nmax = sb("nmax", [P, 2, 4])
        ex = [sb(f"ex{k}", [P, 2, 2, SEQ]) for k in range(2)]
        pt = sb("pt", [P, 2, 2, 2, SEQ])
        rden = sb("rden", [P, 2, G])
        o = sb("o", [P, 2, NQ, HD])
        ot = sb("ot", [P, 2, NH2, P])
        y = sb("y", [P, 2, 2, P])
        th = sb("th", [P, 2 * P])
        z = sb("z", [P, 2 * P])
        x2 = sb("x2", [P, 2, 2 * P])
        idx = sb("idx", [P, 2, 2], U32)
        ps_s = [ps(f"ps_s{k}", [P, 2, 512]) for k in range(2)]
        ps_t = ps("ps_t", [P, 2, 512])
        ps_o = ps("ps_o", [P, 512])
        ps_p = ps("ps_p", [P, 512])
        names = """one lower_set x_high x_low q_high q_low rel p_done rope_done rot_done v_done s_done max_done exp_done t_done ta_done td_done
            pv_done rd_done o_done ot_ps ota_done otd_done wo_ps wo_done idx_done th_done z1_done z_done x2_done""".split()
        S = {n: ctx.enter_context(nc.semaphore("c_" + n)) for n in names}
        x_in, y_in, gathered, stored = ([ctx.enter_context(nc.semaphore(f"c_{n}{u}")) for u in range(2)]
                                  for n in ("x_in", "y_in", "gathered", "stored"))
        flat = lambda t: t[:, :, :].rearrange("p n d -> p (n d)")
        U = 2 * NKV
        RELS = 32
        LEAD, DEPTH, TAIL = 4, 4, 2
        block = ctx.enter_context(nc.Block())

        @block.sync
        def _(sp):
            def load_x(s, u):
                wait(sp, S["x_low"], s - 1)
                sp.dma_start(xnt[:, u, :], io["xnt1"][:, bass.ds(s * SEQ, SEQ)]).then_inc(x_in[u], 16)

            load_x(0, 0)

            def step(s, u, turn, on):
                if on(-1):
                    load_x(s + 1, 1 - u)
                if on(2):
                    b = s - 2
                    wait(sp, S["z1_done"], b - 1)
                    sp.dma_start(y[:, u, :, :], io["xn1"].rearrange("(n p) d -> p n d", p=P)[:, bass.ds(2 * b, 2), :]
                                 ).then_inc(y_in[u], 16)
                if on(4):
                    b = s - 4
                    sp.wait_ge(S["x2_done"], b + 1)
                    sp.dma_start(io["out"].rearrange("(n p) d -> p n d", p=P)[:, bass.ds(2 * b, 2), :],
                                 x2[:, u, :].rearrange("p (t d) -> p t d", t=2)).then_inc(stored[u], 16)
                if on(0):
                    for kind, (first, last) in enumerate(((0, 1), (1, G + 1))):
                        sp.wait_ge(S["rot_done"], (G + 1) * s + last)
                        dst = qt[:, :, :] if kind else kt[:, u, :, :]
                        for i in range(4):
                            for x in range(2):
                                for half in range(2):
                                    sp.dma_start(dst[64 * half + 32 * x:64 * half + 32 * x + 32, i:(NQ if kind else NKV):4, :],
                                                 rot[32 * i:32 * i + 32, first:last, x, :]).then_inc(S["rel"], 16)

            steps(sp, NB, DEPTH, LEAD, step, TAIL)
            for u in range(2):
                sp.wait_ge(stored[u], 16 * NB // 2)

        @block.gpsimd
        def _(pool):
            pool.memset(v[:, :, :, :, HD:HD + 1], 1.0).then_inc(S["one"], 1)

            def split_x(s, u):
                pool.wait_ge(S["x_high"], s + 1)
                pool.tensor_tensor(xnt_parts[1][:, u, :], xnt[:, u, :], xnt_parts[0][:, u, :], ALU.subtract
                                   ).then_inc(S["x_low"], 1)

            pool.memset(lower[:, :], 1.0).then_inc(S["lower_set"], 1)
            pool.wait_ge(S["lower_set"], 1)
            pool.affine_select(out=lower[:, :], in_=lower[:, :], compare_op=ALU.is_ge, fill=0.0, base=-HD,
                               pattern=[[0, 1]], channel_multiplier=1).then_inc(S["lower_set"], 1)
            def rotate(s, k):
                pool.wait_ge(S["rope_done"], (G + 1) * s + (k + 1))
                if k == 0:
                    wait(pool, S["rel"], 16 * RELS * s)
                r = k % 2
                pool.tensor_tensor(rot[:, k, 0, :], prod[:, r, 0, :], prod[:, r, 1, :], ALU.subtract)
                pool.tensor_tensor(rot[:, k, 1, :], prod[:, r, 2, :], prod[:, r, 3, :], ALU.add).then_inc(S["rot_done"], 1)

            split_x(0, 0)
            rotate(0, 0)

            def step(s, u, turn, on):
                if on(2):
                    wait(pool, gathered[u], 32 * (turn - 1))
                    pool.tensor_copy(idx[:, u, :], slot[:, bass.ds(2 * (s - 2), 2)]).then_inc(S["idx_done"], 1)
                for k in range(G):
                    if on(1):
                        r, heads = 1 - u, slice(G * k, G * k + G)
                        pool.wait_ge(S["q_high"], NKV * (s - 1) + (k + 1))
                        pool.tensor_tensor(k_parts[1][:, k, :], kt[:, r, k, :], k_parts[0][:, k, :], ALU.subtract)
                        pool.tensor_tensor(q_stack[:, heads, :], qt[:, heads, P:SEQ], q_stack[:, heads, :], ALU.subtract
                                           ).then_inc(S["q_low"], 1)
                    if on(0):
                        rotate(s, k + 1)
                if on(-1):
                    split_x(s + 1, 1 - u)
                if on(2):
                    pool.wait_ge(S["idx_done"], s - 1)
                    pool.wait_ge(y_in[u], 16 * turn)
                if on(3):
                    b = s - 3
                    wait(pool, stored[1 - u], 16 * (turn + u - 2))
                    pool.wait_ge(S["z_done"], b + 1)
                    pool.tensor_tensor(x2[:, 1 - u, :], z[:, :], flat(x_all)[:, bass.ds(2 * P * b, 2 * P)], ALU.add
                                       ).then_inc(S["x2_done"], 1)
                if on(-1):
                    rotate(s + 1, 0)
                if on(2):
                    for t in range(2):
                        pool.indirect_dma_start(
                            out=y[:, u, t, :], out_offset=None, in_=io["slots_out"],
                            in_offset=bass.IndirectOffsetOnAxis(ap=idx[:, u, t:t + 1], axis=0),
                            bounds_check=E * CAP - 1, oob_is_err=False).then_inc(gathered[u], 16)

            steps(pool, NB, DEPTH, LEAD, step, TAIL)

        @block.tensor
        def _(pe):
            def mask_scores(b, k):
                n, t = b * U + k, k // NKV
                if k == 0:
                    pe.wait_ge(S["rel"], 16 * RELS * (b + 1))
                wait(pe, S["exp_done"], n - 1)
                sc = ps_s[k % 2]
                for half in range(2):
                    pe.matmul(window(sc[:, half, :], [(2 * P, 2), (1, P)], t * P), identb[:, :],
                              window(maskb[:, :], [(0, 2), (1, P)]), start=True, stop=False, skip_group_check=True)

            def scores(b, u, k, w):
                t, g = k // NKV, k % NKV
                cols = P * (t + 1)
                if t == 1 and w == 0:
                    pe.wait_ge(S["q_low"], NKV * b + (g + 1))
                for half in range(2):
                    out, head = ps_s[k % 2][:, half, 2 * P * w:2 * P * w + cols], G * g + 2 * w + half
                    if t == 0:
                        last = pe.matmul(out, qt[64 * half:64 * half + 64, head, 0:P], kt[64 * half:64 * half + 64, u, g, 0:P],
                                         start=False, stop=True, skip_group_check=True)
                    else:
                        pe.matmul(out, q_stack[:, head, :], k_parts[0][:, g, :], start=False, stop=False, skip_group_check=True)
                        last = pe.matmul(out, q_stack[:, head, :], k_parts[1][:, g, :], start=False, stop=True,
                                         skip_group_check=True)
                if w == 1:
                    last.then_inc(S["s_done"], 1)

            def project(s, u, k):
                if k == 0:
                    pe.wait_ge(S["x_low"], s + 1)
                    wait(pe, S["v_done"], s)
                    wait(pe, S["wo_done"], 2 * (s - 3) + 1)
                else:
                    pe.wait_ge(S["rope_done"], (G + 1) * s + k)
                    if k == 1:
                        wait(pe, S["wo_done"], 2 * (s - 2))
                if k <= G:
                    for x in range(2):
                        last = product_of_parts(pe, ps_p[:, SEQ * x:SEQ * x + SEQ], [w[:, k, x, :] for w in wq],
                                                [part[:, u, :] for part in xnt_parts])
                else:
                    for t in range(2):
                        last = product_of_parts(pe, ps_p[:, SEQ * t:SEQ * t + SEQ], [part[:, u, P * t:P * t + P] for part in xnt_parts],
                                                [w[:, :] for w in wv])
                last.then_inc(S["p_done"], 1)

            def turn_probs(b, k):
                n, t = b * U + k, k // NKV
                pe.wait_ge(S["exp_done"], n + 1)
                wait(pe, S["ta_done"], n)
                wait(pe, S["td_done"], n)
                outs = 2 * b - 1 if k <= 1 else 2 * b if k <= 5 else 2 * b + 1
                wait(pe, S["ota_done"], outs)
                wait(pe, S["otd_done"], outs)
                for w in range(2):
                    for half in range(2):
                        for blk in range(t + 1):
                            at = P * (half * (t + 1) + blk)
                            last = pe.transpose(ps_t[:, w, at:at + P], ex[k % 2][:, half, w, P * blk:P * blk + P], ident[:, :])
                last.then_inc(S["t_done"], 1)

            def weigh(b, r, k):
                n, t, g = b * U + k, k // NKV, k % NKV
                pe.wait_ge(S["ta_done"], n + 1)
                pe.wait_ge(S["td_done"], n + 1)
                pe.wait_ge(S["v_done"], b + 1)
                wait(pe, S["o_done"], n)
                for w in range(2):
                    for half in range(2):
                        h = 2 * w + half
                        for blk in range(t + 1):
                            at = P * (half * (t + 1) + blk)
                            last = pe.matmul(ps_o[:, (HD + 1) * h:(HD + 1) * (h + 1)], pt[:, k % 2, w, at // SEQ, at % SEQ:at % SEQ + P],
                                             v[:, r, blk, g, :], start=(blk == 0), stop=(blk == t))
                last.then_inc(S["pv_done"], 1)

            project(0, 0, 0)

            def step(s, u, turn, on):
                for k in range(U):
                    if on(1):
                        mask_scores(s - 1, k)
                        scores(s - 1, 1 - u, k, 0)
                    if on(2) and k in (0, 4):
                        b, t = s - 2, k // 4
                        pe.wait_ge(S["o_done"], b * U + (4 * t + 4))
                        n = (b + 1) * U + k - 2
                        last_unit = n if on(1) else min(n, NB * U)
                        pe.wait_ge(S["ta_done"], last_unit)
                        pe.wait_ge(S["td_done"], last_unit)
                        for j in range(NH2):
                            last = pe.transpose(ps_t[:, j // 4, P * (j % 4):P * (j % 4) + P], o[:, t, 2 * j:2 * j + 2, :]
                                                .rearrange("p a d -> p (a d)"), ident[:, :])
                        last.then_inc(S["ot_ps"], 1)
                    if on(1):
                        scores(s - 1, 1 - u, k, 1)
                    if on(0) and k <= G:
                        project(s, u, k + 1)
                    if on(-1) and k == U - 1:
                        project(s + 1, 1 - u, 0)
                    if (on(1) if k >= 2 else on(2)):
                        turn_probs(s - 1 if k >= 2 else s - 2, (k - 2) % U)
                    if (on(1) if k >= 3 else on(2)):
                        weigh(s - 1 if k >= 3 else s - 2, (1 - u) if k >= 3 else u, (k - 3) % U)
                    if on(2) and k >= 6:
                        b, t = s - 2, k - 6
                        pe.wait_ge(S["ota_done"], 2 * b + (t + 1))
                        pe.wait_ge(S["otd_done"], 2 * b + (t + 1))
                        if k == 6:
                            pe.wait_ge(S["v_done"], s + 1 if on(0) else NB)
                            wait(pe, S["wo_done"], 2 * b)
                        else:
                            pe.wait_ge(S["wo_done"], 2 * b + 1)
                            if on(-1):
                                pe.wait_ge(S["rope_done"], (G + 1) * (s + 1) + 1)
                        for j in range(NH2):
                            last = pe.matmul(ps_p[:, 0:P], ot[:, t, j, :], wo[:, j, :], start=(j == 0), stop=(j == NH2 - 1))
                        last.then_inc(S["wo_ps"], 1)

            steps(pe, NB, DEPTH, LEAD, step, TAIL)

        @block.scalar
        def _(act):
            def split_x(s, u, turn):
                act.wait_ge(x_in[u], 16 * (turn + 1))
                wait(act, S["p_done"], 6 * (s - 1))
                act.activation(xnt_parts[0][:, u, :], xnt[:, u, :], ACT.Copy).then_inc(S["x_high"], 1)

            act.wait_ge(S["lower_set"], 2)
            split_x(0, 0, 0)

            def step(s, u, turn, on):
                for k in range(U):
                    if on(2) and k in (0, 4):
                        b, t = s - 2, k // 4
                        act.wait_ge(S["ot_ps"], 2 * b + (t + 1))
                        wait(act, S["wo_ps"], 2 * (b - 1) + (t + 1))
                        act.activation(ot[:, t, 0:4, :].rearrange("p j n -> p (j n)"), ps_t[:, 0, :], ACT.Copy).then_inc(S["ota_done"], 1)
                    if (on(1) if k >= 2 else on(2)):
                        b, kk = (s - 1 if k >= 2 else s - 2), (k - 2) % U
                        n, t = b * U + kk, kk // NKV
                        act.wait_ge(S["t_done"], n + 1)
                        wait(act, S["pv_done"], n - 1)
                        act.activation(pt[:, kk % 2, 0, 0:t + 1, :], ps_t[:, 0, 0:SEQ * (t + 1)].rearrange("p (a n) -> p a n", n=SEQ),
                                       ACT.Copy).then_inc(S["ta_done"], 1)
                    if on(1) and k < NKV:
                        r, heads = 1 - u, slice(G * k, G * k + G)
                        if k == 0:
                            act.wait_ge(S["rel"], 16 * RELS * s)
                            wait(act, S["s_done"], U * (s - 1))
                        act.activation(q_stack[:, heads, :], qt[:, heads, P:SEQ], ACT.Copy, scale=lower[:, :])
                        act.activation(k_parts[0][:, k, :], kt[:, r, k, :], ACT.Copy).then_inc(S["q_high"], 1)
                    if on(1):
                        b = s - 1
                        n, t = b * U + k, k // NKV
                        cols = P * (t + 1)
                        act.wait_ge(S["max_done"], n + 1)
                        wait(act, S["t_done"], n - 1)
                        for half in range(2):
                            for w in range(2):
                                last = act.activation(ex[k % 2][:, half, w, 0:cols], ps_s[k % 2][:, half, 2 * P * w:2 * P * w + cols],
                                                      ACT.Exp, bias=nmax[:, k % 2, 2 * half + w:2 * half + w + 1])
                        last.then_inc(S["exp_done"], 1)
                    if on(-1) and k == 5:
                        split_x(s + 1, 1 - u, turn + u)
                    if on(3) and k == 5:
                        b, r = s - 3, 1 - u
                        act.wait_ge(gathered[r], 32 * (turn + u - 1))
                        act.activation(th[:, :], y[:, r, :, :].rearrange("p t n -> p (t n)"), ACT.Tanh, scale=0.5
                                       ).then_inc(S["th_done"], 1)

            steps(act, NB, DEPTH, LEAD, step, TAIL)

        @block.vector
        def _(dve):
            dve.wait_ge(S["one"], 1)

            def rope_products(s, k):
                dve.wait_ge(S["p_done"], 6 * s + (k + 1))
                wait(dve, S["rot_done"], (G + 1) * s + max(k - 1, 0))
                tab, r = int(k == 0), k % 2
                for j, (x, f) in enumerate(((0, 0), (1, 1), (1, 0), (0, 1))):
                    last = dve.scalar_tensor_tensor(out=prod[:, r, j, :], in0=ps_p[:, SEQ * x:SEQ * x + SEQ],
                                                    scalar=bq[:, k, x:x + 1], in1=rope[:, tab, f, :],
                                                    op0=ALU.add, op1=ALU.mult)
                last.then_inc(S["rope_done"], 1)

            rope_products(0, 0)

            def step(s, u, turn, on):
                for k in range(U):
                    if on(2) and k in (0, 4):
                        b, t = s - 2, k // 4
                        dve.wait_ge(S["ot_ps"], 2 * b + (t + 1))
                        wait(dve, S["wo_ps"], 2 * (b - 1) + (t + 1))
                        dve.tensor_copy(ot[:, t, 4:8, :].rearrange("p j n -> p (j n)"), ps_t[:, 1, :]).then_inc(S["otd_done"], 1)
                    if on(1):
                        b = s - 1
                        n, t = b * U + k, k // NKV
                        dve.wait_ge(S["s_done"], n + 1)
                        wait(dve, S["exp_done"], n - 1)
                        dve.tensor_reduce(nmax[:, k % 2, :].rearrange("p (h w) -> p h w", h=2),
                                          ps_s[k % 2][:, :, :].rearrange("p h (w n) -> p h w n", w=2)[:, :, :, 0:P * (t + 1)],
                                          AX_X, ALU.max, negate=True).then_inc(S["max_done"], 1)
                    if on(0) and k < G:
                        rope_products(s, k + 1)
                    if on(-1) and k == U - 1:
                        rope_products(s + 1, 0)
                    if on(0) and k == G:
                        dve.wait_ge(S["p_done"], 6 * (s + 1))
                        wait(dve, S["pv_done"], U * (s - 1))
                        for t in range(2):
                            last = dve.tensor_tensor(v[:, u, t, :, 0:HD],
                                                     ps_p[:, SEQ * t:SEQ * t + SEQ].rearrange("p (g d) -> p g d", g=NKV),
                                                     rows[:, R_BV1:R_BV1 + SEQ].rearrange("p (g d) -> p g d", g=NKV), ALU.add)
                        last.then_inc(S["v_done"], 1)
                    if (on(1) if k >= 2 else on(2)):
                        b, kk = (s - 1 if k >= 2 else s - 2), (k - 2) % U
                        n, t = b * U + kk, kk // NKV
                        dve.wait_ge(S["t_done"], n + 1)
                        wait(dve, S["pv_done"], n - 1)
                        dve.tensor_copy(pt[:, kk % 2, 1, 0:t + 1, :], ps_t[:, 1, 0:SEQ * (t + 1)].rearrange("p (a n) -> p a n", n=SEQ)
                                        ).then_inc(S["td_done"], 1)
                    if (on(1) if k >= 3 else on(2)):
                        b, kk = (s - 1 if k >= 3 else s - 2), (k - 3) % U
                        n, t, g = b * U + kk, kk // NKV, kk % NKV
                        heads = ps_o[:, 0:G * (HD + 1)].rearrange("p (h d) -> p h d", h=G)
                        dve.wait_ge(S["pv_done"], n + 1)
                        dve.reciprocal(rden[:, kk % 2, :], heads[:, :, HD]).then_inc(S["rd_done"], 1)
                        dve.wait_ge(S["rd_done"], n + 1)
                        if g == 0:
                            wait(dve, S["ot_ps"], 2 * (b - 1) + (t + 1))
                        dve.tensor_tensor(o[:, t, G * g:G * g + G, :], heads[:, :, 0:HD],
                                          window(rden[:, kk % 2, :], [(1, G), (0, HD)]), ALU.mult).then_inc(S["o_done"], 1)
                    if on(3) and k == 6:
                        b, r = s - 3, 1 - u
                        dve.wait_ge(S["th_done"], b + 1)
                        wait(dve, S["x2_done"], b)
                        dve.scalar_tensor_tensor(out=z[:, :], in0=th[:, :], scalar=1.0,
                                                 in1=y[:, r, :, :].rearrange("p t n -> p (t n)"), op0=ALU.add, op1=ALU.mult
                                                 ).then_inc(S["z1_done"], 1)
                        dve.wait_ge(S["z1_done"], b + 1)
                        dve.scalar_tensor_tensor(out=z[:, :], in0=z[:, :], scalar=0.5, in1=flat(s_all)[:, bass.ds(2 * P * b, 2 * P)],
                                                 op0=ALU.mult, op1=ALU.mult).then_inc(S["z_done"], 1)
                    if on(2) and k >= 6:
                        b, t = s - 2, k - 6
                        dve.wait_ge(S["wo_ps"], 2 * b + (t + 1))
                        dve.tensor_tensor(s_all[:, bass.ds(2 * b + t, 1), :].rearrange("p a d -> p (a d)"), ps_p[:, 0:P],
                                          rows[:, R_BO1:R_BO1 + P], ALU.add).then_inc(S["wo_done"], 1)

            steps(dve, NB, DEPTH, LEAD, step, TAIL)
            dve.wait_ge(S["wo_done"], 2 * NB)


def program(nc, io):
    with ExitStack() as ctx:
        sb = lambda n, s, d=F32: ctx.enter_context(nc.sbuf_tensor(n, s, d))
        outer = {
            "x": sb("x_all", [P, NT, D]), "s": sb("s_all", [P, NT, D]),
            "ident": sb("ident", [P, P]), "identb": sb("identb", [P, P], BF16),
            "mask": sb("mask", [P, P]), "maskb": sb("maskb", [P, P], BF16), "rows": sb("rows", [P, R_COLS]),
            "ones": sb("ones", [P, P]), "upto": sb("upto", [P, P]), "slot": sb("slot", [P, NT], U32),
        }
        with ExitStack() as c2:
            s_id = c2.enter_context(nc.semaphore("s_id"))
            s_z = c2.enter_context(nc.semaphore("s_z"))
            s_rows = c2.enter_context(nc.semaphore("s_rows"))
            block = c2.enter_context(nc.Block())

            @block.sync
            def _(sp):
                sp.dma_start(outer["rows"][:, :], io["rows"].partition_broadcast(P)).then_inc(s_rows, 16)
                sp.wait_ge(s_rows, 16)

            @block.gpsimd
            def _(pool):
                pool.memset(outer["ident"][:, :], 0.0).then_inc(s_z, 1)
                pool.memset(outer["mask"][:, :], 0.0).then_inc(s_z, 1)
                pool.memset(outer["upto"][:, :], 1.0).then_inc(s_z, 1)
                pool.wait_ge(s_z, 3)
                pool.affine_select(out=outer["ident"][:, :], in_=outer["ident"][:, :], compare_op=ALU.not_equal, fill=1.0,
                                   base=0, pattern=[[-1, P]], channel_multiplier=1).then_inc(s_id, 1)
                pool.affine_select(out=outer["mask"][:, :], in_=outer["mask"][:, :], compare_op=ALU.is_ge, fill=MASKED,
                                   base=0, pattern=[[-1, P]], channel_multiplier=1).then_inc(s_id, 1)

                pool.affine_select(out=outer["upto"][:, :], in_=outer["upto"][:, :], compare_op=ALU.is_ge, fill=0.0,
                                   base=0, pattern=[[1, P]], channel_multiplier=-1).then_inc(s_id, 1)
                pool.wait_ge(s_id, 3)

            @block.vector
            def _(dve):
                dve.memset(outer["ones"][:, :], 1.0)
                dve.wait_ge(s_id, 3)
                dve.tensor_copy(outer["identb"][:, :], outer["ident"][:, :])
                dve.tensor_copy(outer["maskb"][:, :], outer["mask"][:, :]).then_inc(s_z, 1)
                dve.wait_ge(s_z, 4)
        with ExitStack() as first:
            sb1 = lambda n, s, d=F32: first.enter_context(nc.sbuf_tensor(n, s, d))
            layer = dict(outer, xnt=sb1("xnt_all", [P, NT * P]), logits0=sb1("logits0", [P, NT, E]),
                         ffn0_w1=[sb1(f"ffn0_w1_{n}", [P, E + 1, H0], F32R) for n in ("high", "low")])
            local_and_topk_attention(nc, layer, io)
            mixture_of_all_experts(nc, layer, io)
        with ExitStack() as second:
            sb2 = lambda n, s, d=F32: second.enter_context(nc.sbuf_tensor(n, s, d))
            layer = dict(outer, wq1=[sb2(f"wq1_{n}", [P, NQ // 4 + 1, 2, P], F32R) for n in ("high", "low")],
                         wv1=[sb2(f"wv1_{n}", [P, NKV * HD], F32R) for n in ("high", "low")],
                         bq1=sb2("bq1", [P, NQ // 4 + 1, 2]), wo1=sb2("wo1", [P, NQ // 2, P]),
                         rope=sb2("rope_tables", [P, 2, 2, SEQ]))
            mixture_by_slots(nc, layer, io)
            rotary_attention(nc, layer, io)




def rope_tables():
    import numpy as np

    inv = (1.0 / np.float32(10000.0) ** (np.arange(0, HD, 2, dtype=np.float32) / np.float32(HD))).astype(np.float32)
    ang = (np.arange(SEQ, dtype=np.float32)[None, :] * inv[:, None]).astype(np.float32).astype(np.float64)
    one = np.stack([np.cos(ang), np.sin(ang)], axis=1)
    return np.tile(np.stack([one / HD ** 0.5, one], axis=1), (4, 1, 1, 1)).astype(np.float32)


def kernel(**inputs):
    import numpy as _np
    import concourse.bacc as _bacc
    from concourse import mybir as _mybir
    from concourse.bass_utils import run_bass_kernel_spmd as _run

    x = {k: _np.asarray(v) for k, v in inputs.items()}
    col = lambda v: v.reshape(-1, 1)
    halves = lambda w: w.reshape(len(w), -1, 4, 2, HD // 2).transpose(0, 1, 3, 2, 4).reshape(len(w), -1, 2, P)
    arrays = {
        "x": x["L0_attn_mu"].reshape(NB * SEQ, D),
        "w0": _np.concatenate([x["L0_attn_Wq"], x["L0_attn_Wk"], x["L0_attn_Wm1"][:D], x["L0_attn_Wm1"][D:],
                               x["L0_attn_Wv"], x["L0_attn_Wm2"], x["L0_attn_Wo"][:D], x["L0_attn_Wo"][D:],
                               x["L0_ffn_router_w"], col(x["L0_attn_bq"]), col(x["L0_attn_bk"]), col(x["L0_attn_bm1"]),
                               col(x["L0_attn_bv"]), col(x["L0_attn_bm2"])], axis=1),
        "rows": _np.concatenate([x["L0_attn_bo"], x["L0_ffn_router_b"], x["L1_ffn_b_sw"], x["L1_attn_bo"],
                                 x["L1_attn_bv"], _np.arange(E, 0, -1, dtype=_np.float32),
                                 CAP * _np.arange(E, dtype=_np.float32) - 1, CAP * _np.arange(1, E + 1, dtype=_np.float32) - 1]),
        "ffn0_w1": _np.concatenate([x["L0_ffn_sw1"][None], x["L0_ffn_rw1"]]).transpose(1, 0, 2),
        "ffn0_b1": _np.concatenate([x["L0_ffn_sb1"][None], x["L0_ffn_rb1"]]).reshape(-1, P).T,
        "ffn0_w2": _np.concatenate([x["L0_ffn_sw2"][None], x["L0_ffn_rw2"]]).reshape(E + 1, H0 // P, P, D).transpose(2, 0, 1, 3),
        "ffn0_b2": _np.concatenate([x["L0_ffn_rb2"], x["L0_ffn_sb2"][None]]),
        "wsw": x["L1_ffn_W_sw"],
        "wq1": _np.concatenate([halves(x["L1_attn_Wk"]), halves(x["L1_attn_Wq"])], axis=1),
        "bq1": _np.concatenate([halves(x["L1_attn_bk"][None])[0], halves(x["L1_attn_bq"][None])[0]]).transpose(2, 0, 1),
        "wv1": x["L1_attn_Wv"],
        "wo1": x["L1_attn_Wo"].reshape(NQ // 2, P, D).transpose(1, 0, 2),
        "rope": rope_tables(),
        "ffn1_w1": x["L1_ffn_W1"].reshape(E * P, FF),
        "ffn1_w2": x["L1_ffn_W2"].reshape(E, FF // P, P, D).transpose(0, 2, 1, 3).reshape(E * P, FF // P * D),
        "ffn1_b1": x["L1_ffn_b1"].reshape(E, FF // P, P).transpose(0, 2, 1).reshape(E * P, FF // P),
        "ffn1_b2": x["L1_ffn_b2"],
    }
    arrays = {f"{k}_dram": _np.ascontiguousarray(v) for k, v in arrays.items()}
    nc = _bacc.Bacc("TRN2", target_bir_lowering=False, num_devices=1)
    io = {k[:-5]: nc.dram_tensor(k, a.shape, _mybir.dt.from_np(a.dtype), kind="ExternalInput").ap()
          for k, a in arrays.items()}
    io["out"] = nc.dram_tensor("out_dram", (NB * SEQ, D), F32, kind="ExternalOutput").ap()
    io["xn1"] = nc.dram_tensor("xn1_scratch", (NB * SEQ, D), F32, kind="Internal").ap()
    io["xnt1"] = nc.dram_tensor("xnt1_scratch", (P, NB * SEQ), F32, kind="Internal").ap()
    io["slots_in"] = nc.dram_tensor("slots_in_scratch", (E * CAP, D), F32, kind="Internal").ap()
    io["slots_out"] = nc.dram_tensor("slots_out_scratch", (E * CAP, D), F32, kind="Internal").ap()
    program(nc, io)
    r = _run(nc, [arrays], core_ids=[0])
    return r.results[0]["out_dram"].reshape(NB, SEQ, D)
```

```python
from contextlib import ExitStack

import concourse.bass as bass
from concourse import mybir

F32 = mybir.dt.float32
F32R = mybir.dt.float32r
BF16 = mybir.dt.bfloat16
U32 = mybir.dt.uint32
ALU = mybir.AluOpType
ACT = mybir.ActivationFunctionType
AX_X = mybir.AxisListType.X

P = 128
D = 128
SEQ = 256
NB = 32
NT = NB * SEQ // P
WIN = 4
TOPK = 8
E = 8
H0 = 256
NQ, NKV, HD = 16, 4, 64
FF = 512
CAP = NB * SEQ // E
EPS = 1e-5
MASKED = -1e30
TAKEN = -3e38
FAR = 1e6
GS = 2.0 ** 0.5 / 1.41421

W0 = {n: slice(P * k, P * k + P) for k, n in enumerate(["q", "k", "m1a", "m1b", "v", "m2", "oa", "ob"])}
W0_ROUTER = slice(8 * P, 8 * P + E)
W0_BIAS = {n: slice(8 * P + E + k, 8 * P + E + k + 1) for k, n in enumerate(["q", "k", "m1", "v", "m2"])}
W0_COLS = 8 * P + E + 5
R_BO0, R_RB0, R_RB1, R_BO1, R_BV1 = 0, 128, 136, 144, 272
R_PREF, R_SLOT, R_LAST = 528, 536, 544
R_COLS = 552


def wait(eng, sem, value):
    if not (isinstance(value, int) and value <= 0):
        eng.wait_ge(sem, value)


def steps(eng, rounds, depth, lead, step, tail=0):
    for s in range(lead):
        step(s, s % 2, s // 2, lambda k: 0 <= s - k)
    with eng.Fori(0, (rounds - lead - tail) // 2) as i:
        for u in range(2):
            step(2 * i + (lead + u), u, i + lead // 2, lambda k: True)
    for s in range(rounds - tail, rounds + depth):
        step(s, s % 2, s // 2, lambda k: s - k < rounds)


def window(ap, pattern, offset=0):
    return bass.AP(ap.tensor, ap.offset + offset, [list(ap.ap[0])] + [list(x) for x in pattern])


def product_of_parts(pe, out, lhs, rhs, start=True, stop=True):
    pe.matmul(out, lhs[0], rhs[0], start=start, stop=False)
    pe.matmul(out, lhs[1], rhs[0], start=False, stop=False)
    return pe.matmul(out, lhs[0], rhs[1], start=False, stop=stop)


def norm_statistics(dve, stats, mean, var, tmp, chain, done):
    even, odd = stats[:, :, 1], stats[:, :, 4]
    dve.tensor_tensor(mean, even, odd, ALU.add)
    dve.tensor_tensor(tmp, even, odd, ALU.subtract)
    dve.tensor_tensor(var, stats[:, :, 2], stats[:, :, 5], ALU.add).then_inc(chain, 1)
    dve.wait_ge(chain, done + 1)
    dve.tensor_scalar(mean, mean, 0.5, None, ALU.mult)
    dve.tensor_tensor(tmp, tmp, tmp, ALU.mult)
    dve.tensor_scalar(var, var, 1.0 / D, None, ALU.mult).then_inc(chain, 1)
    dve.wait_ge(chain, done + 2)
    dve.tensor_scalar(tmp, tmp, 0.25, None, ALU.mult).then_inc(chain, 1)
    dve.wait_ge(chain, done + 3)
    dve.tensor_tensor(var, var, tmp, ALU.add).then_inc(chain, 1)
    dve.wait_ge(chain, done + 4)


def local_and_topk_attention(nc, outer, io):
    with ExitStack() as ctx:
        sb = lambda n, s, d=F32: ctx.enter_context(nc.sbuf_tensor("a_" + n, s, d))
        ps = lambda n, s, d=F32: ctx.enter_context(nc.psum_tensor("a_" + n, s, d))
        sem = lambda n: ctx.enter_context(nc.semaphore("a_" + n))
        x_all, s_all, xnt_all, logits0 = outer["x"], outer["s"], outer["xnt"], outer["logits0"]
        ident, identb, maskb, rows = outer["ident"], outer["identb"], outer["maskb"], outer["rows"]

        w = sb("w", [P, W0_COLS])
        wt = sb("wt", [P, 2, P])
        wvo = sb("wvo", [P, P + E])
        wm2o = sb("wm2o", [P, P])
        bcols = sb("bcols", [P, 2, P])
        vbias = sb("vbias", [P, P])
        stats = sb("stats", [P, NT, 6])
        mean, var, std, rstd = (sb(n, [P, NT]) for n in ("mean", "var", "std", "rstd"))
        xn = sb("xn", [P, 2, SEQ])
        xnt = sb("xnt", [P, 2, SEQ])
        qk = sb("qk", [P, 2, 2, SEQ])
        amsg = sb("amsg", [P, 2, SEQ])
        bmsg = sb("bmsg", [P, 2, WIN + SEQ])
        pre = sb("pre", [P, 2, WIN * SEQ])
        th = sb("th", [P, 2, WIN * SEQ])
        act4 = sb("act4", [P, WIN * SEQ])
        pairs = sb("pairs", [P, 2 * SEQ])
        msum = sb("msum", [P, 2, SEQ])
        top = sb("top", [P, 2, 2, 8])
        nmax = sb("nmax", [P, 2, 2])
        rest = sb("rest", [P, 2, 384])
        ex = sb("ex", [P, 2, 384])
        ex8 = sb("ex8", [P, 2, 8])
        den = sb("den", [P, 2, 2])
        rden = sb("rden", [P, 2, 2])
        prob = sb("prob", [P, 2, 384])
        probt = sb("probt", [P, 2, 384])
        gn = sb("gn", [P, 2, SEQ])
        w1, w1_parts = sb("w1", [P, E + 1, H0]), outer["ffn0_w1"]

        ps_t = ps("ps_t", [P, 512])
        ps_qk = ps("ps_qk", [P, 512])
        ps_ab = ps("ps_ab", [P, 512])
        ps_v = ps("ps_v", [P, 512])
        ps_s = [ps(f"ps_s{k}", [P, 512]) for k in range(2)]
        ps_pt = ps("ps_pt", [P, 512])
        ps_gl = ps("ps_gl", [P, 512])

        names = """w1_in w1_high w1_low w_in wt_ps wt_sb bc fold_ps vb_ps ready zero
            st var_done std_done rs_done chain xn_done t_done xnt_done copied qk_ps qk_done ab_ps ab_done v_ps v_done
            s_done max_done nm_done ex_done rden_done prob_done pt_ps pt_done pre_done th_done
            act4_done pairs_done sum_done l_done g_done gn_done s0_done""".split()
        S = {n: sem(n) for n in names}
        XC = 16
        x_in = [sem(f"x_in{c}") for c in range(NT // XC)]
        LEAD, DEPTH = 6, 5
        SC = float(D) ** -0.5
        vw = ps_v[:, 0:2 * (P + E)].rearrange("p (t n) -> p t n", t=2)
        block = ctx.enter_context(nc.Block())

        @block.sync
        def _(sp):
            sp.dma_start(w[:, :], io["w0"]).then_inc(S["w_in"], 16)
            xv = io["x"].rearrange("(n p) d -> p n d", p=P)
            for c, sem_x in enumerate(x_in):
                n = slice(c * XC, c * XC + XC)
                sp.dma_start(x_all[:, n, :], xv[:, n, :]).then_inc(sem_x, 16)
            sp.dma_start(w1[:, :, :], io["ffn0_w1"]).then_inc(S["w1_in"], 16)
            for sem_x in x_in:
                sp.wait_ge(sem_x, 16)

        @block.gpsimd
        def _(pool):
            pool.memset(bmsg[:, :, 0:WIN], 0.0).then_inc(S["zero"], 1)
            pool.wait_ge(S["w1_high"], 1)
            pool.tensor_tensor(w1_parts[1][:, :, :], w1[:, :, :], w1_parts[0][:, :, :], ALU.subtract).then_inc(S["w1_low"], 1)
            pool.wait_ge(S["zero"], 1)

            def step(s, u, turn, on):
                if on(4):
                    b = s - 4
                    pool.wait_ge(S["act4_done"], b + 1)
                    wait(pool, S["sum_done"], b)
                    pool.tensor_tensor(pairs[:, :], act4[:, 0:2 * SEQ], act4[:, 2 * SEQ:4 * SEQ], ALU.add).then_inc(S["pairs_done"], 1)
                if on(2):
                    b, r = s - 2, u
                    pool.wait_ge(S["ab_done"], b + 1)
                    wait(pool, S["act4_done"], b - 1)
                    pool.tensor_tensor(
                        pre[:, r, :].rearrange("p (w n) -> p w n", w=WIN),
                        window(amsg[:, r, :], [(0, WIN), (1, SEQ)]),
                        window(bmsg[:, r, :], [(1, WIN), (1, SEQ)]), ALU.add).then_inc(S["pre_done"], 1)
                if on(1):
                    b, r = s - 1, 1 - u
                    pool.wait_ge(S["xnt_done"], b + 1)
                    pool.tensor_copy(xnt_all[:, bass.ds(b * SEQ, SEQ)], xnt[:, r, :]).then_inc(S["copied"], 1)

            steps(pool, NB, DEPTH, LEAD, step)

        @block.tensor
        def _(pe):
            pe.wait_ge(S["w_in"], 16)
            pe.transpose(ps_t[:, 0:P], w[:, W0["v"]], ident[:, :])
            pe.transpose(ps_t[:, P:2 * P], w[:, W0["m2"]], ident[:, :]).then_inc(S["wt_ps"], 1)
            pe.wait_ge(S["wt_sb"], 1)
            pe.matmul(ps_qk[:, 0:P], wt[:, 0, :], w[:, W0["ob"]], start=True, stop=True)
            pe.matmul(ps_qk[:, P:2 * P], wt[:, 1, :], w[:, W0["oa"]], start=True, stop=True).then_inc(S["fold_ps"], 1)
            pe.wait_ge(S["bc"], 2)
            pe.matmul(ps_ab[:, 0:P], bcols[:, 0, :], w[:, W0["ob"]], start=True, stop=False)
            pe.matmul(ps_ab[:, 0:P], bcols[:, 1, :], w[:, W0["oa"]], start=False, stop=True).then_inc(S["vb_ps"], 1)
            pe.wait_ge(S["ready"], 4)

            def step(s, u, turn, on):
                if on(2):
                    b, r = s - 2, u
                    pe.wait_ge(S["qk_done"], b + 1)
                    wait(pe, S["ex_done"], b - 1)
                    sc = ps_s[r]
                    pe.matmul(sc[:, 0:P], identb[:, :], maskb[:, :], start=True, stop=False, skip_group_check=True)
                    pe.matmul(sc[:, 2 * P:3 * P], identb[:, :], maskb[:, :], start=False, stop=False, skip_group_check=True)
                    pe.matmul(sc[:, 0:P], qk[:, r, 0, 0:P], qk[:, r, 1, 0:P], start=False, stop=False, skip_group_check=True)
                    pe.matmul(sc[:, P:3 * P], qk[:, r, 0, P:SEQ], qk[:, r, 1, :], start=False, stop=True,
                              skip_group_check=True).then_inc(S["s_done"], 1)
                if on(1):
                    b, r = s - 1, 1 - u
                    pe.wait_ge(S["xnt_done"], b + 1)
                    wait(pe, S["qk_done"], b)
                    for j, n in enumerate(("q", "k")):
                        last = pe.matmul(ps_qk[:, SEQ * j:SEQ * j + SEQ], w[:, W0[n]], xnt[:, r, :], start=True, stop=True)
                    last.then_inc(S["qk_ps"], 1)
                    wait(pe, S["ab_done"], b)
                    for j, n in enumerate(("m1a", "m1b")):
                        last = pe.matmul(ps_ab[:, SEQ * j:SEQ * j + SEQ], w[:, W0[n]], xnt[:, r, :], start=True, stop=True)
                    last.then_inc(S["ab_ps"], 1)
                    wait(pe, S["v_done"], b)
                    for t in range(2):
                        last = pe.matmul(vw[:, t, :], xnt[:, r, P * t:P * t + P], wvo[:, :], start=True, stop=True)
                    last.then_inc(S["v_ps"], 1)
                if on(3):
                    b, r = s - 3, 1 - u
                    pe.wait_ge(S["prob_done"], b + 1)
                    wait(pe, S["pt_done"], b)
                    for k in range(3):
                        last = pe.transpose(ps_pt[:, P * k:P * k + P], prob[:, r, P * k:P * k + P], ident[:, :])
                    last.then_inc(S["pt_ps"], 1)
                if on(4):
                    b, r = s - 4, u
                    pe.wait_ge(S["sum_done"], b + 1)
                    wait(pe, S["s0_done"], b)
                    for t in range(2):
                        last = pe.matmul(ps_gl[:, SEQ + P * t:SEQ + P * t + P], msum[:, r, P * t:P * t + P], wm2o[:, :],
                                         start=True, stop=True)
                    last.then_inc(S["l_done"], 1)
                    pe.wait_ge(S["pt_done"], b + 1)
                    pe.wait_ge(S["v_done"], b + 1)
                    v = [s_all[:, bass.ds(2 * b + t, 1), :] for t in range(2)]
                    pe.matmul(ps_gl[:, 0:P], probt[:, r, 0:P], v[0], start=True, stop=True)
                    pe.matmul(ps_gl[:, P:SEQ], probt[:, r, P:2 * P], v[0], start=True, stop=False)
                    pe.matmul(ps_gl[:, P:SEQ], probt[:, r, 2 * P:3 * P], v[1], start=False,
                              stop=True).then_inc(S["g_done"], 1)
                if on(0):
                    b, r = s, u
                    pe.wait_ge(S["xn_done"], b + 1)
                    wait(pe, S["xnt_done"], b)
                    for t in range(2):
                        last = pe.transpose(ps_t[:, P * t:P * t + P], xn[:, r, P * t:P * t + P], ident[:, :])
                    last.then_inc(S["t_done"], 1)

            steps(pe, NB, DEPTH, LEAD, step)

        @block.scalar
        def _(act):
            act.wait_ge(S["w1_in"], 16)
            act.activation(w1_parts[0][:, :, :], w1[:, :, :], ACT.Copy).then_inc(S["w1_high"], 1)
            act.wait_ge(S["var_done"], 1)
            act.activation(std[:, :], var[:, :], ACT.Sqrt).then_inc(S["std_done"], 1)
            act.wait_ge(S["wt_ps"], 1)
            act.activation(wt[:, :, :], ps_t[:, 0:2 * P].rearrange("p (a n) -> p a n", a=2), ACT.Copy).then_inc(S["wt_sb"], 1)
            act.wait_ge(S["w_in"], 16)
            act.activation(wvo[:, P:P + E], w[:, W0_ROUTER], ACT.Copy).then_inc(S["ready"], 1)
            act.wait_ge(S["fold_ps"], 1)
            act.activation(wvo[:, 0:P], ps_qk[:, 0:P], ACT.Copy).then_inc(S["ready"], 1)
            act.activation(wm2o[:, :], ps_qk[:, P:2 * P], ACT.Copy, scale=0.5 / WIN).then_inc(S["ready"], 1)

            def step(s, u, turn, on):
                if on(1):
                    b, r = s - 1, 1 - u
                    act.wait_ge(S["qk_ps"], b + 1)
                    wait(act, S["s_done"], b - 1)
                    for j, n in enumerate(("q", "k")):
                        last = act.activation(qk[:, r, j, :], ps_qk[:, SEQ * j:SEQ * j + SEQ], ACT.Identity,
                                              bias=w[:, W0_BIAS[n]])
                    last.then_inc(S["qk_done"], 1)
                    act.wait_ge(S["ab_ps"], b + 1)
                    wait(act, S["pre_done"], b - 1)
                    act.activation(amsg[:, r, :], ps_ab[:, 0:SEQ], ACT.Identity, bias=w[:, W0_BIAS["m1"]])
                    act.activation(bmsg[:, r, WIN:WIN + SEQ], ps_ab[:, SEQ:2 * SEQ], ACT.Copy).then_inc(S["ab_done"], 1)
                if on(2):
                    b, r = s - 2, u
                    act.wait_ge(S["nm_done"], b + 1)
                    wait(act, S["prob_done"], b - 1)
                    wait(act, S["rden_done"], b - 1)
                    for t, c in enumerate((slice(0, P), slice(P, 3 * P))):
                        act.activation(ex8[:, t, :], top[:, r, t, :], ACT.Exp, bias=nmax[:, r, t:t + 1], scale=SC,
                                       accum_out=den[:, r, t:t + 1])
                        last = act.activation(ex[:, r, c], ps_s[r][:, c], ACT.Exp, bias=nmax[:, r, t:t + 1], scale=SC)
                    last.then_inc(S["ex_done"], 1)
                if on(3):
                    b, r = s - 3, 1 - u
                    act.wait_ge(S["pt_ps"], b + 1)
                    wait(act, S["g_done"], b - 1)
                    act.activation(probt[:, r, :], ps_pt[:, 0:384], ACT.Copy).then_inc(S["pt_done"], 1)
                if on(0):
                    b, r = s, u
                    act.wait_ge(S["t_done"], b + 1)
                    wait(act, S["v_ps"], b - 1)
                    wait(act, S["copied"], b - 1)
                    act.activation(xnt[:, r, :], ps_t[:, 0:SEQ], ACT.Copy).then_inc(S["xnt_done"], 1)
                if on(4):
                    b, r = s - 4, u
                    act.wait_ge(S["g_done"], b + 1)
                    act.wait_ge(S["rden_done"], b + 1)
                    wait(act, S["s0_done"], b - 1)
                    for t in range(2):
                        last = act.activation(gn[:, r, P * t:P * t + P], ps_gl[:, P * t:P * t + P], ACT.Copy,
                                              scale=rden[:, r, t:t + 1])
                    last.then_inc(S["gn_done"], 1)
                if on(2):
                    b, r = s - 2, u
                    act.wait_ge(S["pre_done"], b + 1)
                    wait(act, S["act4_done"], b - 1)
                    act.activation(th[:, r, :], pre[:, r, :], ACT.Tanh, scale=0.5).then_inc(S["th_done"], 1)

            steps(act, NB, DEPTH, LEAD, step)

        @block.vector
        def _(dve):
            for c, sem_x in enumerate(x_in):
                dve.wait_ge(sem_x, 16)
                for n in range(c * XC, c * XC + XC):
                    last = dve.bn_stats(stats[:, n, :], x_all[:, n, :])
            last.then_inc(S["st"], 1)
            dve.wait_ge(S["st"], 1)
            norm_statistics(dve, stats[:, :, :], mean[:, :], var[:, :], rstd[:, :], S["chain"], 0)
            dve.tensor_scalar(var[:, :], var[:, :], EPS, None, ALU.add).then_inc(S["var_done"], 1)
            dve.wait_ge(S["std_done"], 1)
            dve.reciprocal(rstd[:, :], std[:, :]).then_inc(S["rs_done"], 1)
            dve.wait_ge(S["rs_done"], 1)
            dve.wait_ge(S["w_in"], 16)
            for j, n in enumerate(("v", "m2")):
                dve.tensor_scalar(bcols[:, j, :], outer["ones"][:, 0:P], w[:, W0_BIAS[n]], None, ALU.mult).then_inc(S["bc"], 1)
            dve.wait_ge(S["vb_ps"], 1)
            dve.tensor_tensor(vbias[:, :], ps_ab[:, 0:P], rows[:, R_BO0:R_BO0 + P], ALU.add).then_inc(S["ready"], 1)
            dve.wait_ge(S["ready"], 4)

            def step(s, u, turn, on):
                if on(4):
                    b, r = s - 4, u
                    wait(dve, S["gn_done"], b - 1)
                    dve.reciprocal(rden[:, r, :], den[:, r, :]).then_inc(S["rden_done"], 1)
                if on(3):
                    b, r = s - 3, 1 - u
                    dve.wait_ge(S["ex_done"], b + 1)
                    wait(dve, S["pt_ps"], b - 1)
                    dve.scalar_tensor_tensor(out=prob[:, r, :], in0=rest[:, r, :], scalar=TAKEN, in1=ex[:, r, :],
                                             op0=ALU.is_equal, op1=ALU.mult).then_inc(S["prob_done"], 1)
                if on(5):
                    b, r = s - 5, 1 - u
                    if on(2):
                        wait(dve, S["ex_done"], s - 3)
                        dve.wait_ge(S["s_done"], s - 1)
                    dve.wait_ge(S["gn_done"], b + 1)
                    dve.tensor_tensor(s_all[:, bass.ds(b * 2, 2), :], ps_gl[:, SEQ:2 * SEQ].rearrange("p (t n) -> p t n", t=2),
                                      gn[:, r, :].rearrange("p (t n) -> p t n", t=2), ALU.add).then_inc(S["s0_done"], 1)
                if on(2):
                    b, r = s - 2, u
                    if not on(5):
                        wait(dve, S["ex_done"], s - 3)
                        dve.wait_ge(S["s_done"], s - 1)
                    for t, c in enumerate((slice(0, P), slice(P, 3 * P))):
                        last = dve.max(top[:, r, t, :], ps_s[r][:, c])
                    last.then_inc(S["max_done"], 1)
                    dve.wait_ge(S["max_done"], b + 1)
                    dve.tensor_scalar(nmax[:, r, :], top[:, r, :, 0], -SC, None, ALU.mult)
                    for t, c in enumerate((slice(0, P), slice(P, 3 * P))):
                        last = dve.match_replace(rest[:, r, c], top[:, r, t, :], ps_s[r][:, c], TAKEN)
                    last.then_inc(S["nm_done"], 1)
                if on(4):
                    b, r = s - 4, u
                    dve.wait_ge(S["pairs_done"], b + 1)
                    wait(dve, S["l_done"], b - 1)
                    dve.tensor_tensor(msum[:, r, :], pairs[:, 0:SEQ], pairs[:, SEQ:2 * SEQ], ALU.add).then_inc(S["sum_done"], 1)
                if on(0):
                    b, r = s, u
                    wait(dve, S["t_done"], b - 1)
                    for t in range(2):
                        last = dve.tensor_scalar(xn[:, r, P * t:P * t + P], x_all[:, 2 * b + t, :],
                                                 mean[:, bass.ds(2 * b + t, 1)], rstd[:, bass.ds(2 * b + t, 1)],
                                                 ALU.subtract, ALU.mult)
                    last.then_inc(S["xn_done"], 1)
                if on(3):
                    b, r = s - 3, 1 - u
                    dve.wait_ge(S["th_done"], b + 1)
                    wait(dve, S["pairs_done"], b)
                    dve.scalar_tensor_tensor(out=act4[:, :], in0=th[:, r, :], scalar=1.0, in1=pre[:, r, :],
                                             op0=ALU.add, op1=ALU.mult).then_inc(S["act4_done"], 1)
                if on(1):
                    b = s - 1
                    dve.wait_ge(S["v_ps"], b + 1)
                    dve.tensor_tensor(s_all[:, bass.ds(b * 2, 2), :], vw[:, :, 0:P], window(vbias[:, :], [(0, 2), (1, P)]), ALU.add)
                    dve.tensor_tensor(logits0[:, bass.ds(b * 2, 2), :], vw[:, :, P:P + E],
                                      window(rows[:, R_RB0:R_RB0 + E], [(0, 2), (1, E)]), ALU.add).then_inc(S["v_done"], 1)

            steps(dve, NB, DEPTH, LEAD, step)
            dve.wait_ge(S["s0_done"], NB)


def softmax_of_experts(dve, link, logits, ex_wait, work, row):
    dve_max = row
    link(dve.tensor_reduce(dve_max, logits, AX_X, ALU.max))
    link(dve.tensor_tensor(work, logits, over_experts(dve_max), ALU.subtract))
    ex_wait()
    link(dve.tensor_reduce(row, work, AX_X, ALU.add))
    link(dve.reciprocal(row, row))
    link(dve.tensor_tensor(work, work, over_experts(row), ALU.mult))


def over_experts(ap):
    return bass.AP(ap.tensor, ap.offset, [list(x) for x in ap.ap] + [[0, E]])


def over_tiles(ap):
    return bass.AP(ap.tensor, ap.offset, [list(ap.ap[0]), [0, NT], [1, E]])


def first_of_the_largest(link, dve, values, out, pref, row):
    link(dve.tensor_reduce(row, values, AX_X, ALU.max))
    link(dve.tensor_tensor(out, values, over_experts(row), ALU.is_equal))
    link(dve.tensor_tensor(out, out, pref, ALU.mult))
    link(dve.tensor_reduce(row, out, AX_X, ALU.max))
    return dve.tensor_tensor(out, out, over_experts(row), ALU.is_equal)


def mixture_of_all_experts(nc, outer, io):
    with ExitStack() as ctx:
        sb = lambda n, s, d=F32: ctx.enter_context(nc.sbuf_tensor("b_" + n, s, d))
        ps = lambda n, s, d=F32: ctx.enter_context(nc.psum_tensor("b_" + n, s, d))
        x_all, s_all, xnt_all, logits0, slot = (outer[k] for k in ("x", "s", "xnt", "logits0", "slot"))
        ident, rows = outer["ident"], outer["rows"]
        NX = E + 1
        HC = H0 // P
        TC = 4
        CT = TC * P
        NC = NT // TC
        w1_parts = outer["ffn0_w1"]
        xnt_parts = [sb(f"xnt_{n}", [P, 2, CT], F32R) for n in ("high", "low")]
        w2 = sb("w2", [P, NX, HC, P])
        b1 = sb("b1", [P, NX * HC])
        b2 = sb("b2", [NX, P])
        wsw = sb("wsw", [P, E])
        probs = sb("probs", [P, NT, E])
        one1 = sb("one1", [P, NT, E])
        one2 = sb("one2", [P, NT, E])
        row = sb("row", [P, NT])
        wx = sb("wx", [P, NT, NX])
        wxs = sb("wxs", [P, 2, TC * NX])
        wt = sb("wt", [NX, 2, CT])
        h = sb("h", [P, 2, HC, CT])
        acc = sb("acc", [P, 2, TC, P])
        th = sb("th", [P, CT])
        z = sb("z", [P, CT])
        x1 = sb("x1", [P, TC, P])
        stats = sb("stats", [P, TC, 6])
        mean, var, std, rstd = (sb(n, [P, TC]) for n in ("mean", "var", "std", "rstd"))
        xs = sb("xs", [P, 2, TC, P])
        logits1 = sb("logits1", [P, TC, E])
        best = sb("best", [P, TC])
        chosen = sb("chosen", [P, TC, E])
        taken = sb("taken", [P, E])
        place = sb("place", [P, TC, E])
        full = sb("full", [P, TC, E])
        idx = sb("idx", [P, 2, TC], U32)
        xst = sb("xst", [P, CT])
        ps_h = [ps(f"ps_h{k}", [P, HC, CT]) for k in range(2)]
        ps_o = [ps(f"ps_o{k}", [P, TC, P]) for k in range(2)]
        ps_m = ps("ps_m", [P, 512])
        ps_t = ps("ps_t", [P, CT])
        counts = ps_m[:, P:P + (TC + 1) * E]
        zeros = sb("zeros", [P, 1024])
        names = """xnt_high xnt_low zeros_set slots_cleared w2_in b_in shifted exped chain ready one wxs_done wt_ps wt_done up_done gelu_done down_done acc_done
            th_done x1_done var_done std_done xs_done kept t_done xst_done r_done logits_done chosen_done count_done place_chain idx_done xst_out""".split()
        S = {n: ctx.enter_context(nc.semaphore("b_" + n)) for n in names}
        xs_out, scattered = ([ctx.enter_context(nc.semaphore(f"b_{n}{u}")) for u in range(2)] for n in ("xs_out", "scattered"))
        LEAD, DEPTH = 4, 2
        CLEARS = E * CAP * D // (P * 1024)
        LINKS, PLACE_LINKS = 12, 6
        block = ctx.enter_context(nc.Block())

        @block.sync
        def _(sp):
            sp.dma_start(b1[:, :], io["ffn0_b1"]).then_inc(S["b_in"], 16)
            sp.dma_start(b2[:, :], io["ffn0_b2"]).then_inc(S["b_in"], 16)
            sp.dma_start(wsw[:, :], io["wsw"]).then_inc(S["b_in"], 16)
            sp.dma_start(w2[:, :, :, :], io["ffn0_w2"]).then_inc(S["w2_in"], 16)
            sp.wait_ge(S["zeros_set"], 1)
            for c in range(CLEARS):
                sp.dma_start(io["slots_in"].rearrange("(c p r) d -> c p (r d)", c=CLEARS, p=P)[c], zeros[:, :]
                             ).then_inc(S["slots_cleared"], 16)

            def step(s, u, turn, on):
                if on(1):
                    c = s - 1
                    sp.wait_ge(S["xs_done"], c + 1)
                    sp.dma_start(io["xn1"].rearrange("(n p) d -> p n d", p=P)[:, bass.ds(c * TC, TC), :],
                                 xs[:, 1 - u, :, :]).then_inc(xs_out[1 - u], 16)
                    sp.wait_ge(S["xst_done"], c + 1)
                    sp.dma_start(io["xnt1"][:, bass.ds(c * CT, CT)], xst[:, :]).then_inc(S["xst_out"], 16)

            steps(sp, NC, DEPTH, LEAD, step)
            sp.wait_ge(S["slots_cleared"], 16 * CLEARS)
            for u in range(2):
                sp.wait_ge(xs_out[u], 16 * NC // 2)
            sp.wait_ge(S["xst_out"], 16 * NC)

        @block.gpsimd
        def _(pool):
            pool.memset(zeros[:, :], 0.0).then_inc(S["zeros_set"], 1)
            pool.memset(wx[:, :, E:NX], 1.0).then_inc(S["one"], 1)
            pool.wait_ge(S["zeros_set"], 1)
            CLEARED = 2
            FIRST = 0

            def split_low(s, u, cols):
                pool.tensor_tensor(xnt_parts[1][:, u, :], xnt_all[:, cols], xnt_parts[0][:, u, :],
                                   ALU.subtract).then_inc(S["xnt_low"], 1)

            def step(s, u, turn, on):
                if on(0):
                    wait(pool, S["up_done"], (s - 1) * NX)
                    cols = bass.ds(s * CT, CT)
                    pool.tensor_copy(xnt_parts[0][:, u, :], xnt_all[:, cols]).then_inc(S["xnt_high"], 1)
                    pool.wait_ge(S["xnt_high"], s + 1)
                    if s is FIRST:
                        split_low(s, u, cols)
                        pool.wait_ge(S["ready"], 1)
                        pool.wait_ge(S["one"], 1)
                    wait(pool, S["wt_ps"], s - 1)
                    pool.tensor_copy(wxs[:, u, :].rearrange("p (t e) -> p t e", t=TC),
                                     wx[:, bass.ds(s * TC, TC), :]).then_inc(S["wxs_done"], 1)
                    if s is not FIRST:
                        split_low(s, u, cols)
                if on(2):
                    pool.wait_ge(S["idx_done"], s - 1)
                    if s is CLEARED:
                        pool.wait_ge(S["slots_cleared"], 16 * CLEARS)
                if on(1):
                    pool.wait_ge(S["x1_done"], s)
                    pool.tensor_copy(x_all[:, bass.ds((s - 1) * TC, TC), :], x1[:, :, :]).then_inc(S["kept"], 1)
                if on(2):
                    for t in range(TC):
                        pool.indirect_dma_start(
                            out=io["slots_in"], out_offset=bass.IndirectOffsetOnAxis(ap=idx[:, u, t:t + 1], axis=0),
                            in_=xs[:, u, t, :], in_offset=None, bounds_check=E * CAP - 1,
                            oob_is_err=False).then_inc(scattered[u], 16)

            steps(pool, NC, DEPTH, LEAD, step)
            pool.wait_ge(S["kept"], NC)
            for u in range(2):
                pool.wait_ge(scattered[u], 16 * TC * NC // 2)

        @block.tensor
        def _(pe):
            pe.wait_ge(S["b_in"], 48)
            pe.wait_ge(S["w2_in"], 16)

            def up(s, u, e):
                g = s * NX + e
                if e == 0:
                    pe.wait_ge(S["xnt_low"], s + 1)
                wait(pe, S["gelu_done"], g - 1)
                for j in range(HC):
                    last = product_of_parts(pe, ps_h[(u + e) % 2][:, j, :], [w[:, e, P * j:P * j + P] for w in w1_parts],
                                            [x[:, u, :] for x in xnt_parts])
                last.then_inc(S["up_done"], 1)

            def down(s, u, e):
                g = s * NX + e
                pe.wait_ge(S["gelu_done"], g + 1)
                wait(pe, S["acc_done"], g - 1)
                if e == 0:
                    pe.wait_ge(S["wt_done"], s + 1)
                for t in range(TC):
                    for j in range(HC):
                        last = pe.matmul(ps_o[(u + e) % 2][:, t, :], h[:, (u + e) % 2, j, P * t:P * t + P], w2[:, e, j, :],
                                         start=(j == 0), stop=(j == HC - 1 and e > 0))
                    if e == 0:
                        last = pe.matmul(ps_o[u][:, t, :], wt[:, u, P * t:P * t + P], b2[:, :], start=False, stop=True)
                last.then_inc(S["down_done"], 1)

            def step(s, u, turn, on):
                for e in range(NX):
                    if on(0):
                        up(s, u, e)
                    if e == 0 and on(0):
                        pe.wait_ge(S["wxs_done"], s + 1)
                        wait(pe, S["logits_done"], s - 1)
                        wait(pe, S["place_chain"], (s - 2) * PLACE_LINKS)
                        wait(pe, S["wt_done"], s)
                        for t in range(TC):
                            last = pe.transpose(ps_m[0:NX, P * t:P * t + P], wxs[:, u, NX * t:NX * t + NX], ident[:, :])
                        last.then_inc(S["wt_ps"], 1)
                    if e == 7 and on(1):
                        pe.wait_ge(S["xs_done"], s)
                        wait(pe, S["xst_done"], s - 1)
                        for t in range(TC):
                            last = pe.transpose(ps_t[:, P * t:P * t + P], xs[:, 1 - u, t, :], ident[:, :])
                        last.then_inc(S["t_done"], 1)
                    if e == 0 and on(1):
                        down(s - 1, 1 - u, NX - 1)
                    if e > 0 and on(0):
                        down(s, u, e - 1)
                    if e == 3 and on(2):
                        pe.wait_ge(S["chosen_done"], s - 1)
                        pe.wait_ge(S["wt_done"], s + 1 if on(0) else NC)
                        pe.matmul(counts[:, 0:TC * E], outer["upto"][:, :], chosen[:, :, :].rearrange("p t e -> p (t e)"),
                                  start=True, stop=False, skip_group_check=True)
                        for t in range(TC):
                            last = pe.matmul(counts[:, E * (t + 1):E * (TC + 1)], outer["ones"][:, :],
                                             window(chosen[:, t, :], [(0, TC - t), (1, E)]), start=False, stop=(t == TC - 1),
                                             skip_group_check=True)
                        last.then_inc(S["count_done"], 1)
                    if e == 8 and on(1):
                        pe.wait_ge(S["xst_done"], s)
                        pe.wait_ge(S["wt_done"], s + 1 if on(0) else NC)
                        for t in range(TC):
                            last = pe.matmul(ps_m[:, E * t:E * t + E], xst[:, P * t:P * t + P], wsw[:, :], start=True, stop=True)
                        last.then_inc(S["r_done"], 1)

            steps(pe, NC, DEPTH, LEAD, step)

        @block.scalar
        def _(act):
            act.wait_ge(S["shifted"], 1)
            act.activation(probs[:, :, :], probs[:, :, :], ACT.Exp).then_inc(S["exped"], 1)

            def step(s, u, turn, on):
                for e in range(NX):
                    if on(0):
                        g = s * NX + e
                        act.wait_ge(S["up_done"], g + 1)
                        wait(act, S["down_done"], g - 1)
                        for j in range(HC):
                            last = act.activation(h[:, (u + e) % 2, j, :], ps_h[(u + e) % 2][:, j, :], ACT.Gelu,
                                                  bias=b1[:, HC * e + j:HC * e + j + 1])
                        last.then_inc(S["gelu_done"], 1)
                    if e == 1 and on(1):
                        act.wait_ge(S["acc_done"], s * NX)
                        act.activation(th[:, :], acc[:, 1 - u, :, :].rearrange("p t n -> p (t n)"), ACT.Tanh,
                                       scale=0.5).then_inc(S["th_done"], 1)
                    if e == 4 and on(1):
                        act.wait_ge(S["var_done"], s)
                        act.activation(std[:, :], var[:, :], ACT.Sqrt).then_inc(S["std_done"], 1)
                    if e == 7 and on(1):
                        act.wait_ge(S["t_done"], s)
                        wait(act, S["xst_out"], (s - 1) * 16)
                        act.activation(xst[:, :], ps_t[:, :], ACT.Copy).then_inc(S["xst_done"], 1)

            steps(act, NC, DEPTH, LEAD, step)

        @block.vector
        def _(dve):
            count = [0]

            def link(ins):
                count[0] += 1
                ins.then_inc(S["chain"], 1)
                dve.wait_ge(S["chain"], count[0])

            def take_exp():
                dve.sem_inc(S["shifted"], 1)
                dve.wait_ge(S["exped"], 1)

            softmax_of_experts(dve, link, logits0[:, :, :], take_exp, probs[:, :, :], row[:, :])
            pref = over_tiles(rows[:, R_PREF:R_PREF + E])
            link(first_of_the_largest(link, dve, probs[:, :, :], one1[:, :, :], pref, row[:, :]))
            flat = lambda t: t[:, :, :].rearrange("p n e -> p (n e)")
            link(dve.scalar_tensor_tensor(out=flat(one2), in0=flat(one1), scalar=-2.0, in1=flat(probs),
                                          op0=ALU.mult, op1=ALU.add))
            link(dve.tensor_copy(wx[:, :, 0:E], one2[:, :, :]))
            link(first_of_the_largest(link, dve, wx[:, :, 0:E], one2[:, :, :], pref, row[:, :]))
            link(dve.tensor_tensor(one1[:, :, :], one1[:, :, :], one2[:, :, :], ALU.add))
            dve.tensor_tensor(wx[:, :, 0:E], one1[:, :, :], probs[:, :, :], ALU.mult).then_inc(S["ready"], 1)
            dve.wait_ge(S["ready"], 1)
            link(dve.tensor_copy(taken[:, :], rows[:, R_SLOT:R_SLOT + E]))
            base = count[0]

            def step(s, u, turn, on):
                def linked(j, ins):
                    ins.then_inc(S["chain"], 1)
                    dve.wait_ge(S["chain"], (s - 1) * LINKS + (base + j + 1))

                for e in range(NX):
                    if e == 0 and on(0):
                        dve.wait_ge(S["wt_ps"], s + 1)
                        dve.tensor_copy(wt[:, u, :], ps_m[0:NX, :]).then_inc(S["wt_done"], 1)
                    c, v = (s - 1, 1 - u) if e == 0 else (s, u)
                    done = e - 1 if e else NX - 1
                    if on(1) if e == 0 else on(0):
                        g = c * NX + done
                        dve.wait_ge(S["down_done"], g + 1)
                        if done == 0:
                            dve.tensor_copy(acc[:, v, :, :], ps_o[v][:, :, :]).then_inc(S["acc_done"], 1)
                        else:
                            dve.wait_ge(S["acc_done"], g)
                            for t in range(TC):
                                last = dve.scalar_tensor_tensor(
                                    out=acc[:, v, t, :], in0=ps_o[(v + done) % 2][:, t, :],
                                    scalar=wx[:, bass.ds(c * TC + t, 1), done - 1:done],
                                    in1=acc[:, v, t, :], op0=ALU.mult, op1=ALU.add)
                            last.then_inc(S["acc_done"], 1)
                    if e == 2 and on(1):
                        b, r = s - 1, 1 - u
                        dve.wait_ge(S["th_done"], b + 1)
                        linked(0, dve.scalar_tensor_tensor(out=z[:, :], in0=th[:, :], scalar=1.0,
                                                           in1=acc[:, r, :, :].rearrange("p t n -> p (t n)"),
                                                           op0=ALU.add, op1=ALU.mult))
                        linked(1, dve.scalar_tensor_tensor(
                            out=z[:, :], in0=z[:, :], scalar=0.5, op0=ALU.mult, op1=ALU.mult,
                            in1=s_all[:, :, :].rearrange("p n d -> p (n d)")[:, bass.ds(b * CT, CT)]))
                        wait(dve, S["kept"], b)
                        dve.tensor_tensor(x1[:, :, :], z[:, :].rearrange("p (t n) -> p t n", t=TC),
                                          x_all[:, bass.ds(b * TC, TC), :], ALU.add).then_inc(S["x1_done"], 1)
                        dve.wait_ge(S["x1_done"], b + 1)
                    if e == 3 and on(1):
                        for t in range(TC):
                            last = dve.bn_stats(stats[:, t, :], x1[:, t, :])
                        linked(2, last)
                        norm_statistics(dve, stats[:, :, :], mean[:, :], var[:, :], rstd[:, :], S["chain"],
                                        (s - 1) * LINKS + (base + 3))
                        dve.tensor_scalar(var[:, :], var[:, :], EPS, None, ALU.add).then_inc(S["var_done"], 1)
                    if e == 5 and on(1):
                        b = s - 1
                        dve.wait_ge(S["std_done"], b + 1)
                        linked(7, dve.reciprocal(rstd[:, :], std[:, :]))
                        wait(dve, xs_out[1 - u], 16 * (turn + u - 1))
                        wait(dve, scattered[1 - u], 16 * TC * (turn + u - 1))
                        for t in range(TC):
                            last = dve.tensor_scalar(xs[:, 1 - u, t, :], x1[:, t, :], mean[:, t:t + 1], rstd[:, t:t + 1],
                                                     ALU.subtract, ALU.mult)
                        last.then_inc(S["xs_done"], 1)
                    if e == 8 and on(1):
                        b = s - 1
                        dve.wait_ge(S["r_done"], b + 1)
                        dve.tensor_tensor(logits1[:, :, :], ps_m[:, 0:TC * E].rearrange("p (t e) -> p t e", t=TC),
                                          window(rows[:, R_RB1:R_RB1 + E], [(0, TC), (1, E)]), ALU.add).then_inc(S["logits_done"], 1)
                        dve.wait_ge(S["logits_done"], b + 1)
                        links = iter(range(8, LINKS))
                        first_of_the_largest(lambda ins: linked(next(links), ins), dve, logits1[:, :, :], chosen[:, :, :],
                                             window(rows[:, R_PREF:R_PREF + E], [(0, TC), (1, E)]), best[:, :]
                                             ).then_inc(S["chosen_done"], 1)
                        dve.wait_ge(S["chosen_done"], b + 1)
                    if e == 4 and on(2):
                        b = s - 2

                        def placed(j, ins):
                            ins.then_inc(S["place_chain"], 1)
                            dve.wait_ge(S["place_chain"], (s - 2) * PLACE_LINKS + (j + 1))

                        dve.wait_ge(S["count_done"], b + 1)
                        placed(0, dve.tensor_tensor(place[:, :, :], counts[:, 0:TC * E].rearrange("p (t e) -> p t e", t=TC),
                                                    window(taken[:, :], [(0, TC), (1, E)]), ALU.add))
                        placed(1, dve.tensor_tensor(taken[:, :], taken[:, :], counts[:, TC * E:(TC + 1) * E], ALU.add))
                        placed(2, dve.tensor_tensor(full[:, :, :], place[:, :, :],
                                                    window(rows[:, R_LAST:R_LAST + E], [(0, TC), (1, E)]), ALU.is_gt))
                        placed(3, dve.scalar_tensor_tensor(out=place[:, :, :], in0=full[:, :, :], scalar=FAR, in1=place[:, :, :],
                                                           op0=ALU.mult, op1=ALU.add))
                        placed(4, dve.tensor_tensor(place[:, :, :], place[:, :, :], chosen[:, :, :], ALU.mult))
                        placed(5, dve.tensor_reduce(best[:, :], place[:, :, :], AX_X, ALU.add))
                        wait(dve, scattered[u], 16 * TC * (turn - 1))
                        dve.tensor_copy(idx[:, u, :], best[:, :])
                        dve.tensor_copy(slot[:, bass.ds(b * TC, TC)], best[:, :]).then_inc(S["idx_done"], 1)

            steps(dve, NC, DEPTH, LEAD, step)
            dve.wait_ge(S["idx_done"], NC)


def project_heads(pe, out, att, u, k):
    x, wq, wv = att["xnt1"], att["wq1"], att["wv1"]
    for j in range(2):
        cols = slice(SEQ * j, SEQ * j + SEQ)
        if k <= NQ // NKV:
            last = product_of_parts(pe, out[:, cols], [w[:, k, j, :] for w in wq], [part[:, u, :] for part in x])
        else:
            last = product_of_parts(pe, out[:, cols], [part[:, u, P * j:P * j + P] for part in x], [w[:, :] for w in wv])
    return last


def rope_products(dve, ps, att, k):
    for j, (x, f) in enumerate(((0, 0), (1, 1), (1, 0), (0, 1))):
        last = dve.scalar_tensor_tensor(out=att["prod"][:, k % 2, j, :], in0=ps[:, SEQ * x:SEQ * x + SEQ],
                                        scalar=att["bq1"][:, k, x:x + 1], in1=att["rope"][:, int(k == 0), f, :],
                                        op0=ALU.add, op1=ALU.mult)
    return last


def rotate(pool, att, k):
    prod, rot = att["prod"], att["rot"]
    pool.tensor_tensor(rot[:, k, 0, :], prod[:, k % 2, 0, :], prod[:, k % 2, 1, :], ALU.subtract)
    return pool.tensor_tensor(rot[:, k, 1, :], prod[:, k % 2, 2, :], prod[:, k % 2, 3, :], ALU.add)


def add_value_bias(dve, ps, att, rows, u):
    for t in range(2):
        last = dve.tensor_tensor(att["v"][:, u, t, :, 0:HD],
                                 ps[:, SEQ * t:SEQ * t + SEQ].rearrange("p (g d) -> p g d", g=NKV),
                                 rows[:, R_BV1:R_BV1 + SEQ].rearrange("p (g d) -> p g d", g=NKV), ALU.add)
    return last


def regroup(sp, att, u, queries, rel):
    rot = att["rot"]
    dst = att["qt"] if queries else att["kt"][:, u, :, :]
    groups = slice(1, NQ // NKV + 1) if queries else slice(0, 1)
    for i in range(4):
        for x in range(2):
            for half in range(2):
                sp.dma_start(dst[64 * half + 32 * x:64 * half + 32 * x + 32, i:(NQ if queries else NKV):4, :],
                             rot[32 * i:32 * i + 32, groups, x, :]).then_inc(rel, 16)


def mixture_by_slots(nc, outer, io):
    with ExitStack() as ctx:
        sb = lambda n, s, d=F32: ctx.enter_context(nc.sbuf_tensor("d_" + n, s, d))
        ps = lambda n, s, d=F32: ctx.enter_context(nc.psum_tensor("d_" + n, s, d))
        ident, rows, R = outer["ident"], outer["rows"], outer["sems"]
        G = NQ // NKV
        zeros = sb("zeros", [P, FF])
        wq1 = sb("wq1", [P, NQ // NKV + 1, 2, P])
        wv1 = sb("wv1", [P, NKV * HD])
        x1t = sb("x1t", [P, 2, SEQ])
        FC = FF // P
        TC = 4
        CT = TC * P
        w1 = sb("w1", [P, 2, FF])
        w1_parts = [sb(f"w1_{n}", [P, 2, FF], F32R) for n in ("high", "low")]
        w2 = sb("w2", [P, 2, FC, P])
        b1 = sb("b1", [P, 2, FC])
        b1s = sb("b1s", [P, 2, FC])
        b2 = sb("b2", [P, 2, P])
        xin = sb("xin", [P, 2, 2, TC, P])
        xt_parts = [sb(f"xt_{n}", [P, 2, CT], F32R) for n in ("high", "low")]
        h = sb("h", [P, 2, FC, CT])
        y = sb("y", [P, 2, TC, P])
        ps_t = ps("ps_t", [P, CT])
        ps_h = [ps(f"ps_h{k}", [P, 2, CT]) for k in range(2)]
        ps_o = [ps(f"ps_o{k}", [P, TC, P]) for k in range(2)]
        names = "zeros_set w1_high w1_low xt_high next_in next_high next_done b1_done t_done xt_done up_done gelu_done down_done y_done".split()
        S = {n: ctx.enter_context(nc.semaphore("d_" + n)) for n in names}
        loaded = [ctx.enter_context(nc.semaphore(f"d_loaded{u}")) for u in range(2)]
        stored = [ctx.enter_context(nc.semaphore(f"d_stored{u}")) for u in range(2)]
        heads = [window(ps_o[k][:, :, :], [(1, TC * P)]) for k in range(2)]
        FIRST, SECOND, THIRD = 0, 1, 2
        x_in = [ctx.enter_context(nc.semaphore(f"d_x_in{u}")) for u in range(2)]
        X_LOADS, LOADS = 2, 3
        LEAD, DEPTH, TAIL = 2, 1, 2
        block = ctx.enter_context(nc.Block())

        @block.sync
        def _(sp):
            def step(s, u, turn, on):
                if on(0):
                    wait(sp, S["t_done"], 2 * (s - 1))
                    sp.dma_start(xin[:, u, :, :, :], io["slots_in"].rearrange("(n p) d -> p n d", p=P)
                                 [:, bass.ds(s * 2 * TC, 2 * TC), :].rearrange("p (c t) d -> p c t d", c=2)).then_inc(x_in[u], 16)
                    wait(sp, S["w1_low"], s - 1)
                    sp.dma_start(w1[:, u, :], io["ffn1_w1"][bass.ds(s * P, P), :]).then_inc(x_in[u], 16)
                    if s is FIRST:
                        for dst, src in ((x1t[:, :, :], io["xnt1"][:, 0:2 * SEQ].rearrange("p (u n) -> p u n", u=2)), (wq1[:, :, :, :], io["wq1"]), (wv1[:, :], io["wv1"]),
                                         (outer["bq1"][:, :, :], io["bq1"]), (outer["rope"][:, :, :, :], io["rope"]),
                                         (outer["wo1"][:, :, :], io["wo1"])):
                            sp.dma_start(dst, src).then_inc(S["next_in"], 16)
                    wait(sp, S["y_done"], 2 * (s - 1))
                    sp.dma_start(w2[:, u, :, :].rearrange("p j d -> p (j d)"), io["ffn1_w2"][bass.ds(s * P, P), :]).then_inc(loaded[u], 16)
                    sp.dma_start(b1[:, u, :], io["ffn1_b1"][bass.ds(s * P, P), :]).then_inc(loaded[u], 16)
                    sp.dma_start(b2[:, u, :], io["ffn1_b2"][bass.ds(s, 1), :].rearrange("a d -> (a d)").partition_broadcast(P)
                                 ).then_inc(loaded[u], 16)

                if s is SECOND:
                    sp.wait_ge(R["rot_done"], 1)
                    regroup(sp, outer, 0, False, R["rel"])
                if s is THIRD:
                    sp.wait_ge(R["rot_done"], G + 1)
                    regroup(sp, outer, 0, True, R["rel"])

            steps(sp, E, DEPTH, THIRD + 2, step, TAIL)

        @block.gpsimd
        def _(pool):
            pool.memset(zeros[:, :], 0.0).then_inc(S["zeros_set"], 1)
            pool.wait_ge(S["zeros_set"], 1)
            pool.memset(outer["v"][:, :, :, :, HD:HD + 1], 1.0).then_inc(R["one"], 1)
            slots = io["slots_out"].rearrange("(n p) d -> p n d", p=P)

            def step(s, u, turn, on):
                if on(0):
                    pool.wait_ge(x_in[u], 16 * X_LOADS * (turn + 1))
                    wait(pool, S["up_done"], 4 * (s - 1))
                    pool.tensor_tensor(w1_parts[0][:, u, :], w1[:, u, :], zeros[:, :], ALU.add).then_inc(S["w1_high"], 1)
                    pool.wait_ge(S["w1_high"], s + 1)
                    pool.tensor_tensor(w1_parts[1][:, u, :], w1[:, u, :], w1_parts[0][:, u, :], ALU.subtract
                                       ).then_inc(S["w1_low"], 1)
                if s is FIRST:
                    pool.wait_ge(S["next_high"], 1)
                    pool.tensor_tensor(outer["xnt1"][1][:, :, :], x1t[:, :, :], outer["xnt1"][0][:, :, :], ALU.subtract)
                    pool.tensor_tensor(outer["wq1"][1][:, 0, :, :], wq1[:, 0, :, :], outer["wq1"][0][:, 0, :, :], ALU.subtract
                                       ).then_inc(S["next_done"], 1)
                    pool.tensor_tensor(outer["wq1"][1][:, 1:G + 1, :, :], wq1[:, 1:G + 1, :, :], outer["wq1"][0][:, 1:G + 1, :, :],
                                       ALU.subtract)
                    pool.tensor_tensor(outer["wv1"][1][:, :], wv1[:, :], outer["wv1"][0][:, :], ALU.subtract).then_inc(S["next_done"], 1)
                    for k in range(G + 1):
                        pool.wait_ge(R["rope_done"], k + 1)
                        rotate(pool, outer, k).then_inc(R["rot_done"], 1)
                for c in range(2):
                    if on(1):
                        pool.wait_ge(S["y_done"], 2 * s - 1 + c)
                        pool.dma_start(slots[:, bass.ds((s - 1) * 2 * TC + c * TC, TC), :], y[:, c, :, :]).then_inc(stored[c], 16)

            steps(pool, E, DEPTH, LEAD, step, TAIL)
            for c in range(2):
                pool.wait_ge(stored[c], 16 * E)

        @block.tensor
        def _(pe):
            def turn_x(m, u, turn, c):
                if c == 0:
                    pe.wait_ge(x_in[u], 16 * X_LOADS * (turn + 1))
                wait(pe, S["xt_done"], m)
                for t in range(TC):
                    last = pe.transpose(ps_t[:, P * t:P * t + P], xin[:, u, c, t, :], ident[:, :])
                last.then_inc(S["t_done"], 1)

            def up(s, u, c):
                m = 2 * s + c
                pe.wait_ge(S["xt_done"], m + 1)
                if c == 0:
                    pe.wait_ge(S["w1_low"], s + 1)
                for q in range(2):
                    wait(pe, S["gelu_done"], 2 * m - 1 + q)
                    for j in range(2):
                        last = product_of_parts(pe, ps_h[q][:, j, :], [w[:, u, P * (2 * q + j):P * (2 * q + j) + P] for w in w1_parts],
                                                [x[:, c, :] for x in xt_parts])
                    last.then_inc(S["up_done"], 1)

            def down(s, u, turn, c):
                m = 2 * s + c
                if c == 0:
                    pe.wait_ge(loaded[u], 16 * LOADS * (turn + 1))
                pe.wait_ge(S["gelu_done"], 2 * m + 2)
                wait(pe, S["y_done"], m - 1)
                for t in range(TC):
                    for j in range(FC):
                        last = pe.matmul(ps_o[c][:, t, :], h[:, c, j, P * t:P * t + P], w2[:, u, j, :],
                                         start=(j == 0), stop=(j == FC - 1))
                last.then_inc(S["down_done"], 1)

            def project(k):
                pe.wait_ge(S["next_done"], min(k + 1, 2))
                wait(pe, R["rope_done"], k - 1)
                project_heads(pe, heads[k % 2], outer, 0, k).then_inc(R["p_done"], 1)

            turn_x(0, 0, 0, 0)

            def step(s, u, turn, on):
                if on(0):
                    up(s, u, 0)
                    if s is FIRST:
                        project(0)
                        project(1)
                    turn_x(2 * s + 1, u, turn, 1)
                    if s is FIRST:
                        project(2)
                if on(1):
                    down(s - 1, 1 - u, turn, 1)
                if on(0):
                    up(s, u, 1)
                    if s is FIRST:
                        project(3)
                        project(4)
                        project(5)
                if on(-1):
                    turn_x(2 * s + 2, 1 - u, turn + u, 0)
                if on(0):
                    if s is FIRST:
                        pe.wait_ge(R["rope_done"], G + 1)
                        pe.wait_ge(R["v_done"], 1)
                    down(s, u, turn, 0)

            steps(pe, E, DEPTH, LEAD, step, TAIL)

        @block.scalar
        def _(act):
            def take_x(m, c):
                act.wait_ge(S["t_done"], m + 1)
                act.activation(xt_parts[0][:, c, :], ps_t[:, :], ACT.Copy).then_inc(S["xt_high"], 1)

            take_x(0, 0)
            act.wait_ge(S["next_in"], 96)
            act.activation(outer["xnt1"][0][:, :, :], x1t[:, :, :], ACT.Copy)
            act.activation(outer["wq1"][0][:, :, :, :], wq1[:, :, :, :], ACT.Copy)
            act.activation(outer["wv1"][0][:, :], wv1[:, :], ACT.Copy).then_inc(S["next_high"], 1)

            def step(s, u, turn, on):
                for c in range(2):
                    if on(0):
                        m = 2 * s + c
                        if c == 0:
                            act.wait_ge(S["b1_done"], s + 1)
                        wait(act, S["down_done"], m - 1)
                        for q in range(2):
                            act.wait_ge(S["up_done"], 2 * m + q + 1)
                            for j in range(2):
                                last = act.activation(h[:, c, 2 * q + j, :], ps_h[q][:, j, :], ACT.Gelu,
                                                      bias=b1s[:, u, 2 * q + j:2 * q + j + 1], scale=GS)
                            last.then_inc(S["gelu_done"], 1)
                    if on(0) if c == 0 else on(-1):
                        take_x(2 * s + c + 1, 1 - c)

            steps(act, E, DEPTH, LEAD, step, TAIL)

        @block.vector
        def _(dve):
            def split_x(m, c):
                dve.wait_ge(S["xt_high"], m + 1)
                dve.tensor_tensor(xt_parts[1][:, c, :], ps_t[:, :], xt_parts[0][:, c, :], ALU.subtract).then_inc(S["xt_done"], 1)

            def add_bias(m, u, s, c):
                dve.wait_ge(S["down_done"], m + 1)
                wait(dve, stored[c], 16 * s)
                dve.scalar_tensor_tensor(out=y[:, c, :, :], in0=ps_o[c][:, :, :], scalar=1.0 / GS,
                                         in1=window(b2[:, u, :], [(0, TC), (1, P)]),
                                         op0=ALU.mult, op1=ALU.add).then_inc(S["y_done"], 1)

            def rope(k):
                dve.wait_ge(R["p_done"], k + 1)
                wait(dve, R["rot_done"], k - 1)
                rope_products(dve, heads[k % 2], outer, k).then_inc(R["rope_done"], 1)

            split_x(0, 0)

            def step(s, u, turn, on):
                if on(0):
                    dve.wait_ge(loaded[u], 16 * LOADS * (turn + 1))
                    wait(dve, S["gelu_done"], 4 * (s - 1))
                    dve.tensor_scalar(b1s[:, u, :], b1[:, u, :], GS, None, ALU.mult).then_inc(S["b1_done"], 1)
                    if s is FIRST:
                        dve.wait_ge(S["next_in"], 96)
                        rope(0)
                        rope(1)
                    split_x(2 * s + 1, 1)
                    if s is FIRST:
                        rope(2)
                        rope(3)
                        rope(4)
                        dve.wait_ge(R["p_done"], 6)
                        dve.wait_ge(R["one"], 1)
                        add_value_bias(dve, heads[1], outer, rows, 0).then_inc(R["v_done"], 1)
                if on(1):
                    add_bias(2 * s - 1, 1 - u, s - 1, 1)
                if on(-1):
                    split_x(2 * s + 2, 0)
                if on(0):
                    add_bias(2 * s, u, s, 0)

            steps(dve, E, DEPTH, LEAD, step, TAIL)


def rotary_attention(nc, outer, io):
    with ExitStack() as ctx:
        sb = lambda n, s, d=F32: ctx.enter_context(nc.sbuf_tensor("c_" + n, s, d))
        ps = lambda n, s, d=F32: ctx.enter_context(nc.psum_tensor("c_" + n, s, d))
        x_all = outer["x"]
        s_all, ident, identb, maskb, rows, slot = (outer[k] for k in ("s", "ident", "identb", "maskb", "rows", "slot"))
        G = NQ // NKV
        NH2 = NQ // 2
        wo, xnt_parts, rot, qt, kt, v = (outer[k] for k in ("wo1", "xnt1", "rot", "qt", "kt", "v"))
        xnt = sb("xnt", [P, 2, SEQ])
        q_stack = sb("q_stack", [P, NQ, P], F32R)
        lower = sb("lower", [P, 1])
        k_parts = [sb(f"k_{n}", [P, NKV, SEQ], F32R) for n in ("high", "low")]
        nmax = sb("nmax", [P, 2, 4])
        ex = [sb(f"ex{k}", [P, 2, 2, SEQ]) for k in range(2)]
        pt = sb("pt", [P, 2, 2, 2, SEQ])
        rden = sb("rden", [P, 2, G])
        o = sb("o", [P, 2, NQ, HD])
        ot = sb("ot", [P, 2, NH2, P])
        y = sb("y", [P, 2, 2, P])
        th = sb("th", [P, 2 * P])
        z = sb("z", [P, 2 * P])
        x2 = sb("x2", [P, 2, 2 * P])
        idx = sb("idx", [P, 2, 2], U32)
        ps_s = [ps(f"ps_s{k}", [P, 2, 512]) for k in range(2)]
        ps_t = ps("ps_t", [P, 2, 512])
        ps_o = ps("ps_o", [P, 512])
        ps_p = ps("ps_p", [P, 512])
        names = """lower_set x_high x_low q_high q_low s_done max_done exp_done t_done ta_done td_done
            pv_done rd_done o_done ot_ps ota_done otd_done wo_ps wo_done idx_done th_done z1_done z_done x2_done""".split()
        S = {n: ctx.enter_context(nc.semaphore("c_" + n)) for n in names}
        S.update(outer["sems"])
        x_in, y_in, gathered, stored = ([ctx.enter_context(nc.semaphore(f"c_{n}{u}")) for u in range(2)]
                                  for n in ("x_in", "y_in", "gathered", "stored"))
        flat = lambda t: t[:, :, :].rearrange("p n d -> p (n d)")
        U = 2 * NKV
        RELS = 32
        LEAD, DEPTH, TAIL = 4, 4, 2

        def anew(s):
            return not (isinstance(s, int) and s == 0)

        block = ctx.enter_context(nc.Block())

        @block.sync
        def _(sp):
            def load_x(s, u):
                wait(sp, S["x_low"], s - 3)
                sp.dma_start(xnt[:, u, :], io["xnt1"][:, bass.ds(s * SEQ, SEQ)]).then_inc(x_in[u], 16)

            def step(s, u, turn, on):
                if on(-1) and anew(s):
                    load_x(s + 1, 1 - u)
                if on(2):
                    b = s - 2
                    wait(sp, S["z1_done"], b - 1)
                    sp.dma_start(y[:, u, :, :], io["xn1"].rearrange("(n p) d -> p n d", p=P)[:, bass.ds(2 * b, 2), :]
                                 ).then_inc(y_in[u], 16)
                if on(4):
                    b = s - 4
                    sp.wait_ge(S["x2_done"], b + 1)
                    sp.dma_start(io["out"].rearrange("(n p) d -> p n d", p=P)[:, bass.ds(2 * b, 2), :],
                                 x2[:, u, :].rearrange("p (t d) -> p t d", t=2)).then_inc(stored[u], 16)
                if on(0) and anew(s):
                    sp.wait_ge(S["rot_done"], (G + 1) * s + 1)
                    regroup(sp, outer, u, False, S["rel"])
                    sp.wait_ge(S["rot_done"], (G + 1) * (s + 1))
                    regroup(sp, outer, u, True, S["rel"])

            steps(sp, NB, DEPTH, LEAD, step, TAIL)
            for u in range(2):
                sp.wait_ge(stored[u], 16 * NB // 2)

        @block.gpsimd
        def _(pool):
            def split_x(s, u):
                pool.wait_ge(S["x_high"], s - 1)
                pool.tensor_tensor(xnt_parts[1][:, u, :], xnt[:, u, :], xnt_parts[0][:, u, :], ALU.subtract
                                   ).then_inc(S["x_low"], 1)

            pool.memset(lower[:, :], 1.0).then_inc(S["lower_set"], 1)
            pool.wait_ge(S["lower_set"], 1)
            pool.affine_select(out=lower[:, :], in_=lower[:, :], compare_op=ALU.is_ge, fill=0.0, base=-HD,
                               pattern=[[0, 1]], channel_multiplier=1).then_inc(S["lower_set"], 1)
            def rotate_group(s, k):
                pool.wait_ge(S["rope_done"], (G + 1) * s + (k + 1))
                if k == 0:
                    wait(pool, S["rel"], 16 * RELS * s)
                rotate(pool, outer, k).then_inc(S["rot_done"], 1)

            def step(s, u, turn, on):
                if on(2):
                    wait(pool, gathered[u], 32 * (turn - 1))
                    pool.tensor_copy(idx[:, u, :], slot[:, bass.ds(2 * (s - 2), 2)]).then_inc(S["idx_done"], 1)
                for k in range(G):
                    if on(1):
                        r, heads = 1 - u, slice(G * k, G * k + G)
                        pool.wait_ge(S["q_high"], NKV * (s - 1) + (k + 1))
                        pool.tensor_tensor(k_parts[1][:, k, :], kt[:, r, k, :], k_parts[0][:, k, :], ALU.subtract)
                        pool.tensor_tensor(q_stack[:, heads, :], qt[:, heads, P:SEQ], q_stack[:, heads, :], ALU.subtract
                                           ).then_inc(S["q_low"], 1)
                    if on(0) and anew(s):
                        rotate_group(s, k + 1)
                if on(-1) and anew(s):
                    split_x(s + 1, 1 - u)
                if on(2):
                    pool.wait_ge(S["idx_done"], s - 1)
                    pool.wait_ge(y_in[u], 16 * turn)
                if on(3):
                    b = s - 3
                    wait(pool, stored[1 - u], 16 * (turn + u - 2))
                    pool.wait_ge(S["z_done"], b + 1)
                    pool.tensor_tensor(x2[:, 1 - u, :], z[:, :], flat(x_all)[:, bass.ds(2 * P * b, 2 * P)], ALU.add
                                       ).then_inc(S["x2_done"], 1)
                if on(-1):
                    rotate_group(s + 1, 0)
                if on(2):
                    for t in range(2):
                        pool.indirect_dma_start(
                            out=y[:, u, t, :], out_offset=None, in_=io["slots_out"],
                            in_offset=bass.IndirectOffsetOnAxis(ap=idx[:, u, t:t + 1], axis=0),
                            bounds_check=E * CAP - 1, oob_is_err=False).then_inc(gathered[u], 16)

            steps(pool, NB, DEPTH, LEAD, step, TAIL)

        @block.tensor
        def _(pe):
            def mask_scores(b, k):
                n, t = b * U + k, k // NKV
                if k == 0:
                    pe.wait_ge(S["rel"], 16 * RELS * (b + 1))
                wait(pe, S["exp_done"], n - 1)
                sc = ps_s[k % 2]
                for half in range(2):
                    pe.matmul(window(sc[:, half, :], [(2 * P, 2), (1, P)], t * P), identb[:, :],
                              window(maskb[:, :], [(0, 2), (1, P)]), start=True, stop=False, skip_group_check=True)

            def scores(b, u, k, w):
                t, g = k // NKV, k % NKV
                cols = P * (t + 1)
                if t == 1 and w == 0:
                    pe.wait_ge(S["q_low"], NKV * b + (g + 1))
                for half in range(2):
                    out, head = ps_s[k % 2][:, half, 2 * P * w:2 * P * w + cols], G * g + 2 * w + half
                    if t == 0:
                        last = pe.matmul(out, qt[64 * half:64 * half + 64, head, 0:P], kt[64 * half:64 * half + 64, u, g, 0:P],
                                         start=False, stop=True, skip_group_check=True)
                    else:
                        pe.matmul(out, q_stack[:, head, :], k_parts[0][:, g, :], start=False, stop=False, skip_group_check=True)
                        last = pe.matmul(out, q_stack[:, head, :], k_parts[1][:, g, :], start=False, stop=True,
                                         skip_group_check=True)
                if w == 1:
                    last.then_inc(S["s_done"], 1)

            def project(s, u, k):
                if k == 0:
                    wait(pe, S["x_low"], s - 1)
                    wait(pe, S["v_done"], s)
                    wait(pe, S["wo_done"], 2 * (s - 3) + 1)
                else:
                    pe.wait_ge(S["rope_done"], (G + 1) * s + k)
                    if k == 1:
                        wait(pe, S["wo_done"], 2 * (s - 2))
                project_heads(pe, ps_p, outer, u, k).then_inc(S["p_done"], 1)

            def turn_probs(b, k):
                n, t = b * U + k, k // NKV
                pe.wait_ge(S["exp_done"], n + 1)
                outs = 2 * b - 1 if k <= 1 else 2 * b if k <= 5 else 2 * b + 1
                for w in range(2):
                    wait(pe, S[("ta_done", "td_done")[w]], n)
                    wait(pe, S[("ota_done", "otd_done")[w]], outs)
                    for half in range(2):
                        for blk in range(t + 1):
                            at = P * (half * (t + 1) + blk)
                            last = pe.transpose(ps_t[:, w, at:at + P], ex[k % 2][:, half, w, P * blk:P * blk + P], ident[:, :])
                last.then_inc(S["t_done"], 1)

            def weigh(b, r, k):
                n, t, g = b * U + k, k // NKV, k % NKV
                pe.wait_ge(S["v_done"], b + 1)
                wait(pe, S["o_done"], n)
                for w in range(2):
                    pe.wait_ge(S[("ta_done", "td_done")[w]], n + 1)
                    for half in range(2):
                        h = 2 * w + half
                        for blk in range(t + 1):
                            at = P * (half * (t + 1) + blk)
                            last = pe.matmul(ps_o[:, (HD + 1) * h:(HD + 1) * (h + 1)], pt[:, k % 2, w, at // SEQ, at % SEQ:at % SEQ + P],
                                             v[:, r, blk, g, :], start=(blk == 0), stop=(blk == t))
                last.then_inc(S["pv_done"], 1)

            def step(s, u, turn, on):
                for k in range(U):
                    if on(1):
                        mask_scores(s - 1, k)
                        scores(s - 1, 1 - u, k, 0)
                    if on(2) and k in (0, 4):
                        b, t = s - 2, k // 4
                        pe.wait_ge(S["o_done"], b * U + (4 * t + 4))
                        n = (b + 1) * U + k - 2
                        last_unit = n if on(1) else min(n, NB * U)
                        for j in range(NH2):
                            if j % 4 == 0:
                                pe.wait_ge(S[("ta_done", "td_done")[j // 4]], last_unit)
                            last = pe.transpose(ps_t[:, j // 4, P * (j % 4):P * (j % 4) + P], o[:, t, 2 * j:2 * j + 2, :]
                                                .rearrange("p a d -> p (a d)"), ident[:, :])
                        last.then_inc(S["ot_ps"], 1)
                    if on(1):
                        scores(s - 1, 1 - u, k, 1)
                    if on(0) and anew(s) and k <= G:
                        project(s, u, k + 1)
                    if on(-1) and k == U - 1:
                        project(s + 1, 1 - u, 0)
                    if (on(1) if k >= 2 else on(2)):
                        turn_probs(s - 1 if k >= 2 else s - 2, (k - 2) % U)
                    if (on(1) if k >= 3 else on(2)):
                        weigh(s - 1 if k >= 3 else s - 2, (1 - u) if k >= 3 else u, (k - 3) % U)
                    if on(2) and k >= 6:
                        b, t = s - 2, k - 6
                        pe.wait_ge(S["ota_done"], 2 * b + (t + 1))
                        pe.wait_ge(S["otd_done"], 2 * b + (t + 1))
                        if k == 6:
                            pe.wait_ge(S["v_done"], s + 1 if on(0) else NB)
                            wait(pe, S["wo_done"], 2 * b)
                        else:
                            pe.wait_ge(S["wo_done"], 2 * b + 1)
                            if on(-1):
                                pe.wait_ge(S["rope_done"], (G + 1) * (s + 1) + 1)
                        for j in range(NH2):
                            last = pe.matmul(ps_p[:, 0:P], ot[:, t, j, :], wo[:, j, :], start=(j == 0), stop=(j == NH2 - 1))
                        last.then_inc(S["wo_ps"], 1)

            steps(pe, NB, DEPTH, LEAD, step, TAIL)

        @block.scalar
        def _(act):
            def split_x(s, u, turn):
                act.wait_ge(x_in[u], 16 * turn)
                wait(act, S["p_done"], 6 * (s - 1))
                act.activation(xnt_parts[0][:, u, :], xnt[:, u, :], ACT.Copy).then_inc(S["x_high"], 1)

            act.wait_ge(S["lower_set"], 2)
            def step(s, u, turn, on):
                for k in range(U):
                    if on(2) and k in (0, 4):
                        b, t = s - 2, k // 4
                        act.wait_ge(S["ot_ps"], 2 * b + (t + 1))
                        wait(act, S["wo_ps"], 2 * (b - 1) + (t + 1))
                        act.activation(ot[:, t, 0:4, :].rearrange("p j n -> p (j n)"), ps_t[:, 0, :], ACT.Copy).then_inc(S["ota_done"], 1)
                    if (on(1) if k >= 2 else on(2)):
                        b, kk = (s - 1 if k >= 2 else s - 2), (k - 2) % U
                        n, t = b * U + kk, kk // NKV
                        act.wait_ge(S["t_done"], n + 1)
                        wait(act, S["pv_done"], n - 1)
                        act.activation(pt[:, kk % 2, 0, 0:t + 1, :], ps_t[:, 0, 0:SEQ * (t + 1)].rearrange("p (a n) -> p a n", n=SEQ),
                                       ACT.Copy).then_inc(S["ta_done"], 1)
                    if on(1) and k < NKV:
                        r, heads = 1 - u, slice(G * k, G * k + G)
                        if k == 0:
                            act.wait_ge(S["rel"], 16 * RELS * s)
                            wait(act, S["s_done"], U * (s - 1))
                        act.activation(q_stack[:, heads, :], qt[:, heads, P:SEQ], ACT.Copy, scale=lower[:, :])
                        act.activation(k_parts[0][:, k, :], kt[:, r, k, :], ACT.Copy).then_inc(S["q_high"], 1)
                    if on(1):
                        b = s - 1
                        n, t = b * U + k, k // NKV
                        cols = P * (t + 1)
                        act.wait_ge(S["max_done"], n + 1)
                        wait(act, S["t_done"], n - 1)
                        for half in range(2):
                            for w in range(2):
                                last = act.activation(ex[k % 2][:, half, w, 0:cols], ps_s[k % 2][:, half, 2 * P * w:2 * P * w + cols],
                                                      ACT.Exp, bias=nmax[:, k % 2, 2 * half + w:2 * half + w + 1])
                        last.then_inc(S["exp_done"], 1)
                    if on(-1) and anew(s) and k == 5:
                        split_x(s + 1, 1 - u, turn + u)
                    if on(3) and k == 5:
                        b, r = s - 3, 1 - u
                        act.wait_ge(gathered[r], 32 * (turn + u - 1))
                        act.activation(th[:, :], y[:, r, :, :].rearrange("p t n -> p (t n)"), ACT.Tanh, scale=0.5
                                       ).then_inc(S["th_done"], 1)

            steps(act, NB, DEPTH, LEAD, step, TAIL)

        @block.vector
        def _(dve):
            def rope_group(s, k):
                dve.wait_ge(S["p_done"], 6 * s + (k + 1))
                wait(dve, S["rot_done"], (G + 1) * s + max(k - 1, 0))
                rope_products(dve, ps_p, outer, k).then_inc(S["rope_done"], 1)

            def step(s, u, turn, on):
                for k in range(U):
                    if on(2) and k in (0, 4):
                        b, t = s - 2, k // 4
                        dve.wait_ge(S["ot_ps"], 2 * b + (t + 1))
                        wait(dve, S["wo_ps"], 2 * (b - 1) + (t + 1))
                        dve.tensor_copy(ot[:, t, 4:8, :].rearrange("p j n -> p (j n)"), ps_t[:, 1, :]).then_inc(S["otd_done"], 1)
                    if on(1):
                        b = s - 1
                        n, t = b * U + k, k // NKV
                        dve.wait_ge(S["s_done"], n + 1)
                        wait(dve, S["exp_done"], n - 1)
                        dve.tensor_reduce(nmax[:, k % 2, :].rearrange("p (h w) -> p h w", h=2),
                                          ps_s[k % 2][:, :, :].rearrange("p h (w n) -> p h w n", w=2)[:, :, :, 0:P * (t + 1)],
                                          AX_X, ALU.max, negate=True).then_inc(S["max_done"], 1)
                    if on(0) and anew(s) and k < G:
                        rope_group(s, k + 1)
                    if on(-1) and k == U - 1:
                        rope_group(s + 1, 0)
                    if on(0) and anew(s) and k == G:
                        dve.wait_ge(S["p_done"], 6 * (s + 1))
                        wait(dve, S["pv_done"], U * (s - 1))
                        add_value_bias(dve, ps_p, outer, rows, u).then_inc(S["v_done"], 1)
                    if (on(1) if k >= 2 else on(2)):
                        b, kk = (s - 1 if k >= 2 else s - 2), (k - 2) % U
                        n, t = b * U + kk, kk // NKV
                        dve.wait_ge(S["t_done"], n + 1)
                        wait(dve, S["pv_done"], n - 1)
                        dve.tensor_copy(pt[:, kk % 2, 1, 0:t + 1, :], ps_t[:, 1, 0:SEQ * (t + 1)].rearrange("p (a n) -> p a n", n=SEQ)
                                        ).then_inc(S["td_done"], 1)
                    if (on(1) if k >= 3 else on(2)):
                        b, kk = (s - 1 if k >= 3 else s - 2), (k - 3) % U
                        n, t, g = b * U + kk, kk // NKV, kk % NKV
                        heads = ps_o[:, 0:G * (HD + 1)].rearrange("p (h d) -> p h d", h=G)
                        dve.wait_ge(S["pv_done"], n + 1)
                        dve.reciprocal(rden[:, kk % 2, :], heads[:, :, HD]).then_inc(S["rd_done"], 1)
                        dve.wait_ge(S["rd_done"], n + 1)
                        if g == 0:
                            wait(dve, S["ot_ps"], 2 * (b - 1) + (t + 1))
                        dve.tensor_tensor(o[:, t, G * g:G * g + G, :], heads[:, :, 0:HD],
                                          window(rden[:, kk % 2, :], [(1, G), (0, HD)]), ALU.mult).then_inc(S["o_done"], 1)
                    if on(3) and k == 6:
                        b, r = s - 3, 1 - u
                        dve.wait_ge(S["th_done"], b + 1)
                        wait(dve, S["x2_done"], b)
                        dve.scalar_tensor_tensor(out=z[:, :], in0=th[:, :], scalar=1.0,
                                                 in1=y[:, r, :, :].rearrange("p t n -> p (t n)"), op0=ALU.add, op1=ALU.mult
                                                 ).then_inc(S["z1_done"], 1)
                        dve.wait_ge(S["z1_done"], b + 1)
                        dve.scalar_tensor_tensor(out=z[:, :], in0=z[:, :], scalar=0.5, in1=flat(s_all)[:, bass.ds(2 * P * b, 2 * P)],
                                                 op0=ALU.mult, op1=ALU.mult).then_inc(S["z_done"], 1)
                    if on(2) and k >= 6:
                        b, t = s - 2, k - 6
                        dve.wait_ge(S["wo_ps"], 2 * b + (t + 1))
                        dve.tensor_tensor(s_all[:, bass.ds(2 * b + t, 1), :].rearrange("p a d -> p (a d)"), ps_p[:, 0:P],
                                          rows[:, R_BO1:R_BO1 + P], ALU.add).then_inc(S["wo_done"], 1)

            steps(dve, NB, DEPTH, LEAD, step, TAIL)
            dve.wait_ge(S["wo_done"], 2 * NB)


def program(nc, io):
    with ExitStack() as ctx:
        sb = lambda n, s, d=F32: ctx.enter_context(nc.sbuf_tensor(n, s, d))
        outer = {
            "x": sb("x_all", [P, NT, D]), "s": sb("s_all", [P, NT, D]),
            "ident": sb("ident", [P, P]), "identb": sb("identb", [P, P], BF16),
            "mask": sb("mask", [P, P]), "maskb": sb("maskb", [P, P], BF16), "rows": sb("rows", [P, R_COLS]),
            "ones": sb("ones", [P, P]), "upto": sb("upto", [P, P]), "slot": sb("slot", [P, NT], U32),
        }
        with ExitStack() as c2:
            s_id = c2.enter_context(nc.semaphore("s_id"))
            s_z = c2.enter_context(nc.semaphore("s_z"))
            s_rows = c2.enter_context(nc.semaphore("s_rows"))
            block = c2.enter_context(nc.Block())

            @block.sync
            def _(sp):
                sp.dma_start(outer["rows"][:, :], io["rows"].partition_broadcast(P)).then_inc(s_rows, 16)
                sp.wait_ge(s_rows, 16)

            @block.gpsimd
            def _(pool):
                pool.memset(outer["ident"][:, :], 0.0).then_inc(s_z, 1)
                pool.memset(outer["mask"][:, :], 0.0).then_inc(s_z, 1)
                pool.memset(outer["upto"][:, :], 1.0).then_inc(s_z, 1)
                pool.wait_ge(s_z, 3)
                pool.affine_select(out=outer["ident"][:, :], in_=outer["ident"][:, :], compare_op=ALU.not_equal, fill=1.0,
                                   base=0, pattern=[[-1, P]], channel_multiplier=1).then_inc(s_id, 1)
                pool.affine_select(out=outer["mask"][:, :], in_=outer["mask"][:, :], compare_op=ALU.is_ge, fill=MASKED,
                                   base=0, pattern=[[-1, P]], channel_multiplier=1).then_inc(s_id, 1)

                pool.affine_select(out=outer["upto"][:, :], in_=outer["upto"][:, :], compare_op=ALU.is_ge, fill=0.0,
                                   base=0, pattern=[[1, P]], channel_multiplier=-1).then_inc(s_id, 1)
                pool.wait_ge(s_id, 3)

            @block.vector
            def _(dve):
                dve.memset(outer["ones"][:, :], 1.0)
                dve.wait_ge(s_id, 3)
                dve.tensor_copy(outer["identb"][:, :], outer["ident"][:, :])
                dve.tensor_copy(outer["maskb"][:, :], outer["mask"][:, :]).then_inc(s_z, 1)
                dve.wait_ge(s_z, 4)
        with ExitStack() as first:
            sb1 = lambda n, s, d=F32: first.enter_context(nc.sbuf_tensor(n, s, d))
            layer = dict(outer, xnt=sb1("xnt_all", [P, NT * P]), logits0=sb1("logits0", [P, NT, E]),
                         ffn0_w1=[sb1(f"ffn0_w1_{n}", [P, E + 1, H0], F32R) for n in ("high", "low")])
            local_and_topk_attention(nc, layer, io)
            mixture_of_all_experts(nc, layer, io)
        with ExitStack() as second:
            sb2 = lambda n, s, d=F32: second.enter_context(nc.sbuf_tensor(n, s, d))
            layer = dict(outer, wq1=[sb2(f"wq1_{n}", [P, NQ // NKV + 1, 2, P], F32R) for n in ("high", "low")],
                         wv1=[sb2(f"wv1_{n}", [P, NKV * HD], F32R) for n in ("high", "low")],
                         xnt1=[sb2(f"xnt1_{n}", [P, 2, SEQ], F32R) for n in ("high", "low")],
                         bq1=sb2("bq1", [P, NQ // NKV + 1, 2]), wo1=sb2("wo1", [P, NQ // 2, P]),
                         rope=sb2("rope_tables", [P, 2, 2, SEQ]),
                         prod=sb2("prod", [P, 2, 4, SEQ]),
                         rot=sb2("rot", [P, NQ // NKV + 1, 2, SEQ]),
                         qt=sb2("qt", [P, NQ, SEQ]), kt=sb2("kt", [P, 2, NKV, SEQ]),
                         v=sb2("v", [P, 2, 2, NKV, HD + 1]),
                         sems={n: second.enter_context(nc.semaphore(n))
                               for n in ("one", "p_done", "rope_done", "rot_done", "v_done", "rel")})
            mixture_by_slots(nc, layer, io)
            rotary_attention(nc, layer, io)


def rope_tables():
    import numpy as np

    inv = (1.0 / np.float32(10000.0) ** (np.arange(0, HD, 2, dtype=np.float32) / np.float32(HD))).astype(np.float32)
    ang = (np.arange(SEQ, dtype=np.float32)[None, :] * inv[:, None]).astype(np.float32).astype(np.float64)
    one = np.stack([np.cos(ang), np.sin(ang)], axis=1)
    return np.tile(np.stack([one / HD ** 0.5, one], axis=1), (4, 1, 1, 1)).astype(np.float32)


def kernel(**inputs):
    import numpy as _np
    import concourse.bacc as _bacc
    from concourse import mybir as _mybir
    from concourse.bass_utils import run_bass_kernel_spmd as _run

    x = {k: _np.asarray(v) for k, v in inputs.items()}
    col = lambda v: v.reshape(-1, 1)
    halves = lambda w: w.reshape(len(w), -1, 4, 2, HD // 2).transpose(0, 1, 3, 2, 4).reshape(len(w), -1, 2, P)
    arrays = {
        "x": x["L0_attn_mu"].reshape(NB * SEQ, D),
        "w0": _np.concatenate([x["L0_attn_Wq"], x["L0_attn_Wk"], x["L0_attn_Wm1"][:D], x["L0_attn_Wm1"][D:],
                               x["L0_attn_Wv"], x["L0_attn_Wm2"], x["L0_attn_Wo"][:D], x["L0_attn_Wo"][D:],
                               x["L0_ffn_router_w"], col(x["L0_attn_bq"]), col(x["L0_attn_bk"]), col(x["L0_attn_bm1"]),
                               col(x["L0_attn_bv"]), col(x["L0_attn_bm2"])], axis=1),
        "rows": _np.concatenate([x["L0_attn_bo"], x["L0_ffn_router_b"], x["L1_ffn_b_sw"], x["L1_attn_bo"],
                                 x["L1_attn_bv"], _np.arange(E, 0, -1, dtype=_np.float32),
                                 CAP * _np.arange(E, dtype=_np.float32) - 1, CAP * _np.arange(1, E + 1, dtype=_np.float32) - 1]),
        "ffn0_w1": _np.concatenate([x["L0_ffn_sw1"][None], x["L0_ffn_rw1"]]).transpose(1, 0, 2),
        "ffn0_b1": _np.concatenate([x["L0_ffn_sb1"][None], x["L0_ffn_rb1"]]).reshape(-1, P).T,
        "ffn0_w2": _np.concatenate([x["L0_ffn_sw2"][None], x["L0_ffn_rw2"]]).reshape(E + 1, H0 // P, P, D).transpose(2, 0, 1, 3),
        "ffn0_b2": _np.concatenate([x["L0_ffn_rb2"], x["L0_ffn_sb2"][None]]),
        "wsw": x["L1_ffn_W_sw"],
        "wq1": _np.concatenate([halves(x["L1_attn_Wk"]), halves(x["L1_attn_Wq"])], axis=1),
        "bq1": _np.concatenate([halves(x["L1_attn_bk"][None])[0], halves(x["L1_attn_bq"][None])[0]]).transpose(2, 0, 1),
        "wv1": x["L1_attn_Wv"],
        "wo1": x["L1_attn_Wo"].reshape(NQ // 2, P, D).transpose(1, 0, 2),
        "rope": rope_tables(),
        "ffn1_w1": x["L1_ffn_W1"].reshape(E * P, FF),
        "ffn1_w2": x["L1_ffn_W2"].reshape(E, FF // P, P, D).transpose(0, 2, 1, 3).reshape(E * P, FF // P * D),
        "ffn1_b1": x["L1_ffn_b1"].reshape(E, FF // P, P).transpose(0, 2, 1).reshape(E * P, FF // P),
        "ffn1_b2": x["L1_ffn_b2"],
    }
    arrays = {f"{k}_dram": _np.ascontiguousarray(v) for k, v in arrays.items()}
    nc = _bacc.Bacc("TRN2", target_bir_lowering=False, num_devices=1)
    io = {k[:-5]: nc.dram_tensor(k, a.shape, _mybir.dt.from_np(a.dtype), kind="ExternalInput").ap()
          for k, a in arrays.items()}
    io["out"] = nc.dram_tensor("out_dram", (NB * SEQ, D), F32, kind="ExternalOutput").ap()
    io["xn1"] = nc.dram_tensor("xn1_scratch", (NB * SEQ, D), F32, kind="Internal").ap()
    io["xnt1"] = nc.dram_tensor("xnt1_scratch", (P, NB * SEQ), F32, kind="Internal").ap()
    io["slots_in"] = nc.dram_tensor("slots_in_scratch", (E * CAP, D), F32, kind="Internal").ap()
    io["slots_out"] = nc.dram_tensor("slots_out_scratch", (E * CAP, D), F32, kind="Internal").ap()
    program(nc, io)
    r = _run(nc, [arrays], core_ids=[0])
    return r.results[0]["out_dram"].reshape(NB, SEQ, D)
```
